# Optimizing a Trainium2 kernel written in Bass

```python
import numpy as np
import jax
import jax.numpy as jnp

def _softmax(x, axis=-1):
    return jax.nn.softmax(x, axis=axis)

def _gelu(x):
    return jax.nn.gelu(x, approximate=True)

def _silu(x):
    return jax.nn.silu(x)

def _sigmoid(x):
    return jax.nn.sigmoid(x)

def _layernorm(x, axis=-1, eps=1e-05):
    m = jnp.mean(x, axis=axis, keepdims=True)
    v = jnp.var(x, axis=axis, keepdims=True)
    return (x - m) / jnp.sqrt(v + eps)

def _scatter_add(tgt, idx, src, axis=0):
    return tgt.at[idx].add(src)

def _segment_sum(src, seg, n):
    return jax.ops.segment_sum(src, seg, n)
kernel_name = 'mk_decoder_preln_d1_seqx_r4_75b89a'

def setup_inputs(seed: int=0):
    np.random.seed(seed)
    _w = jnp.asarray

    def _rec_inputs():
        import jax
        import jax.numpy as jnp
        _rk = jax.random.key(seed)
        x = 2.818e-05 + 1 * jax.random.normal(jax.random.fold_in(_rk, 1), (4, 512, 512), jnp.float32)
        _lenS = 512 - jax.random.randint(jax.random.fold_in(_rk, 7), (4,), 0, max(1, 512 // 4) + 1, jnp.int32)
        _lenS2 = 512 - jax.random.randint(jax.random.fold_in(_rk, 8), (4,), 0, max(1, 512 // 4) + 1, jnp.int32)
        _ctx_1024P = jax.random.normal(jax.random.fold_in(_rk, 11), (4, 16, 256), jnp.float32)
        _ctx_1024c = jax.random.dirichlet(jax.random.fold_in(_rk, 511), 0.3 * jnp.ones((16,), jnp.float32), (4, 512))
        _ctx_1024t = jnp.einsum('bsk,bkd->bsd', _ctx_1024c, _ctx_1024P)
        _ctx_1024t = _ctx_1024t * jax.lax.rsqrt(jnp.mean(jnp.square(_ctx_1024t)) + 1e-12) * 0.953939
        ctx_1024 = 7.22013e-05 + 1.00017 * (_ctx_1024t + 0.3 * jax.random.normal(jax.random.fold_in(_rk, 611), (4, 512, 256), jnp.float32))
        return (x, ctx_1024)
    x, ctx_1024 = _rec_inputs()

    def _L0_attn_setup():
        import jax, jax.numpy as jnp
        import numpy as np
        B, S, D = (2, 512, 512)
        H, HD = (16, 128)
        SCALE = 1.0 / np.sqrt(HD)
        key = jax.random.key(seed)
        ks = jax.random.split(key, 5)
        return {'Q_input': jax.random.normal(ks[0], (B, S, D), dtype=jnp.float32), 'Wq': jax.random.normal(ks[1], (D, H * HD), dtype=jnp.float32) * D ** (-0.5), 'Wk': jax.random.normal(ks[2], (D, HD), dtype=jnp.float32) * D ** (-0.5), 'Wv': jax.random.normal(ks[3], (D, HD), dtype=jnp.float32) * D ** (-0.5), 'Wo': jax.random.normal(ks[4], (H * HD, D), dtype=jnp.float32) * (H * HD) ** (-0.5)}
    _L0_attn_all = _L0_attn_setup()
    _L0_attn_in = {k: v for k, v in _L0_attn_all.items() if k in ('Wq', 'Wk', 'Wv', 'Wo')}
    del _L0_attn_all

    def _L0_xattn_setup():
        import jax, jax.numpy as jnp
        import numpy as np
        B_, L_, D_MODEL = (4, 512, 256)
        D_STATE, D_CONV, EXPAND = (16, 4, 2)
        D_INNER = EXPAND * D_MODEL
        DT_RANK = (D_MODEL + 15) // 16

        def silu(x):
            return x * jax.nn.sigmoid(x)
        key = jax.random.key(seed)
        ks = jax.random.split(key, 10)
        f32 = jnp.float32
        hidden_states = jax.random.normal(ks[0], (B_, L_, D_MODEL), dtype=f32)
        z = jax.random.normal(ks[1], (B_, D_INNER, L_), dtype=f32)
        in_proj_w = jax.random.normal(ks[2], (D_INNER, D_MODEL), dtype=f32) * 0.02
        conv_w = jax.random.normal(ks[3], (D_INNER, 1, D_CONV), dtype=f32) * 0.1
        conv_b = jax.random.normal(ks[4], (D_INNER,), dtype=f32) * 0.02
        x_proj_w = jax.random.normal(ks[5], (DT_RANK + 2 * D_STATE, D_INNER), dtype=f32) * 0.02
        dt_proj_w = jax.random.uniform(ks[6], (D_INNER, DT_RANK), dtype=f32, minval=-DT_RANK ** (-0.5), maxval=DT_RANK ** (-0.5))
        dt = jnp.exp(jax.random.uniform(ks[7], (D_INNER,), dtype=f32, minval=np.log(0.001), maxval=np.log(0.1)))
        dt_proj_b = jnp.log(jnp.expm1(dt))
        A_log = jnp.log(jnp.broadcast_to(jnp.arange(1, D_STATE + 1, dtype=f32), (D_INNER, D_STATE)))
        D = jnp.ones((D_INNER,), f32)
        return {'hidden_states': hidden_states, 'z': z, 'in_proj_w': in_proj_w, 'conv_w': conv_w, 'conv_b': conv_b, 'x_proj_w': x_proj_w, 'dt_proj_w': dt_proj_w, 'dt_proj_b': dt_proj_b, 'A_log': A_log, 'D': D}
    _L0_xattn_all = _L0_xattn_setup()
    _L0_xattn_in = {k: v for k, v in _L0_xattn_all.items() if k in ('in_proj_w', 'conv_w', 'conv_b', 'x_proj_w', 'dt_proj_w', 'dt_proj_b', 'A_log', 'D')}
    del _L0_xattn_all

    def _L0_ffn_setup():
        import jax, jax.numpy as jnp
        import numpy as np
        H, LAT, INTER, E, G, TOPK_G, TOP_K = (512, 256, 256, 32, 4, 2, 8)
        SHARED_INTER = 1024
        ROUTED_SCALE = 2.5
        B, S = (2, 256)

        def relu2(x):
            return jnp.square(jax.nn.relu(x))
        key = jax.random.key(seed)
        ks = jax.random.split(key, 9)
        w = 0.02
        return {'hidden_states': jax.random.normal(ks[0], (B, S, H), jnp.float32), 'gate_w': jax.random.normal(ks[1], (E, H), jnp.float32) * w, 'gate_bias': jax.random.normal(ks[2], (E,), jnp.float32) * w, 'fc1_w': jax.random.normal(ks[3], (LAT, H), jnp.float32) * w, 'fc2_w': jax.random.normal(ks[4], (H, LAT), jnp.float32) * w, 'w1': jax.random.normal(ks[5], (E, INTER, LAT), jnp.float32) * w, 'w2': jax.random.normal(ks[6], (E, LAT, INTER), jnp.float32) * w, 'shared_up_w': jax.random.normal(ks[7], (SHARED_INTER, H), jnp.float32) * w, 'shared_down_w': jax.random.normal(ks[8], (H, SHARED_INTER), jnp.float32) * w}
    _L0_ffn_all = _L0_ffn_setup()
    _L0_ffn_in = {k: v for k, v in _L0_ffn_all.items() if k in ('gate_w', 'gate_bias', 'fc1_w', 'fc2_w', 'w1', 'w2', 'shared_up_w', 'shared_down_w')}
    del _L0_ffn_all
    return {'x': x, 'ctx_1024': ctx_1024, 'L0_attn_Wq': _L0_attn_in['Wq'], 'L0_attn_Wk': _L0_attn_in['Wk'], 'L0_attn_Wv': _L0_attn_in['Wv'], 'L0_attn_Wo': _L0_attn_in['Wo'], 'L0_xattn_in_proj_w': _L0_xattn_in['in_proj_w'], 'L0_xattn_conv_w': _L0_xattn_in['conv_w'], 'L0_xattn_conv_b': _L0_xattn_in['conv_b'], 'L0_xattn_x_proj_w': _L0_xattn_in['x_proj_w'], 'L0_xattn_dt_proj_w': _L0_xattn_in['dt_proj_w'], 'L0_xattn_dt_proj_b': _L0_xattn_in['dt_proj_b'], 'L0_xattn_A_log': _L0_xattn_in['A_log'], 'L0_xattn_D': _L0_xattn_in['D'], 'L0_ffn_gate_w': _L0_ffn_in['gate_w'], 'L0_ffn_gate_bias': _L0_ffn_in['gate_bias'], 'L0_ffn_fc1_w': _L0_ffn_in['fc1_w'], 'L0_ffn_fc2_w': _L0_ffn_in['fc2_w'], 'L0_ffn_w1': _L0_ffn_in['w1'], 'L0_ffn_w2': _L0_ffn_in['w2'], 'L0_ffn_shared_up_w': _L0_ffn_in['shared_up_w'], 'L0_ffn_shared_down_w': _L0_ffn_in['shared_down_w']}

def reference(x, ctx_1024, L0_attn_Wq, L0_attn_Wk, L0_attn_Wv, L0_attn_Wo, L0_xattn_in_proj_w, L0_xattn_conv_w, L0_xattn_conv_b, L0_xattn_x_proj_w, L0_xattn_dt_proj_w, L0_xattn_dt_proj_b, L0_xattn_A_log, L0_xattn_D, L0_ffn_gate_w, L0_ffn_gate_bias, L0_ffn_fc1_w, L0_ffn_fc2_w, L0_ffn_w1, L0_ffn_w2, L0_ffn_shared_up_w, L0_ffn_shared_down_w):
    import jax
    import jax.numpy as jnp

    def _L0_attn_ref(Q_input, Wq, Wk, Wv, Wo):
        import jax, jax.numpy as jnp
        import numpy as np
        B, S, D = (2, 512, 512)
        H, HD = (16, 128)
        SCALE = 1.0 / np.sqrt(HD)
        b, s, _ = Q_input.shape
        Q = (Q_input @ Wq).reshape(b, s, H, HD)
        K = Q_input @ Wk
        V = Q_input @ Wv
        scores = jnp.einsum('bshd,btd->bhst', Q, K) * SCALE
        attn = jax.nn.softmax(scores, axis=-1)
        head_out = jnp.einsum('bhst,btd->bshd', attn, V)
        out = head_out.reshape(b, s, H * HD) @ Wo
        return out

    def _L0_xattn_ref(hidden_states, z, in_proj_w, conv_w, conv_b, x_proj_w, dt_proj_w, dt_proj_b, A_log, D):
        import jax, jax.numpy as jnp
        import numpy as np
        B_, L_, D_MODEL = (4, 512, 256)
        D_STATE, D_CONV, EXPAND = (16, 4, 2)
        D_INNER = EXPAND * D_MODEL
        DT_RANK = (D_MODEL + 15) // 16

        def silu(x):
            return x * jax.nn.sigmoid(x)
        Bsz, L, _ = hidden_states.shape
        d_inner, _, d_conv = conv_w.shape
        dt_rank = dt_proj_w.shape[1]
        d_state = A_log.shape[1]
        x = jnp.einsum('bld,ed->bel', hidden_states, in_proj_w)
        xc = jax.lax.conv_general_dilated(x, conv_w, window_strides=(1,), padding=[(d_conv - 1, 0)], feature_group_count=d_inner, dimension_numbers=('NCH', 'OIH', 'NCH'))
        x = silu(xc + conv_b[None, :, None])
        x_dbl = jnp.einsum('bdl,ed->bel', x, x_proj_w)
        dt_low, Bm, Cm = jnp.split(x_dbl, [dt_rank, dt_rank + d_state], axis=1)
        dt = jnp.einsum('brl,dr->bdl', dt_low, dt_proj_w)
        dt = jax.nn.softplus(dt + dt_proj_b[None, :, None])
        A = -jnp.exp(A_log)
        dt_t = jnp.moveaxis(dt, -1, 0)
        B_t = jnp.moveaxis(Bm, -1, 0)
        C_t = jnp.moveaxis(Cm, -1, 0)
        u_t = jnp.moveaxis(x, -1, 0)

        def step(state, inp):
            d, b, c, u = inp
            dA = jnp.exp(d[..., None] * A)
            state = state * dA + (d * u)[..., None] * b[:, None, :]
            y = jnp.einsum('bdn,bn->bd', state, c)
            return (state, y)
        state0 = jnp.zeros((Bsz, d_inner, d_state), x.dtype)
        _, ys = jax.lax.scan(step, state0, (dt_t, B_t, C_t, u_t))
        y = jnp.moveaxis(ys, 0, 2)
        y = y + D[None, :, None] * x
        y = y * silu(z)
        return jnp.swapaxes(y, 1, 2)

    def _L0_ffn_ref(hidden_states, gate_w, gate_bias, fc1_w, fc2_w, w1, w2, shared_up_w, shared_down_w):
        import jax, jax.numpy as jnp
        import numpy as np
        H, LAT, INTER, E, G, TOPK_G, TOP_K = (512, 256, 256, 32, 4, 2, 8)
        SHARED_INTER = 1024
        ROUTED_SCALE = 2.5
        B, S = (2, 256)

        def relu2(x):
            return jnp.square(jax.nn.relu(x))
        orig_shape = hidden_states.shape
        x = hidden_states.reshape(-1, H)
        T = x.shape[0]
        logits = jnp.einsum('th,eh->te', x.astype(jnp.float32), gate_w)
        scores = jax.nn.sigmoid(logits)
        sb = scores + gate_bias
        grp = sb.reshape(T, G, E // G)
        group_scores = jax.lax.top_k(grp, 2)[0].sum(-1)
        _, gidx = jax.lax.top_k(group_scores, TOPK_G)
        gmask = jax.nn.one_hot(gidx, G, dtype=sb.dtype).sum(1)
        masked = jnp.where(gmask[:, :, None] > 0, grp, -jnp.inf).reshape(T, E)
        _, topi = jax.lax.top_k(masked, TOP_K)
        wsel = jnp.take_along_axis(scores, topi, axis=1)
        wsel = wsel / wsel.sum(-1, keepdims=True) * ROUTED_SCALE
        cw = jnp.zeros((T, E), jnp.float32).at[jnp.arange(T)[:, None], topi].add(wsel)
        x_lat = x @ fc1_w.T
        h = relu2(jnp.einsum('tl,eil->eti', x_lat, w1))
        h = h * cw.T[:, :, None]
        y_lat = jnp.einsum('eti,eli->tl', h, w2)
        routed = y_lat @ fc2_w.T
        shared = relu2(x @ shared_up_w.T) @ shared_down_w.T
        return (shared + routed).reshape(orig_shape)
    x = x + _L0_attn_ref(_layernorm(x, axis=-1), L0_attn_Wq, L0_attn_Wk, L0_attn_Wv, L0_attn_Wo)
    x = x + _L0_xattn_ref(ctx_1024, _layernorm(x, axis=-1), L0_xattn_in_proj_w, L0_xattn_conv_w, L0_xattn_conv_b, L0_xattn_x_proj_w, L0_xattn_dt_proj_w, L0_xattn_dt_proj_b, L0_xattn_A_log, L0_xattn_D)
    x = x + _L0_ffn_ref(_layernorm(x, axis=-1), L0_ffn_gate_w, L0_ffn_gate_bias, L0_ffn_fc1_w, L0_ffn_fc2_w, L0_ffn_w1, L0_ffn_w2, L0_ffn_shared_up_w, L0_ffn_shared_down_w)
    return x

_drawn_inputs = setup_inputs


def setup_inputs(seed=0):
    import zlib

    import numpy as np

    out = dict(_drawn_inputs(seed))
    spreads = {'L0_xattn_D': (1.0, 0.6)}
    factors = {'ctx_1024': 2.897,
     'L0_xattn_in_proj_w': 2.901,
     'L0_xattn_conv_w': 2.961,
     'L0_xattn_conv_b': 8.0,
     'L0_xattn_x_proj_w': 8.0,
     'L0_xattn_dt_proj_w': 8.0,
     'L0_xattn_dt_proj_b': 8.0,
     'L0_xattn_A_log': 8.0,
     'L0_ffn_gate_w': 8.0,
     'L0_ffn_gate_bias': 8.0,
     'L0_ffn_fc1_w': 8.0,
     'L0_ffn_fc2_w': 8.0,
     'L0_ffn_w1': 8.0,
     'L0_ffn_w2': 8.0,
     'L0_ffn_shared_up_w': 8.0,
     'L0_ffn_shared_down_w': 8.0}
    for name, (base, spread) in spreads.items():
        noise = np.random.default_rng([zlib.crc32(name.encode()), seed]).standard_normal(out[name].shape)
        drawn = base * np.exp(spread * noise) if base else spread * noise
        out[name] = jnp.asarray(drawn.astype(out[name].dtype))
    for name, factor in factors.items():
        out[name] = (out[name] * factor).astype(out[name].dtype)
    return out
```

```python
from contextlib import ExitStack

import concourse.bass as bass
from concourse import mybir

F32 = mybir.dt.float32
F32R = mybir.dt.float32r
ACT = mybir.ActivationFunctionType
ALU = mybir.AluOpType
AX_X = mybir.AxisListType.X
P = 128
T = 512
HI, LO = 0, 1
XK_KHI, XK_KLO, XK_ROWS = 8, 9, 10
DT, DTU, Y0 = 0, 1, 2
EPS = 1e-5


class Dims:
    def __init__(self, x, ctx_in, wq, wk, in_proj, xproj, dtproj, a_log, w1):
        self.B, _, self.D = x.shape
        self.C = ctx_in.shape[2]
        self.HD = wk.shape[1]
        self.H = wq.shape[1] // self.HD
        self.KT = self.D // P
        self.CT = self.C // P
        self.ST = T // P
        self.R = dtproj.shape[1]
        self.N = a_log.shape[1]
        self.E, self.I, self.L = w1.shape


def split_matmul(pe, out, lhs_hi, lhs_lo, rhs_hi, rhs_lo, start, stop):
    pe.matmul(out, lhs_hi, rhs_hi, start=start, stop=False)
    pe.matmul(out, lhs_hi, rhs_lo, start=False, stop=False)
    return pe.matmul(out, lhs_lo, rhs_hi, start=False, stop=stop)


def split_matmuls(pe, out, lhs, rhs):
    n = len(lhs)
    for k in range(n):
        last = split_matmul(pe, out, *lhs[k], *rhs[k], k == 0, k == n - 1)
    return last


def layer_norm(dve, chain, n0, src, dst, stats, mv, sc, var_ok, std_ok, std_count, done):
    tiles = src.shape[1]
    for s in range(tiles):
        dve.bn_stats(stats[:, s], src[:, s]).then_inc(chain, 1)
    for s in range(tiles):
        dve.wait_ge(chain, n0 + s + 1)
        dve.bn_aggr(mv[:, s], stats[:, s]).then_inc(chain, 1)
    n = n0 + 2 * tiles
    dve.wait_ge(chain, n)
    dve.tensor_scalar(sc[:, 0], mv[:, :, 1], EPS, None, ALU.add).then_inc(var_ok, 1)
    dve.wait_ge(std_ok, std_count)
    dve.reciprocal(sc[:, 2], sc[:, 1]).then_inc(chain, 1)
    dve.wait_ge(chain, n + 1)
    dve.tensor_tensor(sc[:, 3], sc[:, 0], sc[:, 2], ALU.mult).then_inc(chain, 1)
    dve.wait_ge(chain, n + 2)
    dve.tensor_tensor(sc[:, 4], sc[:, 1], sc[:, 3], ALU.add).then_inc(chain, 1)
    dve.wait_ge(chain, n + 3)
    dve.tensor_scalar(sc[:, 3], sc[:, 4], 0.5, None, ALU.mult).then_inc(chain, 1)
    dve.wait_ge(chain, n + 4)
    dve.reciprocal(sc[:, 5], sc[:, 3]).then_inc(chain, 1)
    dve.wait_ge(chain, n + 5)
    for s in range(tiles):
        done(dve.tensor_scalar(dst[:, s], src[:, s], mv[:, s, 0:1], sc[:, 5, s:s + 1], ALU.subtract, ALU.mult))
    return n + 5


def prepare(nc, dm, g, x, ctx_in, Wq, Wk, Wv, in_proj, conv_w, conv_b, xproj, dtproj, dt_b, a_log, d_skip, scr):
    B, KT, ST, CT, N, R, H, HD = dm.B, dm.KT, dm.ST, dm.CT, dm.N, dm.R, dm.H, dm.HD
    with ExitStack() as ctx:
        sb = lambda n, s, d=F32: ctx.enter_context(nc.sbuf_tensor(n, s, d))
        ps = lambda n: ctx.enter_context(nc.psum_tensor(n, [P, T], F32))
        ident = g.ident
        wraw = sb("wraw", [P, KT, HD * 2])
        wk_sp = sb("wk_sp", [P, 2, KT, HD], F32R)
        wv_sp = sb("wv_sp", [P, 2, KT, HD], F32R)
        wi_nat = sb("wi_nat", [P, KT, dm.C])
        wi_t = sb("wi_t", [P, CT, dm.D])
        xp_nat = sb("xp_nat", [R + 2 * N, dm.D])
        xp_t = sb("xp_t", [P, KT, R + 2 * N])
        dp_nat = sb("dp_nat", [P, KT, R])
        dp_t = sb("dp_t", [R, dm.D])
        cw = sb("cw", [P, KT, 4])
        cb = sb("cb", [P, KT])
        db = sb("db", [P, KT])
        dsk = sb("dsk", [P, KT])
        alog = sb("alog", [P, KT, N])
        wq_in = sb("wq_in", [P, H * HD])
        wq_hi = sb("wq_hi", [P, H * HD], F32R)
        wq_lo = sb("wq_lo", [P, H * HD], F32R)

        x_nat = sb("x_nat", [P, ST, T])
        xn = sb("xn", [P, ST, T])
        stats = sb("stats", [P, ST, 6])
        mv = sb("mv", [P, ST, 2])
        sc = sb("sc", [P, 6, ST])
        xk = sb("xk", [P, XK_ROWS, T], F32R)
        v_t = sb("v_t", [P, T])
        v_nat = sb("v_nat", [P, T])
        c_nat = sb("c_nat", [P, ST, dm.C])
        c_t = sb("c_t", [P, CT, T])
        x_pad = sb("x_pad", [P, KT, T + 4])
        acc = sb("acc", [P, KT, T])
        u = sb("u", [P, KT, T])
        xdbl = sb("xdbl", [R + 2 * N, T])
        vraw = sb("vraw", [P, KT, T])
        ea = sb("ea", [P, KT, T])
        el = sb("el", [P, KT, T])
        ew = sb("ew", [P, KT, T])
        mam = sb("mam", [P, 3, KT, T])

        tpx = [ps("tpx0"), ps("tpx1")]
        cps, kps, vps, mps = ps("cps"), ps("kps"), ps("vps"), ps("mps")
        xps = [ps("xps0"), ps("xps1")]

        names = ("w_in wq_ld wq_h wq_l wq_st ident0 ident1 w_tp w_sb w_spl zpad a_ok x_in c_in xn_ok var_ok "
                 "std_ok tpx_ps xk_hi xk_lo k_ps k_hi k_lo v_ps v_sb c_ps ct_ok x_ps xpad_ok conv u_ok m_ps "
                 "xd_ok dv av e_ok l_ok w_ok r_ok cor_ok dt_ok dtu_ok y0_ok chain xk_st v_st mam_st bc_st lmin").split()
        (w_in, wq_ld, wq_h, wq_l, wq_st, ident0, ident1, w_tp, w_sb, w_spl, zpad, a_ok, x_in, c_in, xn_ok, var_ok,
         std_ok, tpx_ps, xk_hi, xk_lo, k_ps, k_hi, k_lo, v_ps, v_sb, c_ps, ct_ok, x_ps, xpad_ok, conv, u_ok, m_ps,
         xd_ok, dv, av, e_ok, l_ok, w_ok, r_ok, cor_ok, dt_ok, dtu_ok, y0_ok, chain, xk_st, v_st, mam_st,
         bc_st, lmin) = [ctx.enter_context(nc.semaphore("p_" + n)) for n in names]
        block = ctx.enter_context(nc.Block())
        bc_v = scr.bc.rearrange("b n two t -> b two n t")
        wq_v = scr.wq.rearrange("h p two k c -> k two p h c")

        @block.sync
        def _(sp):
            sp.sem_inc(xk_st, 16)
            sp.sem_inc(v_st, 16)
            sp.sem_inc(mam_st, 16)
            sp.sem_inc(bc_st, 32)
            sp.sem_inc(wq_st, 32)
            sp.dma_start(x_nat[:], x[0].rearrange("(s p) f -> p s f", p=P)).then_inc(x_in, 16)
            sp.dma_start(c_nat[:], ctx_in[0].rearrange("(s p) f -> p s f", p=P)).then_inc(c_in, 16)
            for dst, src in ((wi_nat[:], in_proj.rearrange("(k p) c -> p k c", p=P)), (xp_nat[:], xproj),
                             (dp_nat[:], dtproj.rearrange("(k p) r -> p k r", p=P)),
                             (wraw[:, :, 0:HD], Wk.rearrange("(k p) d -> p k d", p=P)),
                             (wraw[:, :, HD:2 * HD], Wv.rearrange("(k p) d -> p k d", p=P)),
                             (cw[:], conv_w.rearrange("(k p) o j -> p k (o j)", p=P)),
                             (cb[:], conv_b.rearrange("(k p) -> p k", p=P)),
                             (db[:], dt_b.rearrange("(k p) -> p k", p=P)),
                             (dsk[:], d_skip.rearrange("(k p) -> p k", p=P)),
                             (alog[:], a_log.rearrange("(k p) n -> p k n", p=P))):
                sp.dma_start(dst, src, allow_slow_non_contiguous=True).then_inc(w_in, 16)

            def weights(b):
                sp.wait_ge(wq_st, b * 32 + 32)
                sp.dma_start(wq_in[:], Wq.rearrange("(k p) n -> k p n", p=P)[b]).then_inc(wq_ld, 16)

            def stores(b):
                sp.wait_ge(wq_h, b + 1)
                sp.dma_start(wq_v[b, HI], wq_hi[:].bitcast(F32).rearrange("p (h c) -> p h c", c=HD)).then_inc(wq_st, 16)
                sp.wait_ge(wq_l, b + 1)
                sp.dma_start(wq_v[b, LO], wq_lo[:].bitcast(F32).rearrange("p (h c) -> p h c", c=HD)).then_inc(wq_st, 16)
                sp.wait_ge(v_sb, b * 2 + 3)
                sp.dma_start(scr.v[b], v_nat[:]).then_inc(v_st, 16)
                sp.wait_ge(xk_lo, b * 4 + 4 + 2)
                sp.wait_ge(k_lo, b + 2)
                sp.dma_start(scr.xk[b], xk[:].bitcast(F32)).then_inc(xk_st, 16)
                sp.wait_ge(xd_ok, b + 1)
                for two in range(2):
                    sp.dma_start(bc_v[b, two], xdbl[R + two * N:R + (two + 1) * N, :]).then_inc(bc_st, 16)
                sp.wait_ge(dtu_ok, b + 2)
                sp.wait_ge(y0_ok, b * 4 + 4)
                sp.dma_start(scr.mam[b], mam[:]).then_inc(mam_st, 16)

            for b in range(B - 1):
                weights(b)
                sp.wait_ge(xn_ok, b * 4 + 4)
                sp.dma_start(x_nat[:], x[b + 1].rearrange("(s p) f -> p s f", p=P)).then_inc(x_in, 16)
                sp.wait_ge(c_ps, b * 2 + 2)
                sp.dma_start(c_nat[:], ctx_in[b + 1].rearrange("(s p) f -> p s f", p=P)).then_inc(c_in, 16)
                stores(b)
            weights(B - 1)
            stores(B - 1)
            sp.wait_ge(wq_st, 32 * B + 32)
            sp.wait_ge(mam_st, 16 * B + 16)
            sp.wait_ge(xk_st, 16 * B + 16)
            sp.wait_ge(v_st, 16 * B + 16)
            sp.wait_ge(bc_st, 32 * B + 32)

        @block.gpsimd
        def _(pool):
            pool.sem_inc(cor_ok, 1)
            pool.sem_inc(dt_ok, 1)
            pool.sem_inc(dtu_ok, 1)
            pool.memset(ident[:], 0.0).then_inc(ident0, 1)
            pool.memset(x_pad[:, :, 0:3], 0.0).then_inc(zpad, 1)
            pool.wait_ge(ident0, 1)
            pool.affine_select(out=ident[:], in_=ident[:], compare_op=ALU.not_equal, fill=1.0, base=0,
                               pattern=[[-1, P]], channel_multiplier=1).then_inc(ident1, 1)
            with pool.Fori(0, B) as b:
                pool.wait_ge(wq_h, b + 1)
                pool.tensor_tensor(wq_lo[:], wq_in[:], wq_hi[:].bitcast(F32), ALU.subtract).then_inc(wq_l, 1)
                pool.wait_ge(lmin, b + 1)
                pool.tensor_tensor(ew[:], ea[:], ew[:], ALU.subtract).then_inc(cor_ok, 1)
                pool.wait_ge(r_ok, b + 2)
                pool.wait_ge(cor_ok, b + 2)
                pool.wait_ge(mam_st, b * 16 + 16)
                pool.tensor_tensor(mam[:, DT], vraw[:], ew[:], ALU.add).then_inc(dt_ok, 1)
                pool.wait_ge(dt_ok, b + 2)
                pool.wait_ge(u_ok, b * 4 + 4 + 4)
                pool.tensor_tensor(mam[:, DTU], mam[:, DT], u[:], ALU.mult).then_inc(dtu_ok, 1)

        @block.scalar
        def _(act):
            act.sem_inc(ct_ok, 1)
            act.sem_inc(xpad_ok, 2)
            act.sem_inc(u_ok, 4)
            act.sem_inc(v_sb, 1)
            act.wait_ge(w_tp, 1)
            act.copy(wi_t[:, 0], tpx[0][:]).then_inc(w_sb, 1)
            act.wait_ge(w_tp, 2)
            act.copy(wi_t[:, 1], tpx[1][:]).then_inc(w_sb, 1)
            act.wait_ge(w_tp, 3)
            act.copy(xp_t[:], cps[:, 0:KT * (R + 2 * N)]).then_inc(w_sb, 1)
            act.wait_ge(w_tp, 4)
            act.copy(dp_t[:], kps[0:R, :]).then_inc(w_sb, 1)
            act.wait_ge(w_in, 160)
            act.activation(alog[:], alog[:], ACT.Exp).then_inc(a_ok, 1)
            with act.Fori(0, B) as b:
                act.wait_ge(var_ok, b + 1)
                act.activation(sc[:, 1], sc[:, 0], ACT.Sqrt).then_inc(std_ok, 1)
                for k in range(KT):
                    if k == 0:
                        act.wait_ge(xk_st, b * 16 + 16)
                    act.wait_ge(tpx_ps, b * 4 + k + 1 + 4)
                    act.copy(xk[:, k], tpx[k % 2][:]).then_inc(xk_hi, 1)
                for k in range(CT):
                    act.wait_ge(c_ps, b * 2 + k + 1)
                    act.copy(c_t[:, k], cps[:]).then_inc(ct_ok, 1)
                for e in range(KT):
                    act.wait_ge(x_ps, b * 4 + e + 1)
                    act.wait_ge(conv, b * 16 + 13 + e)
                    act.copy(x_pad[:, e, 3:3 + T], xps[e % 2][:]).then_inc(xpad_ok, 1)
                act.wait_ge(k_ps, b + 1)
                act.copy(xk[:, XK_KHI], kps[:]).then_inc(k_hi, 1)
                act.wait_ge(v_ps, b * 2 + 1)
                act.copy(v_t[:], vps[:]).then_inc(v_sb, 1)
                act.wait_ge(v_ps, b * 2 + 2)
                act.wait_ge(v_st, b * 16 + 16)
                act.copy(v_nat[:], vps[:]).then_inc(v_sb, 1)
                for e in range(KT):
                    if e == 0:
                        act.wait_ge(m_ps, b * 5 + 1)
                        act.wait_ge(dtu_ok, b + 1)
                    act.wait_ge(conv, b * 16 + 12 + e + 1 + 16)
                    act.activation(u[:, e], acc[:, e], ACT.Silu).then_inc(u_ok, 1)
                act.wait_ge(m_ps, b * 5 + 1 + 5)
                act.wait_ge(bc_st, b * 32 + 32)
                act.copy(xdbl[:], mps[0:R + 2 * N, :]).then_inc(xd_ok, 1)
                act.wait_ge(av, b + 1)
                act.activation(ea[:], ea[:], ACT.Exp).then_inc(e_ok, 1)
                act.wait_ge(e_ok, b + 1)
                act.wait_ge(r_ok, b + 1)
                act.activation(el[:], ea[:], ACT.Ln, bias=1.0).then_inc(l_ok, 1)
                act.wait_ge(mam_st, b * 16 + 16)
                act.wait_ge(u_ok, b * 4 + 4 + 4)
                for e in range(KT):
                    act.activation(mam[:, Y0, e], u[:, e], ACT.Copy, scale=dsk[:, e:e + 1]).then_inc(y0_ok, 1)

        @block.vector
        def _(dve):
            dve.sem_inc(xk_lo, 2)
            dve.sem_inc(k_lo, 1)
            dve.sem_inc(conv, 16)
            dve.sem_inc(dv, 1)
            dve.sem_inc(r_ok, 1)
            dve.wait_ge(w_in, 160)
            dve.tensor_copy(wk_sp[:, HI], wraw[:, :, 0:HD]).then_inc(w_spl, 1)
            dve.tensor_copy(wv_sp[:, HI], wraw[:, :, HD:2 * HD]).then_inc(w_spl, 1)
            dve.wait_ge(w_spl, 2)
            dve.tensor_tensor(wk_sp[:, LO], wraw[:, :, 0:HD], wk_sp[:, HI].bitcast(F32), ALU.subtract).then_inc(w_spl, 1)
            dve.tensor_tensor(wv_sp[:, LO], wraw[:, :, HD:2 * HD], wv_sp[:, HI].bitcast(F32),
                              ALU.subtract).then_inc(w_spl, 1)
            dve.wait_ge(a_ok, 1)
            dve.tensor_scalar(g.a_neg[:].rearrange("p n k -> p k n"), alog[:], -1.0, None, ALU.mult).then_inc(a_ok, 1)
            dve.wait_ge(zpad, 1)
            with dve.Fori(0, B) as b:
                dve.wait_ge(wq_ld, b * 16 + 16)
                dve.wait_ge(wq_st, b * 32 + 32)
                dve.tensor_copy(wq_hi[:], wq_in[:]).then_inc(wq_h, 1)
                dve.wait_ge(x_in, b * 16 + 16)
                dve.wait_ge(tpx_ps, b * 4 + 4)
                n = layer_norm(dve, chain, 0, x_nat, xn, stats, mv, sc, var_ok, std_ok, b + 1,
                               lambda ins: ins.then_inc(xn_ok, 1))
                dve.wait_ge(chain, n)
                dve.wait_ge(xn_ok, b * 4 + 4)
                dve.sem_clear(chain)
                for k in range(KT):
                    dve.wait_ge(xk_hi, b * 4 + k + 1)
                    dve.tensor_tensor(xk[:, 4 + k], tpx[k % 2][:], xk[:, k].bitcast(F32), ALU.subtract).then_inc(xk_lo, 1)
                for j in range(4):
                    for e in range(KT):
                        if j == 0:
                            dve.wait_ge(xpad_ok, b * 4 + e + 1 + 2)
                            dve.wait_ge(u_ok, b * 4 + e + 1)
                            ins = dve.tensor_scalar(acc[:, e], x_pad[:, e, 3:3 + T], cw[:, e, 3:4], cb[:, e:e + 1],
                                                    ALU.mult, ALU.add)
                        else:
                            dve.wait_ge(conv, b * 16 + (j - 1) * 4 + e + 1 + 16)
                            ins = dve.scalar_tensor_tensor(acc[:, e], x_pad[:, e, 3 - j:3 - j + T],
                                                           cw[:, e, 3 - j:4 - j], acc[:, e], ALU.mult, ALU.add)
                        ins.then_inc(conv, 1)
                dve.wait_ge(k_hi, b + 1)
                dve.tensor_tensor(xk[:, XK_KLO], kps[:], xk[:, XK_KHI].bitcast(F32), ALU.subtract).then_inc(k_lo, 1)
                for e in range(KT):
                    dve.wait_ge(m_ps, b * 5 + e + 2 + 5)
                    dve.wait_ge(dt_ok, b + 1)
                    dve.tensor_scalar(vraw[:, e], mps[:], db[:, e:e + 1], None, ALU.add).then_inc(dv, 1)
                dve.wait_ge(dv, b * 4 + 4 + 1)
                dve.wait_ge(cor_ok, b + 1)
                dve.scalar_tensor_tensor(ea[:], vraw[:], -1.0, vraw[:], ALU.mult, ALU.min).then_inc(av, 1)
                dve.wait_ge(e_ok, b + 1)
                dve.tensor_scalar(ew[:], ea[:], 1.0, -1.0, ALU.add, ALU.add).then_inc(w_ok, 1)
                dve.wait_ge(l_ok, b + 1)
                dve.wait_ge(w_ok, b + 1)
                dve.tensor_tensor(el[:], el[:], ew[:], ALU.min).then_inc(lmin, 1)
                dve.wait_ge(lmin, b + 1)
                dve.scalar_tensor_tensor(vraw[:], vraw[:], 0.0, el[:], ALU.max, ALU.add).then_inc(r_ok, 1)

        @block.tensor
        def _(pe):
            pe.sem_inc(tpx_ps, 4)
            pe.sem_inc(m_ps, 5)
            pe.wait_ge(ident1, 1)
            pe.wait_ge(w_in, 160)
            for c in range(CT):
                for k in range(KT):
                    last = pe.transpose(tpx[c][:, k * P:k * P + P], wi_nat[:, k, c * P:c * P + P], ident[:])
                last.then_inc(w_tp, 1)
            for k in range(KT):
                w = R + 2 * N
                last = pe.transpose(cps[:, k * w:k * w + w], xp_nat[:, k * P:k * P + P], ident[0:w, 0:w])
            last.then_inc(w_tp, 1)
            for k in range(KT):
                last = pe.transpose(kps[0:R, k * P:k * P + P], dp_nat[:, k, :], ident[:])
            last.then_inc(w_tp, 1)
            pe.wait_ge(w_sb, 4)
            pe.wait_ge(w_spl, 4)
            with pe.Fori(0, B) as b:
                for k in range(KT):
                    if k == 0:
                        pe.wait_ge(xn_ok, b * 4 + 4)
                    pe.wait_ge(xk_lo, b * 4 + k + 1)
                    for s in range(ST):
                        last = pe.transpose(tpx[k % 2][:, s * P:s * P + P], xn[:, s, k * P:k * P + P], ident[:])
                    last.then_inc(tpx_ps, 1)
                for k in range(CT):
                    if k == 0:
                        pe.wait_ge(c_in, b * 16 + 16)
                    pe.wait_ge(ct_ok, b * 2 + k + 1)
                    for s in range(ST):
                        last = pe.transpose(cps[:, s * P:s * P + P], c_nat[:, s, k * P:k * P + P], ident[:])
                    last.then_inc(c_ps, 1)
                pe.wait_ge(ct_ok, b * 2 + 2 + 1)
                for e in range(KT):
                    pe.wait_ge(xpad_ok, b * 4 + e + 1)
                    for k in range(CT):
                        last = pe.matmul(xps[e % 2][:], wi_t[:, k, e * P:e * P + P], c_t[:, k], start=k == 0, stop=k == CT - 1)
                    last.then_inc(x_ps, 1)
                pe.wait_ge(xk_lo, b * 4 + 4 + 2)
                rhs = [(xk[:, k], xk[:, 4 + k]) for k in range(KT)]
                pe.wait_ge(k_lo, b + 1)
                split_matmuls(pe, kps[:], [(wk_sp[:, HI, k], wk_sp[:, LO, k]) for k in range(KT)], rhs).then_inc(k_ps, 1)
                pe.wait_ge(v_sb, b * 2 + 1)
                split_matmuls(pe, vps[:], [(wv_sp[:, HI, k], wv_sp[:, LO, k]) for k in range(KT)], rhs).then_inc(v_ps, 1)
                pe.wait_ge(v_sb, b * 2 + 2)
                for s in range(ST):
                    last = pe.transpose(vps[:, s * P:s * P + P], v_t[:, s * P:s * P + P], ident[:])
                last.then_inc(v_ps, 1)
                pe.wait_ge(u_ok, b * 4 + 4 + 4)
                pe.wait_ge(dv, b * 4 + 1)
                for e in range(KT):
                    last = pe.matmul(mps[0:R + 2 * N, :], xp_t[:, e], u[:, e], start=e == 0, stop=e == KT - 1)
                last.then_inc(m_ps, 1)
                pe.wait_ge(xd_ok, b + 1)
                for e in range(KT):
                    if e:
                        pe.wait_ge(dv, b * 4 + e + 1)
                    pe.matmul(mps[:], dp_t[:, e * P:e * P + P], xdbl[0:R, :], start=True, stop=True).then_inc(m_ps, 1)


def attention_and_scan(nc, dm, g, x, Wo, scr):
    B, KT, ST, N, H, HD = dm.B, dm.KT, dm.ST, dm.N, dm.H, dm.HD
    GH = 4
    TPB = H // GH
    TURNS = B * TPB
    NG = N // TPB
    PIECES = NG * KT
    SCALE = float(HD) ** -0.5
    RING = 4
    with ExitStack() as ctx:
        sb = lambda n, s, d=F32: ctx.enter_context(nc.sbuf_tensor(n, s, d))
        ps = lambda n: ctx.enter_context(nc.psum_tensor(n, [P, T], F32))
        ident = g.ident
        xk_s = sb("xk_s", [P, 2, XK_ROWS, T], F32R)
        wq_s = sb("wq_s", [P, GH, 2, KT, HD], F32R)
        wo_s = sb("wo_s", [P, 2, GH, dm.D])
        v_s = sb("v_s", [P, T])
        q_s = sb("q_s", [P, 2, 2, T], F32R)
        p_s = sb("p_s", [P, 2, ST, T])
        pt_s = sb("pt_s", [P, 2, T])
        o_s = sb("o_s", [P, GH, T])
        xa = sb("xa", [P, 2, ST, T])
        mam_s = sb("mam_s", [P, 2, 3, KT, T])
        d_a = sb("d_a", [P, RING, T])
        hb = sb("hb", [P, RING, T])
        bcs = sb("bcs", [P, 2, 2, T])
        nmax = sb("nmax", [P, GH * ST])
        rsum = sb("rsum", [P, GH * ST])
        rinv = sb("rinv", [P, GH * ST])
        qps, ops = ps("qps"), ps("ops")
        sps = [ps("sps0"), ps("sps1")]
        tps = [ps("tps0"), ps("tps1")]
        ups = [ps("ups0"), ps("ups1")]
        names = ("xk_in v_in wo_in x_in mam_in q_ps q_hi q_lo s_ps smax p_exp rc p_nrm t_ps pt_sb pv o_sb out_ps acc "
                 "m_da m_dbu m_scan m_prod m_add x1_st y_st").split()
        (xk_in, v_in, wo_in, x_in, mam_in, q_ps, q_hi, q_lo, s_ps, smax, p_exp, rc, p_nrm, t_ps, pt_sb, pv, o_sb,
         out_ps, acc, m_da, m_dbu, m_scan, m_prod, m_add, x1_st, y_st) = [
            ctx.enter_context(nc.semaphore("a_" + n)) for n in names]
        wq_in = [ctx.enter_context(nc.semaphore(f"a_wq_in{j}")) for j in range(GH)]
        bc_in = [ctx.enter_context(nc.semaphore(f"a_bc_in{j}")) for j in range(2)]
        block = ctx.enter_context(nc.Block())
        PLAN = [2, 5, 3, 3, 3]
        FIRST = [sum(PLAN[:i]) for i in range(5)]

        def part(i):
            return range(FIRST[i], FIRST[i] + PLAN[i])

        @block.sync
        def _(sp):
            def load_xk(b):
                sp.dma_start(xk_s[:, b % 2].bitcast(F32), scr.xk[b]).then_inc(xk_in, 16)

            def load_wq(G):
                sp.dma_start(wq_s[:, G % GH].bitcast(F32), scr.wq[G % H]).then_inc(wq_in[G % GH], 16)

            def load_bc(n):
                sp.dma_start(bcs[:, n % 2], scr.bc[n // N, n % N].rearrange("(o t) c -> o t c", o=1)
                             .to_broadcast([P, 2, T])).then_inc(bc_in[n % 2], 16)

            def load_mam(b):
                sp.dma_start(mam_s[:, b % 2], scr.mam[b]).then_inc(mam_in, 16)

            def load_x(b):
                sp.dma_start(xa[:, b % 2], x[b].rearrange("(s p) f -> p s f", p=P)).then_inc(x_in, 16)

            def load_wo(it):
                h0 = it % TPB * GH
                sp.dma_start(wo_s[:, it % 2], Wo[h0 * HD:(h0 + GH) * HD, :].rearrange("(h p) f -> p h f", p=P))\
                    .then_inc(wo_in, 16)

            load_wq(0)
            load_xk(0)
            load_bc(0)
            load_mam(0)
            for G in range(1, GH):
                load_wq(G)
            load_bc(1)
            sp.dma_start(v_s[:], scr.v[0]).then_inc(v_in, 16)
            load_x(0)
            for it in range(TURNS):
                for j in range(GH):
                    G = it * GH + j
                    if 2 <= G + 1 < TURNS * NG:
                        sp.wait_ge(m_prod, G * KT)
                        load_bc(G + 1)
                    if G + GH < B * H:
                        sp.wait_ge(q_ps, G + 1)
                        load_wq(G + GH)
                    if j == 0 and it:
                        sp.wait_ge(pv, G * ST + 2)
                        sp.dma_start(v_s[:], scr.v[it // TPB]).then_inc(v_in, 16)
                    b = it // TPB
                    if j == 1:
                        if it >= 2:
                            sp.wait_ge(out_ps, (it - 1) * ST + 4)
                            sp.wait_ge(wo_in, it * 16)
                        load_wo(it)
                    if it % TPB == 0 and j == 1 and b + 1 < B:
                        if b:
                            sp.wait_ge(s_ps, it * GH * ST + 8)
                            sp.wait_ge(xk_in, 16 * (b + 1))
                        load_xk(b + 1)
                    if it % TPB == 0 and j == 2 and b:
                        sp.wait_ge(acc, it * ST + 2)
                        sp.dma_start(scr.x1[b - 1], xa[:, (b - 1) % 2]).then_inc(x1_st, 16)
                        sp.wait_ge(m_add, it * PIECES + 4)
                        sp.dma_start(scr.y[b - 1], mam_s[:, (b - 1) % 2, Y0]).then_inc(y_st, 16)
                    if it % TPB == 0 and j == 3 and b + 1 < B:
                        if b:
                            sp.wait_ge(x1_st, 16 * b)
                            sp.wait_ge(x_in, 16 * (b + 1))
                        load_x(b + 1)
                        if b:
                            sp.wait_ge(y_st, 16 * b)
                            sp.wait_ge(mam_in, 16 * (b + 1))
                        load_mam(b + 1)
            sp.wait_ge(m_add, TURNS * PIECES + 4)
            sp.dma_start(scr.y[B - 1], mam_s[:, (B - 1) % 2, Y0]).then_inc(y_st, 16)
            sp.wait_ge(acc, TURNS * ST + 2)
            sp.dma_start(scr.x1[B - 1], xa[:, (B - 1) % 2]).then_inc(x1_st, 16)
            sp.wait_ge(x1_st, 16 * B)
            sp.wait_ge(y_st, 16 * B)

        def turns(eng, body):
            body(0, 0, 0, 0, 0, True, False)
            with eng.Fori(1, TURNS) as it:
                body(it, eng.snap(it * GH), eng.snap(it * PIECES), eng.snap(it // TPB % 2),
                     eng.snap((it - 1) // TPB % 2), False, False)
            body(TURNS, TURNS * GH, TURNS * PIECES, 0, (TURNS - 1) // TPB % 2, False, True)

        @block.tensor
        def _(pe):
            pe.sem_inc(s_ps, 8)
            pe.sem_inc(t_ps, 8)
            pe.sem_inc(pv, 2)
            pe.sem_inc(out_ps, 4)

            def project(it, g4, slot, j):
                pe.wait_ge(wq_in[j], it * 16 + 16)
                pe.wait_ge(q_lo, g4 + (j + 1))
                if j == 0:
                    pe.wait_ge(xk_in, it // TPB * 16 + 16)
                split_matmuls(pe, qps[:], [(wq_s[:, j, HI, k], wq_s[:, j, LO, k]) for k in range(KT)],
                              [(xk_s[:, slot, k], xk_s[:, slot, 4 + k]) for k in range(KT)]).then_inc(q_ps, 1)

            def scores(g4, g16, slot, j, s):
                i = j * ST + s
                if s == 0:
                    pe.wait_ge(q_lo, g4 + (j + 2))
                pe.wait_ge(p_exp, g16 + (i + 1))
                c = slice(s * P, s * P + P)
                split_matmul(pe, sps[s % 2][:], q_s[:, j % 2, HI, c], q_s[:, j % 2, LO, c], xk_s[:, slot, XK_KHI],
                             xk_s[:, slot, XK_KLO], True, True).then_inc(s_ps, 1)

            def transpose(g16, j, t):
                i = j * ST + t
                if t == 0:
                    pe.wait_ge(p_nrm, g16 + (j * ST + ST))
                pe.wait_ge(pt_sb, g16 + (i + 1))
                for s in range(ST):
                    last = pe.transpose(tps[t % 2][:, s * P:s * P + P], p_s[:, j % 2, s, t * P:t * P + P], ident[:])
                last.then_inc(t_ps, 1)

            def values(it, g4, g16, j, t):
                i = j * ST + t
                if t == 0:
                    if j == 0:
                        pe.wait_ge(v_in, it * 16 + 16)
                    pe.wait_ge(o_sb, g4 + (j + 1))
                pe.wait_ge(pt_sb, g16 + (i + 3))
                pe.matmul(ops[:], v_s[:, t * P:t * P + P], pt_s[:, t % 2], start=t == 0, stop=t == ST - 1)\
                    .then_inc(pv, 1)

            def output(it, g4, g16, s):
                if s == 0:
                    pe.wait_ge(o_sb, g4 + 1)
                    pe.wait_ge(wo_in, it * 16)
                pe.wait_ge(acc, g4 + (s - ST + 1))
                for h in range(GH):
                    last = pe.matmul(ups[s % 2][:], o_s[:, h, s * P:s * P + P], wo_s[:, (it - 1) % 2, h],
                                     start=h == 0, stop=h == GH - 1)
                last.then_inc(out_ps, 1)

            def body(it, g4, g16, slot, prev, first, last):
                if not last:
                    project(it, g4, slot, 0)
                if not first:
                    for t in range(ST):
                        transpose(g16, -1, t)
                        if t:
                            values(it, g4, g16, -1, t - 1)
                    values(it, g4, g16, -1, ST - 1)
                if not last:
                    project(it, g4, slot, 1)
                for s in range(ST):
                    if not last:
                        scores(g4, g16, slot, 0, s)
                    if not first:
                        output(it, g4, g16, s)
                if last:
                    return
                for j in range(1, GH):
                    for s in range(ST):
                        scores(g4, g16, slot, j, s)
                        transpose(g16, j - 1, s)
                        if s:
                            values(it, g4, g16, j - 1, s - 1)
                    values(it, g4, g16, j - 1, ST - 1)
                    if j + 1 < GH:
                        project(it, g4, slot, j + 1)

            turns(pe, body)

        @block.scalar
        def _(act):
            act.sem_inc(p_exp, 2)
            act.sem_inc(pt_sb, 2)
            act.sem_inc(o_sb, 1)

            def q_high(g4, g16, j):
                act.wait_ge(q_ps, g4 + (j + 1))
                act.wait_ge(s_ps, g16 + (j * ST + 4))
                act.activation(q_s[:, j % 2, HI], qps[:], ACT.Copy, scale=SCALE).then_inc(q_hi, 1)

            def exps(g16, j, s):
                i = j * ST + s
                if s == 0:
                    act.wait_ge(t_ps, g16 + (j * ST + 4))
                act.wait_ge(smax, g16 + (i + 1))
                act.activation(p_s[:, j % 2, s], sps[s % 2][:], ACT.Exp, bias=nmax[:, i:i + 1],
                               accum_out=rsum[:, i:i + 1]).then_inc(p_exp, 1)

            def pt_out(g16, j, t):
                i = j * ST + t
                act.wait_ge(t_ps, g16 + (i + 1 + 8))
                act.wait_ge(pv, g16 + (i + 1))
                act.copy(pt_s[:, t % 2], tps[t % 2][:]).then_inc(pt_sb, 1)

            def o_out(g4, g16, j):
                if j == 0:
                    act.wait_ge(out_ps, g4 + 4)
                act.wait_ge(pv, g16 + (j * ST + ST + 2))
                act.copy(o_s[:, j % GH], ops[:]).then_inc(o_sb, 1)

            def decay(it, g16, slot, k):
                if k == 0:
                    act.wait_ge(mam_in, it // TPB * 16 + 16)
                act.wait_ge(m_scan, g16 + (k + 1))
                n = it % TPB * NG + k // KT
                act.activation(d_a[:, k % RING], mam_s[:, slot, DT, k % KT], ACT.Exp,
                               scale=g.a_neg[:, n, k % KT:k % KT + 1]).then_inc(m_da, 1)

            def body(it, g4, g16, slot, prev, first, last):
                pieces = [iter(part(i)) if not last else iter(()) for i in range(5)]

                def decays(i, n=1):
                    for k in range(n):
                        m = next(pieces[i], None)
                        if m is not None:
                            decay(it, g16, slot, m)

                if not last:
                    q_high(g4, g16, 0)
                if not first:
                    for t in range(ST):
                        pt_out(g16, -1, t)
                        if t % 2 == 0:
                            decays(0)
                    o_out(g4, g16, -1)
                decays(0, 9)
                if last:
                    return
                q_high(g4, g16, 1)
                decays(1)
                for s in range(ST):
                    exps(g16, 0, s)
                    decays(1)
                for j in range(1, GH):
                    for s in range(ST):
                        pt_out(g16, j - 1, s)
                        exps(g16, j, s)
                        decays(1 + j)
                    o_out(g4, g16, j - 1)
                    if j + 1 < GH:
                        q_high(g4, g16, j + 1)

            turns(act, body)

        @block.vector
        def _(dve):
            dve.sem_inc(q_lo, 1)
            dve.sem_inc(acc, 2)
            dve.sem_inc(m_scan, 4)

            def q_low(g4, j):
                dve.wait_ge(q_hi, g4 + (j + 1))
                dve.scalar_tensor_tensor(q_s[:, j % 2, LO], qps[:], SCALE, q_s[:, j % 2, HI].bitcast(F32),
                                         ALU.mult, ALU.subtract).then_inc(q_lo, 1)

            def row_max(g16, j, s):
                i = j * ST + s
                dve.wait_ge(s_ps, g16 + (i + 1 + 8))
                dve.tensor_reduce(nmax[:, i:i + 1], sps[s % 2][:], axis=AX_X, op=ALU.max, negate=True).then_inc(smax, 1)

            def normalise(g16, j, s):
                i = j * ST + s
                dve.wait_ge(p_exp, g16 + (i + 1 + 2))
                dve.reciprocal(rinv[:, i:i + 1], rsum[:, i:i + 1]).then_inc(rc, 1)
                dve.wait_ge(rc, g16 + (i + 1))
                dve.tensor_scalar(p_s[:, j % 2, s], p_s[:, j % 2, s], rinv[:, i:i + 1], None, ALU.mult)\
                    .then_inc(p_nrm, 1)

            def add_out(it, g4, prev, s):
                if s == 0:
                    dve.wait_ge(x_in, (it - 1) // TPB * 16 + 16)
                dve.wait_ge(out_ps, g4 + (s + 1))
                dve.wait_ge(acc, g4 + (s - ST + 2))
                dve.tensor_tensor(xa[:, prev, s], ups[s % 2][:], xa[:, prev, s], ALU.add).then_inc(acc, 1)

            def scan(g16, k):
                dve.wait_ge(m_da, g16 + (k + 1))
                dve.wait_ge(m_dbu, g16 + (k + 1))
                dve.tensor_tensor_scan(hb[:, k % RING], d_a[:, k % RING], hb[:, k % RING], 0.0, ALU.mult, ALU.add)\
                    .then_inc(m_scan, 1)

            def times_c(g16, k):
                dve.wait_ge(m_scan, g16 + (k + 1 + 4))
                dve.tensor_tensor(hb[:, k % RING], hb[:, k % RING], bcs[:, k // KT % 2, 1], ALU.mult).then_inc(m_prod, 1)

            def body(it, g4, g16, slot, prev, first, last):
                pieces = [iter(part(i)) if not last else iter(()) for i in range(5)]

                def scans(i, n=1):
                    for k in range(n):
                        m = next(pieces[i], None)
                        if m is not None:
                            scan(g16, m)
                            if m or not first:
                                times_c(g16, m - 1)

                if not last:
                    q_low(g4, 0)
                scans(0, 9)
                if last:
                    times_c(g16, -1)
                else:
                    q_low(g4, 1)
                scans(1)
                for s in range(ST):
                    if not last:
                        row_max(g16, 0, s)
                    scans(1)
                    if not last and s:
                        normalise(g16, 0, s - 1)
                    if not first:
                        add_out(it, g4, prev, s)
                if last:
                    return
                normalise(g16, 0, ST - 1)
                for j in range(1, GH):
                    for s in range(ST):
                        row_max(g16, j, s)
                        scans(1 + j)
                        if s:
                            normalise(g16, j, s - 1)
                    normalise(g16, j, ST - 1)
                    if j + 1 < GH:
                        q_low(g4, j + 1)

            turns(dve, body)

        @block.gpsimd
        def _(pool):
            pool.sem_inc(m_add, 4)

            def dbu(it, g16, slot, k):
                if k == 0:
                    pool.wait_ge(mam_in, it // TPB * 16 + 16)
                n = k // KT
                if k % KT == 0:
                    pool.wait_ge(bc_in[n % 2], it * (NG // 2 * 16) + (n // 2 + 1) * 16)
                pool.wait_ge(m_add, g16 + (k + 1))
                pool.tensor_tensor(hb[:, k % RING], mam_s[:, slot, DTU, k % KT], bcs[:, n % 2, 0], ALU.mult)\
                    .then_inc(m_dbu, 1)

            def add_y(g16, slot, k):
                pool.wait_ge(m_prod, g16 + (k + 1))
                pool.wait_ge(m_add, g16 + (k + 1))
                y = mam_s[:, slot, Y0, k % KT]
                pool.tensor_tensor(y, y, hb[:, k % RING], ALU.add).then_inc(m_add, 1)

            def body(it, g4, g16, slot, prev, first, last):
                for k in range(PIECES if not last else 2):
                    if not last:
                        dbu(it, g16, slot, k)
                    if k >= 2:
                        add_y(g16, slot, k - 2)
                    elif not first:
                        add_y(g16, prev, k - 2)

            for b in range(B):
                body(b * TPB, b * H, b * TPB * PIECES, b % 2, (b - 1) % 2, b == 0, False)
                with pool.Fori(b * TPB + 1, (b + 1) * TPB) as it:
                    body(it, None, pool.snap(it * PIECES), b % 2, b % 2, False, False)
            body(TURNS, None, TURNS * PIECES, 0, (B - 1) % 2, False, True)


def transposed_weights(nc, dm, g, gate_w, fc1_w, fc2_w, up_w, down_w):
    KT, E, L, S = dm.KT, dm.E, dm.L, dm.S
    LT, SJ = L // P, S // P
    with ExitStack() as ctx:
        sb = lambda n, s, d=F32: ctx.enter_context(nc.sbuf_tensor(n, s, d))
        ident = g.ident
        up_n = sb("up_n", [P, SJ, dm.D])
        dn_n = sb("dn_n", [P, KT, S])
        f1_n = sb("f1_n", [P, LT, dm.D])
        f2_n = sb("f2_n", [P, KT, L])
        gt_n = sb("gt_n", [E, dm.D])
        wps = [ctx.enter_context(nc.psum_tensor(f"wps{i}", [P, T], F32)) for i in range(4)]
        gt_in, f1_in, f2_in, up_in, dn_in, w_ps, w_hi, w_lo = [
            ctx.enter_context(nc.semaphore("w_" + n)) for n in "gt_in f1_in f2_in up_in dn_in w_ps w_hi w_lo".split()]
        block = ctx.enter_context(nc.Block())
        items = [(gt_in, [gt_n[:, k * P:k * P + P] for k in range(KT)], g.gate_t[:, HI], g.gate_t[:, LO])]
        for i in range(LT):
            items.append((f1_in, [f1_n[:, i, k * P:k * P + P] for k in range(KT)],
                          g.fc1_t[:, HI, :, i * P:i * P + P], g.fc1_t[:, LO, :, i * P:i * P + P]))
            items.append((f2_in, [f2_n[:, k, i * P:i * P + P] for k in range(KT)], g.fc2_t[:, HI, i], g.fc2_t[:, LO, i]))
        for j in range(SJ):
            items.append((up_in, [up_n[:, j, k * P:k * P + P] for k in range(KT)],
                          g.up_t[:, HI, :, j * P:j * P + P], g.up_t[:, LO, :, j * P:j * P + P]))
        for j in range(SJ):
            items.append((dn_in, [dn_n[:, k, j * P:j * P + P] for k in range(KT)], g.dn_t[:, HI, j], g.dn_t[:, LO, j]))

        def shaped(bank, blocks, like):
            w = blocks[0].shape[0]
            ap = bank[:, 0:len(blocks) * w]
            return ap.rearrange("p (k c) -> p k c", c=w) if len(like.shape) == 3 else ap

        @block.sync
        def _(sp):
            sp.dma_start(gt_n[:], gate_w).then_inc(gt_in, 16)
            sp.dma_start(f1_n[:], fc1_w.rearrange("(j p) f -> p j f", p=P)).then_inc(f1_in, 16)
            sp.dma_start(f2_n[:], fc2_w.rearrange("(j p) f -> p j f", p=P)).then_inc(f2_in, 16)
            sp.dma_start(up_n[:], up_w.rearrange("(j p) f -> p j f", p=P)).then_inc(up_in, 16)
            sp.dma_start(dn_n[:], down_w.rearrange("(j p) f -> p j f", p=P)).then_inc(dn_in, 16)

        @block.tensor
        def _(pe):
            for n, (loaded, blocks, hi, lo) in enumerate(items):
                pe.wait_ge(loaded, 16)
                if n >= 4:
                    pe.wait_ge(w_lo, n - 3)
                for k, blk in enumerate(blocks):
                    w = blk.shape[0]
                    last = pe.transpose(wps[n % 4][:, k * w:k * w + w], blk, ident[0:w, 0:w])
                last.then_inc(w_ps, 1)

        @block.scalar
        def _(act):
            for n, (loaded, blocks, hi, lo) in enumerate(items):
                act.wait_ge(w_ps, n + 1)
                act.copy(hi, shaped(wps[n % 4], blocks, hi)).then_inc(w_hi, 1)

        @block.vector
        def _(dve):
            for n, (loaded, blocks, hi, lo) in enumerate(items):
                dve.wait_ge(w_hi, n + 1)
                dve.tensor_tensor(lo, shaped(wps[n % 4], blocks, hi), hi.bitcast(F32), ALU.subtract).then_inc(w_lo, 1)


def gate_route_shared(nc, dm, g, gate_bias, scr):
    B, KT, ST, E, L, S = dm.B, dm.KT, dm.ST, dm.E, dm.L, dm.S
    LT, SJ = L // P, S // P
    G, TOPG, TOPK, ROUTED = 4, 2, 8, 2.5
    OUT = -1e30
    TAKEN = -3e38
    with ExitStack() as ctx:
        sb = lambda n, s, d=F32: ctx.enter_context(nc.sbuf_tensor(n, s, d))
        ps = lambda n: ctx.enter_context(nc.psum_tensor(n, [P, T], F32))
        ident = g.ident
        x2 = sb("x2", [P, ST, T])
        y_t = sb("y_t", [P, KT, T])
        xn = sb("xn3", [P, ST, T])
        stats = sb("stats3", [P, ST, 6])
        mv = sb("mv3", [P, ST, 2])
        sc = sb("sc3", [P, 6, ST])
        xt = sb("xt", [P, 2, KT, T], F32R)
        s_t = sb("s_t", [P, 2, SJ, T], F32R)
        hr = sb("hr", [P, 2, T])
        bias = sb("bias", [P, E])
        lower = sb("lower", [P, G, G])
        score = sb("score", [P, ST, E])
        sbias = sb("sbias", [P, ST, E])
        top = sb("top", [P, ST, G, 8])
        gs = sb("gs", [P, ST, G])
        gt = sb("gt", [P, ST, G, G])
        eq = sb("eq", [P, ST, G, G])
        rank = sb("rank", [P, ST, G])
        cand = sb("cand", [P, ST, E])
        top8 = sb("top8", [P, ST, 8])
        repl = sb("repl", [P, ST, E])
        cw = sb("cw3", [P, ST, E])
        wsum = sb("wsum", [P, ST])
        winv = sb("winv", [P, ST])
        cw_t = sb("cw_t", [E, T])
        tp = [ps("tp0"), ps("tp1")]
        lg, ct = ps("lg"), ps("ct")
        up = [ps("up0"), ps("up1")]
        dn = [ps("dn0"), ps("dn1")]
        names = ("c_in x_in y_in z_ok var1 std1 sz_ok yt_ps g1 x2_ok var2 std2 xn_ok t_ps xt_hi xt_lo l_ps sc_ok cw_ok "
                 "cwt_ps cwt_sb cw_st f_ps f_hi f_lo u_ps r_ok h_ok h_hi h_lo d_ps d_ok part_st chain low0 low1").split()
        (c_in, x_in, y_in, z_ok, var1, std1, sz_ok, yt_ps, g1, x2_ok, var2, std2, xn_ok, t_ps, xt_hi, xt_lo, l_ps, sc_ok,
         cw_ok, cwt_ps, cwt_sb, cw_st, f_ps, f_hi, f_lo, u_ps, r_ok, h_ok, h_hi, h_lo, d_ps, d_ok, part_st, chain, low0,
         low1) = [ctx.enter_context(nc.semaphore("g_" + n)) for n in names]
        block = ctx.enter_context(nc.Block())

        @block.sync
        def _(sp):
            sp.sem_inc(part_st, 16)
            sp.sem_inc(cw_st, 16)
            sp.dma_start(bias[:], gate_bias.rearrange("(o e) -> o e", o=1).to_broadcast([P, E])).then_inc(c_in, 16)
            for b in range(B):
                if b:
                    sp.wait_ge(part_st, b * 16 + 16)
                sp.dma_start(x2[:], scr.x1[b]).then_inc(x_in, 16)
                if b:
                    sp.wait_ge(yt_ps, b * ST)
                sp.dma_start(y_t[:], scr.y[b]).then_inc(y_in, 16)
                sp.wait_ge(cwt_sb, b + 1)
                sp.dma_start(scr.cw.rearrange("e (b t) -> b e t", b=B)[b], cw_t[:]).then_inc(cw_st, 16)
                sp.wait_ge(d_ok, (b + 1) * ST + 2)
                sp.dma_start(scr.part[b], x2[:]).then_inc(part_st, 16)
            sp.wait_ge(part_st, B * 16 + 16)
            sp.wait_ge(cw_st, B * 16 + 16)

        @block.gpsimd
        def _(pool):
            pool.sem_inc(h_lo, 2)
            pool.memset(lower[:], 1.0).then_inc(low0, 1)
            pool.wait_ge(low0, 1)
            pool.affine_select(out=lower[:], in_=lower[:], compare_op=ALU.is_gt, fill=0.0, base=0,
                               pattern=[[1, G], [-1, G]], channel_multiplier=0).then_inc(low1, 1)
            with pool.Fori(0, B) as b:
                for j in range(SJ):
                    pool.wait_ge(h_hi, b * SJ + j + 1)
                    pool.tensor_tensor(s_t[:, LO, j], hr[:, j % 2], s_t[:, HI, j].bitcast(F32), ALU.subtract)\
                        .then_inc(h_lo, 1)

        @block.scalar
        def _(act):
            act.sem_inc(r_ok, 2)
            with act.Fori(0, B) as b:
                act.wait_ge(var1, b + 1)
                act.activation(sc[:, 1], sc[:, 0], ACT.Sqrt).then_inc(std1, 1)
                for s in range(ST):
                    act.wait_ge(z_ok, b * ST + s + 1)
                    act.activation(xn[:, s], xn[:, s], ACT.Silu).then_inc(sz_ok, 1)
                act.wait_ge(var2, b + 1)
                act.activation(sc[:, 1], sc[:, 0], ACT.Sqrt).then_inc(std2, 1)
                for k in range(KT):
                    act.wait_ge(t_ps, b * KT + k + 1)
                    if k == 0:
                        act.wait_ge(u_ps, b * SJ + 8)
                    act.copy(xt[:, HI, k], tp[k % 2][:]).then_inc(xt_hi, 1)
                act.wait_ge(l_ps, b + 1)
                act.activation(score[:], lg[:, 0:ST * E], ACT.Sigmoid).then_inc(sc_ok, 1)
                for i in range(LT):
                    act.wait_ge(f_ps, b * LT + i + 1)
                    act.copy(g.xl[:, HI, i, bass.ds(b * T, T)], dn[i % 2][:]).then_inc(f_hi, 1)
                def relu(j):
                    act.wait_ge(u_ps, b * SJ + j + 1 + 8)
                    act.wait_ge(h_lo, b * SJ + j + 1)
                    act.activation(hr[:, j % 2], up[j % 2][:], ACT.Relu).then_inc(r_ok, 1)

                def high(j):
                    if j == 0:
                        act.wait_ge(d_ps, b * ST + 4)
                    act.wait_ge(h_ok, b * SJ + j + 1)
                    act.copy(s_t[:, HI, j], hr[:, j % 2]).then_inc(h_hi, 1)

                for j in range(SJ):
                    relu(j)
                    if j:
                        high(j - 1)
                high(SJ - 1)
                act.wait_ge(cwt_ps, b + 1)
                act.wait_ge(cw_st, b * 16 + 16)
                act.copy(cw_t[:], ct[0:E, :]).then_inc(cwt_sb, 1)

        @block.vector
        def _(dve):
            dve.sem_inc(x2_ok, 2)
            dve.sem_inc(xt_lo, 2)
            dve.sem_inc(d_ok, 2)
            dve.sem_inc(f_lo, 2)
            dve.wait_ge(c_in, 16)
            dve.wait_ge(low1, 1)
            with dve.Fori(0, B) as b:
                dve.wait_ge(x_in, b * 16 + 16)
                n = layer_norm(dve, chain, 0, x2, xn, stats, mv, sc, var1, std1, b + 1, lambda i: i.then_inc(z_ok, 1))
                dve.wait_ge(chain, n)
                dve.wait_ge(y_in, b * 16 + 16)
                for s in range(ST):
                    dve.wait_ge(sz_ok, b * ST + s + 1)
                    dve.tensor_tensor(y_t[:, s], y_t[:, s], xn[:, s], ALU.mult).then_inc(g1, 1)
                for s in range(ST):
                    dve.wait_ge(yt_ps, b * ST + s + 1)
                    dve.tensor_tensor(x2[:, s], x2[:, s], tp[s % 2][:], ALU.add).then_inc(x2_ok, 1)
                dve.wait_ge(x2_ok, b * ST + ST + 2)
                n2 = layer_norm(dve, chain, n, x2, xn, stats, mv, sc, var2, std2, b + 1, lambda i: i.then_inc(xn_ok, 1))
                for k in range(KT):
                    dve.wait_ge(xt_hi, b * KT + k + 1)
                    dve.tensor_tensor(xt[:, LO, k], tp[k % 2][:], xt[:, HI, k].bitcast(F32), ALU.subtract).then_inc(xt_lo, 1)

                m = [n2]

                def step(ins, *waits):
                    m[0] += 1
                    ins.then_inc(chain, 1)

                def settled():
                    dve.wait_ge(chain, m[0])

                settled()
                dve.wait_ge(sc_ok, b + 1)
                step(dve.tensor_tensor(sbias[:], score[:], bias[:].unsqueeze(1).to_broadcast([P, ST, E]), ALU.add))
                settled()
                for s in range(ST):
                    for q in range(G):
                        step(dve.max(top[:, s, q], sbias[:, s, q * (E // G):(q + 1) * (E // G)]))
                settled()
                step(dve.tensor_tensor(gs[:], top[:, :, :, 0], top[:, :, :, 1], ALU.add))
                settled()
                for s in range(ST):
                    mine = gs[:, s].unsqueeze(2).to_broadcast([P, G, G])
                    other = gs[:, s].unsqueeze(1).to_broadcast([P, G, G])
                    step(dve.tensor_tensor(gt[:, s], other, mine, ALU.is_gt))
                    step(dve.tensor_tensor(eq[:, s], other, mine, ALU.is_equal))
                settled()
                for s in range(ST):
                    step(dve.tensor_tensor(eq[:, s], eq[:, s], lower[:], ALU.mult))
                settled()
                step(dve.tensor_tensor(gt[:], gt[:], eq[:], ALU.add))
                settled()
                step(dve.tensor_reduce(rank[:], gt[:], axis=AX_X, op=ALU.add))
                settled()
                step(dve.tensor_scalar(rank[:], rank[:], TOPG - 0.5, OUT, ALU.is_gt, ALU.mult))
                settled()
                for s in range(ST):
                    step(dve.tensor_tensor(cand[:, s].rearrange("p (g e) -> p g e", g=G),
                                           sbias[:, s].rearrange("p (g e) -> p g e", g=G),
                                           rank[:, s].unsqueeze(2).to_broadcast([P, G, E // G]), ALU.add))
                settled()
                for s in range(ST):
                    step(dve.max(top8[:, s], cand[:, s]))
                settled()
                for s in range(ST):
                    step(dve.match_replace(repl[:, s], top8[:, s], cand[:, s], TAKEN))
                settled()
                step(dve.scalar_tensor_tensor(cw[:], repl[:], TAKEN, score[:], ALU.is_equal, ALU.mult))
                settled()
                step(dve.tensor_reduce(wsum[:], cw[:], axis=AX_X, op=ALU.add))
                settled()
                step(dve.reciprocal(winv[:], wsum[:]))
                settled()
                for s in range(ST):
                    step(dve.tensor_scalar(cw[:, s], cw[:, s], winv[:, s:s + 1], ROUTED, ALU.mult, ALU.mult))
                settled()
                dve.sem_clear(chain)
                dve.sem_inc(cw_ok, 1)

                for i in range(LT):
                    dve.wait_ge(f_hi, b * LT + i + 1)
                    dve.tensor_tensor(g.xl[:, LO, i, bass.ds(b * T, T)], dn[i % 2][:],
                                      g.xl[:, HI, i, bass.ds(b * T, T)].bitcast(F32), ALU.subtract).then_inc(f_lo, 1)
                for j in range(SJ):
                    dve.wait_ge(r_ok, b * SJ + j + 1 + 2)
                    dve.tensor_tensor(hr[:, j % 2], hr[:, j % 2], hr[:, j % 2], ALU.mult).then_inc(h_ok, 1)
                for s in range(ST):
                    dve.wait_ge(d_ps, b * ST + s + 1 + 4)
                    dve.tensor_tensor(x2[:, s], x2[:, s], dn[s % 2][:], ALU.add).then_inc(d_ok, 1)

        @block.tensor
        def _(pe):
            pe.sem_inc(u_ps, 8)
            pe.sem_inc(d_ps, 4)
            with pe.Fori(0, B) as b:
                for s in range(ST):
                    if s == 0:
                        pe.wait_ge(g1, b * ST + ST)
                        pe.wait_ge(xt_lo, b * KT + 2)
                    pe.wait_ge(x2_ok, b * ST + s + 1)
                    for k in range(KT):
                        last = pe.transpose(tp[s % 2][:, k * P:k * P + P], y_t[:, k, s * P:s * P + P], ident[:])
                    last.then_inc(yt_ps, 1)
                for k in range(KT):
                    if k == 0:
                        pe.wait_ge(xn_ok, b * ST + ST)
                    pe.wait_ge(xt_lo, b * KT + k + 1)
                    for s in range(ST):
                        last = pe.transpose(tp[k % 2][:, s * P:s * P + P], xn[:, s, k * P:k * P + P], ident[:])
                    last.then_inc(t_ps, 1)
                pe.wait_ge(xt_lo, b * KT + KT + 2)
                for s in range(ST):
                    c = slice(s * P, s * P + P)
                    last = split_matmuls(pe, lg[:, s * E:s * E + E], [(xt[:, HI, k, c], xt[:, LO, k, c]) for k in range(KT)],
                                         [(g.gate_t[:, HI, k * E:k * E + E], g.gate_t[:, LO, k * E:k * E + E])
                                          for k in range(KT)])
                last.then_inc(l_ps, 1)
                x_t = [(xt[:, HI, k], xt[:, LO, k]) for k in range(KT)]
                for i in range(LT):
                    pe.wait_ge(d_ok, b * ST + 2)
                    c = slice(i * P, i * P + P)
                    split_matmuls(pe, dn[i % 2][:], [(g.fc1_t[:, HI, k, c], g.fc1_t[:, LO, k, c]) for k in range(KT)],
                                  x_t).then_inc(f_ps, 1)
                for j in range(SJ):
                    pe.wait_ge(r_ok, b * SJ + j + 1)
                    c = slice(j * P, j * P + P)
                    split_matmuls(pe, up[j % 2][:], [(g.up_t[:, HI, k, c], g.up_t[:, LO, k, c]) for k in range(KT)],
                                  x_t).then_inc(u_ps, 1)
                pe.wait_ge(cw_ok, b + 1)
                for s in range(ST):
                    last = pe.transpose(ct[0:E, s * P:s * P + P], cw[:, s], ident[:])
                last.then_inc(cwt_ps, 1)
                pe.wait_ge(h_lo, b * SJ + SJ + 2)
                pe.wait_ge(f_lo, b * LT + LT + 2)
                for s in range(ST):
                    pe.wait_ge(d_ok, b * ST + s + 1)
                    c = slice(s * P, s * P + P)
                    split_matmuls(pe, dn[s % 2][:], [(s_t[:, HI, j, c], s_t[:, LO, j, c]) for j in range(SJ)],
                                  [(g.dn_t[:, HI, j], g.dn_t[:, LO, j]) for j in range(SJ)]).then_inc(d_ps, 1)


def routed_experts(nc, dm, g, w1, w2, scr):
    E, I, L, B = dm.E, dm.I, dm.L, dm.B
    IT, LT = I // P, L // P
    HALVES = 2
    HTOK = B * T // HALVES
    TC = HTOK // T
    TILES = TC * IT
    with ExitStack() as ctx:
        sb = lambda n, s, d=F32: ctx.enter_context(nc.sbuf_tensor(n, s, d))
        ps = lambda n: ctx.enter_context(nc.psum_tensor(n, [P, T], F32))
        ident = g.ident
        w_nat = sb("w_nat", [P, 2, 2, IT * L])
        w_s = sb("w_s", [P, 2, 2, 2, T], F32R)
        cwb = sb("cwb", [P, 2, HTOK])
        rt = sb("rt", [P, 2, T])
        rc = sb("rc", [P, 2, T])
        hf = sb("hf", [P, TILES, T])
        h_s = sb("h_s", [P, TILES, 2, T], F32R)
        yps = [[ps(f"y{l}{c}") for c in range(TC)] for l in range(LT)]
        zps = [ps("z0"), ps("z1")]
        wps = [ps("wt0"), ps("wt1")]
        names = "wt_ps w_hi w_lo z_ps r_ok c_ok h_ok hh_ok hl_ok y_ps ye_hi ye_lo".split()
        (wt_ps, w_hi, w_lo, z_ps, r_ok, c_ok, h_ok, hh_ok, hl_ok, y_ps, ye_hi, ye_lo) = [
            ctx.enter_context(nc.semaphore("e_" + n)) for n in names]
        w_in = [ctx.enter_context(nc.semaphore(f"e_w_in{q}")) for q in range(2)]
        cw_in = [ctx.enter_context(nc.semaphore(f"e_cw_in{q}")) for q in range(2)]
        block = ctx.enter_context(nc.Block())

        @block.sync
        def _(sp):
            for X in range(HALVES * E):
                q, e, half = X % 2, X % E, X // E
                if X >= 2:
                    sp.wait_ge(wt_ps, 2 * (X - 2) + 2)
                for m, w in ((0, w1), (1, w2)):
                    sp.dma_start(w_nat[:, q, m], w[e].rearrange("(a p) c -> p a c", p=P)).then_inc(w_in[q], 16)
                if X >= 2:
                    sp.wait_ge(c_ok, TILES * (X - 2) + TILES)
                sp.dma_start(cwb[:, q], scr.cw[e:e + 1, half * HTOK:(half + 1) * HTOK].to_broadcast([P, HTOK]))\
                    .then_inc(cw_in[q], 16)

        def halves(eng, expert, finish):
            for half in range(HALVES):
                X0 = half * E
                for q in range(2):
                    expert(X0 + q, q, half, 2 * (X0 + q), TILES * (X0 + q), half * (E // 2), q == 0)
                with eng.Fori(1, E // 2) as pair:
                    x2_, x4_ = eng.snap(pair * 4 + 2 * X0), eng.snap(pair * (2 * TILES) + TILES * X0)
                    for q in range(2):
                        expert(None, q, half, x2_ + 2 * q, x4_ + TILES * q, pair + half * (E // 2), False)
                finish(half, X0 + E)

        @block.tensor
        def _(pe):
            pe.sem_inc(y_ps, 8)

            def down(q, n2, n4, first, last):
                pe.wait_ge(w_lo, n2 + (2 + 2))
                for c in range(TC):
                    for i in range(IT):
                        n = c * IT + i
                        pe.wait_ge(hl_ok, n4 + (n + 1 + TILES))
                        for l in range(LT):
                            col = slice(i * L + l * P, i * L + l * P + P)
                            ins = split_matmul(pe, yps[l][c][:], w_s[:, q, 1, HI, col], w_s[:, q, 1, LO, col],
                                               h_s[:, n, HI], h_s[:, n, LO], first and i == 0, last and i == IT - 1)
                        ins.then_inc(y_ps, 1)

            def expert(X, q, half, n2, n4, pair, first):
                pe.wait_ge(w_in[q], pair * 32 + 32)
                for m in range(2):
                    pe.wait_ge(w_lo, n2 + (m + 1))
                    for a in range(2):
                        for c in range(2):
                            col = a * 2 * P + c * P
                            last = pe.transpose(wps[m][:, col:col + P],
                                                w_nat[:, q, m, c * 2 * P + a * P:c * 2 * P + a * P + P], ident[:])
                    last.then_inc(wt_ps, 1)
                if not first:
                    is_first = X is not None and X % E == 1
                    if is_first and half:
                        pe.wait_ge(ye_lo, half * LT * TC)
                    down(1 - q, n2 - 2, n4 - TILES, is_first, False)
                pe.wait_ge(w_lo, n2 + (1 + 2))
                for c in range(TC):
                    for i in range(IT):
                        n = c * IT + i
                        pe.wait_ge(r_ok, n4 + (n + 1))
                        tok = slice(half * HTOK + c * T, half * HTOK + c * T + T)
                        split_matmuls(pe, zps[n % 2][:],
                                      [(w_s[:, q, 0, HI, l * I + i * P:l * I + i * P + P],
                                        w_s[:, q, 0, LO, l * I + i * P:l * I + i * P + P]) for l in range(LT)],
                                      [(g.xl[:, HI, l, tok], g.xl[:, LO, l, tok]) for l in range(LT)]).then_inc(z_ps, 1)

            def finish(half, X):
                down(1, 2 * X - 2, TILES * X - TILES, False, True)

            halves(pe, expert, finish)

        @block.scalar
        def _(act):
            act.sem_inc(r_ok, 2)

            def expert(X, q, half, n2, n4, pair, first):
                for m in range(2):
                    act.wait_ge(wt_ps, n2 + (m + 1))
                    if m == 0:
                        act.wait_ge(y_ps, n4 + 4)
                    act.copy(w_s[:, q, m, HI], wps[m][:]).then_inc(w_hi, 1)
                for n in range(TILES + 1):
                    if n < TILES:
                        act.wait_ge(z_ps, n4 + (n + 1))
                        act.wait_ge(h_ok, n4 + (n + 1))
                        act.activation(rt[:, n % 2], zps[n % 2][:], ACT.Relu).then_inc(r_ok, 1)
                    if n:
                        act.wait_ge(h_ok, n4 + (n + 2))
                        act.wait_ge(y_ps, n4 + (n - 1 + 5))
                        act.copy(h_s[:, n - 1, HI], hf[:, n - 1]).then_inc(hh_ok, 1)

            def finish(half, X):
                for l in range(LT):
                    for c in range(TC):
                        act.wait_ge(y_ps, TILES * X + 8)
                        tok = slice(half * HTOK + c * T, half * HTOK + c * T + T)
                        act.copy(g.yl[:, HI, l, tok], yps[l][c][:]).then_inc(ye_hi, 1)

            halves(act, expert, finish)

        @block.gpsimd
        def _(pool):
            def expert(X, q, half, n2, n4, pair, first):
                pool.wait_ge(cw_in[q], pair * 16 + 16)
                for n in range(TILES):
                    c = n // IT
                    pool.wait_ge(r_ok, n4 + (n + 1 + 2))
                    pool.wait_ge(h_ok, n4 + (n + 1))
                    pool.tensor_tensor(rc[:, n % 2], rt[:, n % 2], cwb[:, q, c * T:c * T + T], ALU.mult).then_inc(c_ok, 1)

            halves(pool, expert, lambda half, X: None)

        @block.vector
        def _(dve):
            dve.sem_inc(w_lo, 2)
            dve.sem_inc(h_ok, 2)
            dve.sem_inc(hl_ok, TILES)

            def expert(X, q, half, n2, n4, pair, first):
                for m in range(2):
                    dve.wait_ge(w_hi, n2 + (m + 1))
                    dve.tensor_tensor(w_s[:, q, m, LO], wps[m][:], w_s[:, q, m, HI].bitcast(F32), ALU.subtract)\
                        .then_inc(w_lo, 1)
                for n in range(TILES + 1):
                    if n < TILES:
                        dve.wait_ge(c_ok, n4 + (n + 1))
                        dve.wait_ge(hl_ok, n4 + (n + 1))
                        dve.tensor_tensor(hf[:, n], rc[:, n % 2], rt[:, n % 2], ALU.mult).then_inc(h_ok, 1)
                    if n:
                        dve.wait_ge(hh_ok, n4 + n)
                        dve.tensor_tensor(h_s[:, n - 1, LO], hf[:, n - 1], h_s[:, n - 1, HI].bitcast(F32),
                                          ALU.subtract).then_inc(hl_ok, 1)

            def finish(half, X):
                for l in range(LT):
                    for c in range(TC):
                        dve.wait_ge(ye_hi, half * LT * TC + l * TC + c + 1)
                        tok = slice(half * HTOK + c * T, half * HTOK + c * T + T)
                        dve.tensor_tensor(g.yl[:, LO, l, tok], yps[l][c][:], g.yl[:, HI, l, tok].bitcast(F32),
                                          ALU.subtract).then_inc(ye_lo, 1)

            halves(dve, expert, finish)


def routed_output(nc, dm, g, scr, out):
    B, ST, LT = dm.B, dm.ST, dm.L // P
    with ExitStack() as ctx:
        part = ctx.enter_context(nc.sbuf_tensor("part", [P, B, ST, T], F32))
        ops = [ctx.enter_context(nc.psum_tensor(f"o{i}", [P, T], F32)) for i in range(4)]
        o_ps, o_ok, o_st = [ctx.enter_context(nc.semaphore("o_" + n)) for n in "ps ok st".split()]
        p_in = [ctx.enter_context(nc.semaphore(f"o_in{b}")) for b in range(B)]
        block = ctx.enter_context(nc.Block())

        @block.sync
        def _(sp):
            for b in range(B):
                sp.dma_start(part[:, b], scr.part[b]).then_inc(p_in[b], 16)
            for b in range(B):
                sp.wait_ge(o_ok, (b + 1) * ST)
                sp.dma_start(out[b].rearrange("(s p) f -> p s f", p=P), part[:, b]).then_inc(o_st, 16)
            sp.wait_ge(o_st, 16 * B)

        @block.tensor
        def _(pe):
            for n in range(B * ST):
                if n >= 4:
                    pe.wait_ge(o_ok, n - 3)
                c = slice(n * P, n * P + P)
                split_matmuls(pe, ops[n % 4][:], [(g.yl[:, HI, l, c], g.yl[:, LO, l, c]) for l in range(LT)],
                              [(g.fc2_t[:, HI, l], g.fc2_t[:, LO, l]) for l in range(LT)]).then_inc(o_ps, 1)

        @block.vector
        def _(dve):
            for n in range(B * ST):
                b, s = n // ST, n % ST
                if s == 0:
                    dve.wait_ge(p_in[b], 16)
                dve.wait_ge(o_ps, n + 1)
                dve.tensor_tensor(part[:, b, s], part[:, b, s], ops[n % 4][:], ALU.add).then_inc(o_ok, 1)


class Held:
    pass


class Scratch:
    pass


def program(nc, a, out):
    dm = Dims(a["x"], a["ctx_1024"], a["L0_attn_Wq"], a["L0_attn_Wk"], a["L0_xattn_in_proj_w"], a["L0_xattn_x_proj_w"],
              a["L0_xattn_dt_proj_w"], a["L0_xattn_A_log"], a["L0_ffn_w1"])
    dm.S = a["L0_ffn_shared_up_w"].shape[0]
    scr = Scratch()
    dram = lambda n, s, d=F32: nc.dram_tensor("s_" + n, s, d, kind="Internal").ap()
    scr.wq = dram("wq", [dm.H, P, 2, dm.KT, dm.HD])
    scr.xk = dram("xk", [dm.B, P, XK_ROWS, T])
    scr.v = dram("v", [dm.B, P, T])
    scr.mam = dram("mam", [dm.B, P, 3, dm.KT, T])
    scr.bc = dram("bc", [dm.B, dm.N, 2, T])
    scr.x1 = dram("x1", [dm.B, P, dm.ST, dm.D])
    scr.part = dram("part", [dm.B, P, dm.ST, dm.D])
    scr.cw = dram("cw", [dm.E, dm.B * T])
    scr.y = dram("y", [dm.B, P, dm.KT, T])
    with ExitStack() as ctx:
        g = Held()
        g.ident = ctx.enter_context(nc.sbuf_tensor("ident", [P, P], F32))
        g.a_neg = ctx.enter_context(nc.sbuf_tensor("a_neg", [P, dm.N, dm.KT], F32))
        prepare(nc, dm, g, a["x"], a["ctx_1024"], a["L0_attn_Wq"], a["L0_attn_Wk"], a["L0_attn_Wv"],
                a["L0_xattn_in_proj_w"], a["L0_xattn_conv_w"], a["L0_xattn_conv_b"], a["L0_xattn_x_proj_w"],
                a["L0_xattn_dt_proj_w"], a["L0_xattn_dt_proj_b"], a["L0_xattn_A_log"], a["L0_xattn_D"], scr)
        attention_and_scan(nc, dm, g, a["x"], a["L0_attn_Wo"], scr)
        held = lambda n, s: ctx.enter_context(nc.sbuf_tensor(n, s, F32R))
        g.fc2_t = held("fc2_t", [P, 2, dm.L // P, dm.D])
        g.xl = held("xl", [P, 2, dm.L // P, dm.B * T])
        with ExitStack() as shared:
            held = lambda n, s: shared.enter_context(nc.sbuf_tensor(n, s, F32R))
            g.gate_t = held("gate_t", [P, 2, dm.KT * dm.E])
            g.fc1_t = held("fc1_t", [P, 2, dm.KT, dm.L])
            g.up_t = held("up_t", [P, 2, dm.KT, dm.S])
            g.dn_t = held("dn_t", [P, 2, dm.S // P, dm.D])
            transposed_weights(nc, dm, g, a["L0_ffn_gate_w"], a["L0_ffn_fc1_w"], a["L0_ffn_fc2_w"],
                               a["L0_ffn_shared_up_w"], a["L0_ffn_shared_down_w"])
            gate_route_shared(nc, dm, g, a["L0_ffn_gate_bias"], scr)
        g.yl = ctx.enter_context(nc.sbuf_tensor("yl", [P, 2, dm.L // P, dm.B * T], F32R))
        routed_experts(nc, dm, g, a["L0_ffn_w1"], a["L0_ffn_w2"], scr)
        routed_output(nc, dm, g, scr, out)


_INS = ['x', 'ctx_1024', 'L0_attn_Wq', 'L0_attn_Wk', 'L0_attn_Wv', 'L0_attn_Wo', 'L0_xattn_in_proj_w',
        'L0_xattn_conv_w', 'L0_xattn_conv_b', 'L0_xattn_x_proj_w', 'L0_xattn_dt_proj_w', 'L0_xattn_dt_proj_b',
        'L0_xattn_A_log', 'L0_xattn_D', 'L0_ffn_gate_w', 'L0_ffn_gate_bias', 'L0_ffn_fc1_w', 'L0_ffn_fc2_w',
        'L0_ffn_w1', 'L0_ffn_w2', 'L0_ffn_shared_up_w', 'L0_ffn_shared_down_w']


def kernel(**inputs):
    import numpy as np
    import concourse.bacc as bacc
    from concourse.bass_utils import run_bass_kernel_spmd

    nc = bacc.Bacc("TRN2", target_bir_lowering=False, num_devices=1)
    arrays, a = {}, {}
    for name in _INS:
        arrays["in_" + name] = v = np.ascontiguousarray(inputs[name])
        a[name] = nc.dram_tensor("in_" + name, v.shape, mybir.dt.from_np(v.dtype), kind="ExternalInput").ap()
    out = nc.dram_tensor("out_0", inputs["x"].shape, F32, kind="ExternalOutput").ap()
    program(nc, a, out)
    r = run_bass_kernel_spmd(nc, [arrays], core_ids=[0])
    return r.results[0]["out_0"]
```

```python
from contextlib import ExitStack

import concourse.bass as bass
from concourse import mybir

F32 = mybir.dt.float32
F32R = mybir.dt.float32r
ACT = mybir.ActivationFunctionType
ALU = mybir.AluOpType
AX_X = mybir.AxisListType.X
P = 128
T = 512
HI, LO = 0, 1
XK_KHI, XK_KLO, XK_ROWS = 8, 9, 10
DT, DTU, Y0 = 0, 1, 2
EPS = 1e-5


class Dims:
    def __init__(self, x, ctx_in, wq, wk, in_proj, xproj, dtproj, a_log, w1):
        self.B, _, self.D = x.shape
        self.C = ctx_in.shape[2]
        self.HD = wk.shape[1]
        self.H = wq.shape[1] // self.HD
        self.KT = self.D // P
        self.CT = self.C // P
        self.ST = T // P
        self.R = dtproj.shape[1]
        self.N = a_log.shape[1]
        self.E, self.I, self.L = w1.shape


def split_matmul(pe, out, lhs_hi, lhs_lo, rhs_hi, rhs_lo, start, stop):
    pe.matmul(out, lhs_hi, rhs_hi, start=start, stop=False)
    pe.matmul(out, lhs_hi, rhs_lo, start=False, stop=False)
    return pe.matmul(out, lhs_lo, rhs_hi, start=False, stop=stop)


def split_matmuls(pe, out, lhs, rhs):
    n = len(lhs)
    for k in range(n):
        last = split_matmul(pe, out, *lhs[k], *rhs[k], k == 0, k == n - 1)
    return last


def free_semaphores(nc, sems):
    nc.clear_and_free_semaphores(sems)
    nc.all_engine_barrier()


def layer_norm(dve, chain, n0, src, dst, stats, mv, sc, var_ok, std_ok, std_count, done):
    tiles = src.shape[1]
    for s in range(tiles):
        dve.bn_stats(stats[:, s], src[:, s]).then_inc(chain, 1)
    for s in range(tiles):
        dve.wait_ge(chain, n0 + s + 1)
        dve.bn_aggr(mv[:, s], stats[:, s]).then_inc(chain, 1)
    n = n0 + 2 * tiles
    dve.wait_ge(chain, n)
    dve.tensor_scalar(sc[:, 0], mv[:, :, 1], EPS, None, ALU.add).then_inc(var_ok, 1)
    dve.wait_ge(std_ok, std_count)
    dve.reciprocal(sc[:, 2], sc[:, 1]).then_inc(chain, 1)
    dve.wait_ge(chain, n + 1)
    dve.tensor_tensor(sc[:, 3], sc[:, 0], sc[:, 2], ALU.mult).then_inc(chain, 1)
    dve.wait_ge(chain, n + 2)
    dve.tensor_tensor(sc[:, 4], sc[:, 1], sc[:, 3], ALU.add).then_inc(chain, 1)
    dve.wait_ge(chain, n + 3)
    dve.tensor_scalar(sc[:, 3], sc[:, 4], 0.5, None, ALU.mult).then_inc(chain, 1)
    dve.wait_ge(chain, n + 4)
    dve.reciprocal(sc[:, 5], sc[:, 3]).then_inc(chain, 1)
    dve.wait_ge(chain, n + 5)
    for s in range(tiles):
        done(dve.tensor_scalar(dst[:, s], src[:, s], mv[:, s, 0:1], sc[:, 5, s:s + 1], ALU.subtract, ALU.mult))
    return n + 5


def prepare(nc, dm, g, x, ctx_in, Wq, Wk, Wv, Wo, in_proj, conv_w, conv_b, xproj, dtproj, dt_b, a_log, d_skip, scr):
    B, KT, ST, CT, N, R, H, HD = dm.B, dm.KT, dm.ST, dm.CT, dm.N, dm.R, dm.H, dm.HD
    with ExitStack() as ctx:
        sb = lambda n, s, d=F32: ctx.enter_context(nc.sbuf_tensor(n, s, d))
        ps = lambda n: ctx.enter_context(nc.psum_tensor(n, [P, T], F32))
        ident = g.ident
        wraw = sb("wraw", [P, KT, HD * 2])
        wk_sp = sb("wk_sp", [P, 2, KT, HD], F32R)
        wv_sp = sb("wv_sp", [P, 2, KT, HD], F32R)
        wi_nat = sb("wi_nat", [P, KT, dm.C])
        wi_t = sb("wi_t", [P, CT, dm.D])
        xp_nat = sb("xp_nat", [R + 2 * N, dm.D])
        xp_t = sb("xp_t", [P, KT, R + 2 * N])
        dp_nat = sb("dp_nat", [P, KT, R])
        dp_t = sb("dp_t", [R, dm.D])
        cw = sb("cw", [P, KT, 4])
        cb = sb("cb", [P, KT])
        db = sb("db", [P, KT])
        dsk = sb("dsk", [P, KT])
        alog = sb("alog", [P, KT, N])
        wq_in = sb("wq_in", [P, H * HD])
        wq_hi = sb("wq_hi", [P, H * HD], F32R)
        wq_lo = sb("wq_lo", [P, H * HD], F32R)
        wo_in = sb("wo_in", [P, H // B, dm.D])
        wo_sp = sb("wo_sp", [P, H // B, 2, dm.D], F32R)

        x_nat = sb("x_nat", [P, ST, T])
        xn = sb("xn", [P, ST, T])
        stats = sb("stats", [P, ST, 6])
        mv = sb("mv", [P, ST, 2])
        sc = sb("sc", [P, 6, ST])
        xk = sb("xk", [P, XK_ROWS, T], F32R)
        v_t = sb("v_t", [P, T])
        v_nat = sb("v_nat", [P, T])
        c_nat = sb("c_nat", [P, ST, dm.C])
        c_t = sb("c_t", [P, CT, T])
        x_pad = sb("x_pad", [P, KT, T + 4])
        acc = sb("acc", [P, KT, T])
        u = sb("u", [P, KT, T])
        xdbl = sb("xdbl", [R + 2 * N, T])
        vraw = sb("vraw", [P, KT, T])
        ea = sb("ea", [P, KT, T])
        el = sb("el", [P, KT, T])
        ew = sb("ew", [P, KT, T])
        mam = sb("mam", [P, 3, KT, T])

        tpx = [ps("tpx0"), ps("tpx1")]
        cps, kps, vps, mps = ps("cps"), ps("kps"), ps("vps"), ps("mps")
        xps = [ps("xps0"), ps("xps1")]

        names = ("w_in wq_ld wq_h wq_l wq_st ident0 ident1 w_tp w_sb w_spl zpad a_ok x_in c_in xn_ok var_ok "
                 "std_ok tpx_ps xk_hi xk_lo k_ps k_hi k_lo v_ps v_sb c_ps ct_ok x_ps xpad_ok conv u_ok m_ps "
                 "xd_ok dv av e_ok l_ok w_ok r_ok cor_ok dt_ok dtu_ok y0_ok chain xk_st v_st mam_st bc_st lmin wo_ld wo_h wo_l wo_st").split()
        (w_in, wq_ld, wq_h, wq_l, wq_st, ident0, ident1, w_tp, w_sb, w_spl, zpad, a_ok, x_in, c_in, xn_ok, var_ok,
         std_ok, tpx_ps, xk_hi, xk_lo, k_ps, k_hi, k_lo, v_ps, v_sb, c_ps, ct_ok, x_ps, xpad_ok, conv, u_ok, m_ps,
         xd_ok, dv, av, e_ok, l_ok, w_ok, r_ok, cor_ok, dt_ok, dtu_ok, y0_ok, chain, xk_st, v_st, mam_st,
         bc_st, lmin, wo_ld, wo_h, wo_l, wo_st) = sems = [nc.alloc_semaphore("p_" + n) for n in names]
        ctx.callback(free_semaphores, nc, sems)
        block = ctx.enter_context(nc.Block())
        bc_v = scr.bc.rearrange("b n two t -> b two n t")
        wo_v = scr.wo.rearrange("(b h) p two f -> b p h two f", b=B)
        wq_v = scr.wq.rearrange("h p two k c -> k two p h c")

        @block.sync
        def _(sp):
            sp.sem_inc(xk_st, 16)
            sp.sem_inc(v_st, 16)
            sp.sem_inc(mam_st, 16)
            sp.sem_inc(bc_st, 32)
            sp.sem_inc(wq_st, 32)
            sp.dma_start(x_nat[:], x[0].rearrange("(s p) f -> p s f", p=P)).then_inc(x_in, 16)
            sp.dma_start(c_nat[:], ctx_in[0].rearrange("(s p) f -> p s f", p=P)).then_inc(c_in, 16)
            for dst, src in ((wi_nat[:], in_proj.rearrange("(k p) c -> p k c", p=P)), (xp_nat[:], xproj),
                             (dp_nat[:], dtproj.rearrange("(k p) r -> p k r", p=P)),
                             (wraw[:, :, 0:HD], Wk.rearrange("(k p) d -> p k d", p=P)),
                             (wraw[:, :, HD:2 * HD], Wv.rearrange("(k p) d -> p k d", p=P)),
                             (cw[:], conv_w.rearrange("(k p) o j -> p k (o j)", p=P)),
                             (cb[:], conv_b.rearrange("(k p) -> p k", p=P)),
                             (db[:], dt_b.rearrange("(k p) -> p k", p=P)),
                             (dsk[:], d_skip.rearrange("(k p) -> p k", p=P)),
                             (alog[:], a_log.rearrange("(k p) n -> p k n", p=P))):
                sp.dma_start(dst, src, allow_slow_non_contiguous=True).then_inc(w_in, 16)

            sp.sem_inc(wo_st, 16)

            def weights(b):
                sp.wait_ge(wo_st, b * 16 + 16)
                sp.dma_start(wo_in[:], Wo.rearrange("(b h p) f -> b p h f", p=P, b=B)[b]).then_inc(wo_ld, 16)
                sp.wait_ge(wq_st, b * 32 + 32)
                sp.dma_start(wq_in[:], Wq.rearrange("(k p) n -> k p n", p=P)[b]).then_inc(wq_ld, 16)

            def stores(b):
                sp.wait_ge(wq_h, b + 1)
                sp.dma_start(wq_v[b, HI], wq_hi[:].bitcast(F32).rearrange("p (h c) -> p h c", c=HD)).then_inc(wq_st, 16)
                sp.wait_ge(wq_l, b + 1)
                sp.dma_start(wq_v[b, LO], wq_lo[:].bitcast(F32).rearrange("p (h c) -> p h c", c=HD)).then_inc(wq_st, 16)
                sp.wait_ge(wo_l, b + 1)
                sp.dma_start(wo_v[b], wo_sp[:].bitcast(F32)).then_inc(wo_st, 16)
                sp.wait_ge(v_sb, b * 2 + 3)
                sp.dma_start(scr.v[b], v_nat[:]).then_inc(v_st, 16)
                sp.wait_ge(xk_lo, b * 4 + 4 + 2)
                sp.wait_ge(k_lo, b + 2)
                sp.dma_start(scr.xk[b], xk[:].bitcast(F32)).then_inc(xk_st, 16)
                sp.wait_ge(xd_ok, b + 1)
                for two in range(2):
                    sp.dma_start(bc_v[b, two], xdbl[R + two * N:R + (two + 1) * N, :]).then_inc(bc_st, 16)
                sp.wait_ge(dtu_ok, b + 2)
                sp.wait_ge(y0_ok, b * 4 + 4)
                sp.dma_start(scr.mam[b], mam[:]).then_inc(mam_st, 16)

            for b in range(B - 1):
                weights(b)
                sp.wait_ge(xn_ok, b * 4 + 4)
                sp.dma_start(x_nat[:], x[b + 1].rearrange("(s p) f -> p s f", p=P)).then_inc(x_in, 16)
                sp.wait_ge(c_ps, b * 2 + 2)
                sp.dma_start(c_nat[:], ctx_in[b + 1].rearrange("(s p) f -> p s f", p=P)).then_inc(c_in, 16)
                stores(b)
            weights(B - 1)
            stores(B - 1)
            sp.wait_ge(wq_st, 32 * B + 32)
            sp.wait_ge(wo_st, 16 * B + 16)
            sp.wait_ge(mam_st, 16 * B + 16)
            sp.wait_ge(xk_st, 16 * B + 16)
            sp.wait_ge(v_st, 16 * B + 16)
            sp.wait_ge(bc_st, 32 * B + 32)

        @block.gpsimd
        def _(pool):
            pool.sem_inc(cor_ok, 1)
            pool.sem_inc(dt_ok, 1)
            pool.sem_inc(dtu_ok, 1)
            pool.memset(ident[:], 0.0).then_inc(ident0, 1)
            pool.memset(x_pad[:, :, 0:3], 0.0).then_inc(zpad, 1)
            pool.wait_ge(ident0, 1)
            pool.affine_select(out=ident[:], in_=ident[:], compare_op=ALU.not_equal, fill=1.0, base=0,
                               pattern=[[-1, P]], channel_multiplier=1).then_inc(ident1, 1)
            with pool.Fori(0, B) as b:
                pool.wait_ge(wq_h, b + 1)
                pool.tensor_tensor(wq_lo[:], wq_in[:], wq_hi[:].bitcast(F32), ALU.subtract).then_inc(wq_l, 1)
                pool.wait_ge(wo_h, b + 1)
                pool.tensor_tensor(wo_sp[:, :, LO], wo_in[:], wo_sp[:, :, HI].bitcast(F32), ALU.subtract).then_inc(wo_l, 1)
                pool.wait_ge(lmin, b + 1)
                pool.tensor_tensor(ew[:], ea[:], ew[:], ALU.subtract).then_inc(cor_ok, 1)
                pool.wait_ge(r_ok, b + 2)
                pool.wait_ge(cor_ok, b + 2)
                pool.wait_ge(mam_st, b * 16 + 16)
                pool.tensor_tensor(mam[:, DT], vraw[:], ew[:], ALU.add).then_inc(dt_ok, 1)
                pool.wait_ge(dt_ok, b + 2)
                pool.wait_ge(u_ok, b * 4 + 4 + 4)
                pool.tensor_tensor(mam[:, DTU], mam[:, DT], u[:], ALU.mult).then_inc(dtu_ok, 1)

        @block.scalar
        def _(act):
            act.sem_inc(ct_ok, 1)
            act.sem_inc(xpad_ok, 2)
            act.sem_inc(u_ok, 4)
            act.sem_inc(v_sb, 1)
            act.wait_ge(w_tp, 1)
            act.copy(wi_t[:, 0], tpx[0][:]).then_inc(w_sb, 1)
            act.wait_ge(w_tp, 2)
            act.copy(wi_t[:, 1], tpx[1][:]).then_inc(w_sb, 1)
            act.wait_ge(w_tp, 3)
            act.copy(xp_t[:], cps[:, 0:KT * (R + 2 * N)]).then_inc(w_sb, 1)
            act.wait_ge(w_tp, 4)
            act.copy(dp_t[:], kps[0:R, :]).then_inc(w_sb, 1)
            act.wait_ge(w_in, 160)
            act.activation(alog[:], alog[:], ACT.Exp).then_inc(a_ok, 1)
            with act.Fori(0, B) as b:
                act.wait_ge(wo_ld, b * 16 + 16)
                act.wait_ge(wo_st, b * 16 + 16)
                act.copy(wo_sp[:, :, HI], wo_in[:]).then_inc(wo_h, 1)
                act.wait_ge(var_ok, b + 1)
                act.activation(sc[:, 1], sc[:, 0], ACT.Sqrt).then_inc(std_ok, 1)
                for k in range(KT):
                    if k == 0:
                        act.wait_ge(xk_st, b * 16 + 16)
                    act.wait_ge(tpx_ps, b * 4 + k + 1 + 4)
                    act.copy(xk[:, k], tpx[k % 2][:]).then_inc(xk_hi, 1)
                for k in range(CT):
                    act.wait_ge(c_ps, b * 2 + k + 1)
                    act.copy(c_t[:, k], cps[:]).then_inc(ct_ok, 1)
                for e in range(KT):
                    act.wait_ge(x_ps, b * 4 + e + 1)
                    act.wait_ge(conv, b * 16 + 13 + e)
                    act.copy(x_pad[:, e, 3:3 + T], xps[e % 2][:]).then_inc(xpad_ok, 1)
                act.wait_ge(k_ps, b + 1)
                act.copy(xk[:, XK_KHI], kps[:]).then_inc(k_hi, 1)
                act.wait_ge(v_ps, b * 2 + 1)
                act.copy(v_t[:], vps[:]).then_inc(v_sb, 1)
                act.wait_ge(v_ps, b * 2 + 2)
                act.wait_ge(v_st, b * 16 + 16)
                act.copy(v_nat[:], vps[:]).then_inc(v_sb, 1)
                for e in range(KT):
                    if e == 0:
                        act.wait_ge(m_ps, b * 5 + 1)
                        act.wait_ge(dtu_ok, b + 1)
                    act.wait_ge(conv, b * 16 + 12 + e + 1 + 16)
                    act.activation(u[:, e], acc[:, e], ACT.Silu).then_inc(u_ok, 1)
                act.wait_ge(m_ps, b * 5 + 1 + 5)
                act.wait_ge(bc_st, b * 32 + 32)
                act.copy(xdbl[:], mps[0:R + 2 * N, :]).then_inc(xd_ok, 1)
                act.wait_ge(av, b + 1)
                act.activation(ea[:], ea[:], ACT.Exp).then_inc(e_ok, 1)
                act.wait_ge(e_ok, b + 1)
                act.wait_ge(r_ok, b + 1)
                act.activation(el[:], ea[:], ACT.Ln, bias=1.0).then_inc(l_ok, 1)
                act.wait_ge(mam_st, b * 16 + 16)
                act.wait_ge(u_ok, b * 4 + 4 + 4)
                for e in range(KT):
                    act.activation(mam[:, Y0, e], u[:, e], ACT.Copy, scale=dsk[:, e:e + 1]).then_inc(y0_ok, 1)

        @block.vector
        def _(dve):
            dve.sem_inc(xk_lo, 2)
            dve.sem_inc(k_lo, 1)
            dve.sem_inc(conv, 16)
            dve.sem_inc(dv, 1)
            dve.sem_inc(r_ok, 1)
            dve.wait_ge(w_in, 160)
            dve.tensor_copy(wk_sp[:, HI], wraw[:, :, 0:HD]).then_inc(w_spl, 1)
            dve.tensor_copy(wv_sp[:, HI], wraw[:, :, HD:2 * HD]).then_inc(w_spl, 1)
            dve.wait_ge(w_spl, 2)
            dve.tensor_tensor(wk_sp[:, LO], wraw[:, :, 0:HD], wk_sp[:, HI].bitcast(F32), ALU.subtract).then_inc(w_spl, 1)
            dve.tensor_tensor(wv_sp[:, LO], wraw[:, :, HD:2 * HD], wv_sp[:, HI].bitcast(F32),
                              ALU.subtract).then_inc(w_spl, 1)
            dve.wait_ge(a_ok, 1)
            dve.tensor_scalar(g.a_neg[:].rearrange("p n k -> p k n"), alog[:], -1.0, None, ALU.mult).then_inc(a_ok, 1)
            dve.wait_ge(zpad, 1)
            with dve.Fori(0, B) as b:
                dve.wait_ge(wq_ld, b * 16 + 16)
                dve.wait_ge(wq_st, b * 32 + 32)
                dve.tensor_copy(wq_hi[:], wq_in[:]).then_inc(wq_h, 1)
                dve.wait_ge(x_in, b * 16 + 16)
                dve.wait_ge(tpx_ps, b * 4 + 4)
                n = layer_norm(dve, chain, 0, x_nat, xn, stats, mv, sc, var_ok, std_ok, b + 1,
                               lambda ins: ins.then_inc(xn_ok, 1))
                dve.wait_ge(chain, n)
                dve.wait_ge(xn_ok, b * 4 + 4)
                dve.sem_clear(chain)
                for k in range(KT):
                    dve.wait_ge(xk_hi, b * 4 + k + 1)
                    dve.tensor_tensor(xk[:, 4 + k], tpx[k % 2][:], xk[:, k].bitcast(F32), ALU.subtract).then_inc(xk_lo, 1)
                for j in range(4):
                    for e in range(KT):
                        if j == 0:
                            dve.wait_ge(xpad_ok, b * 4 + e + 1 + 2)
                            dve.wait_ge(u_ok, b * 4 + e + 1)
                            ins = dve.tensor_scalar(acc[:, e], x_pad[:, e, 3:3 + T], cw[:, e, 3:4], cb[:, e:e + 1],
                                                    ALU.mult, ALU.add)
                        else:
                            dve.wait_ge(conv, b * 16 + (j - 1) * 4 + e + 1 + 16)
                            ins = dve.scalar_tensor_tensor(acc[:, e], x_pad[:, e, 3 - j:3 - j + T],
                                                           cw[:, e, 3 - j:4 - j], acc[:, e], ALU.mult, ALU.add)
                        ins.then_inc(conv, 1)
                dve.wait_ge(k_hi, b + 1)
                dve.tensor_tensor(xk[:, XK_KLO], kps[:], xk[:, XK_KHI].bitcast(F32), ALU.subtract).then_inc(k_lo, 1)
                for e in range(KT):
                    dve.wait_ge(m_ps, b * 5 + e + 2 + 5)
                    dve.wait_ge(dt_ok, b + 1)
                    dve.tensor_scalar(vraw[:, e], mps[:], db[:, e:e + 1], None, ALU.add).then_inc(dv, 1)
                dve.wait_ge(dv, b * 4 + 4 + 1)
                dve.wait_ge(cor_ok, b + 1)
                dve.scalar_tensor_tensor(ea[:], vraw[:], -1.0, vraw[:], ALU.mult, ALU.min).then_inc(av, 1)
                dve.wait_ge(e_ok, b + 1)
                dve.tensor_scalar(ew[:], ea[:], 1.0, -1.0, ALU.add, ALU.add).then_inc(w_ok, 1)
                dve.wait_ge(l_ok, b + 1)
                dve.wait_ge(w_ok, b + 1)
                dve.tensor_tensor(el[:], el[:], ew[:], ALU.min).then_inc(lmin, 1)
                dve.wait_ge(lmin, b + 1)
                dve.scalar_tensor_tensor(vraw[:], vraw[:], 0.0, el[:], ALU.max, ALU.add).then_inc(r_ok, 1)

        @block.tensor
        def _(pe):
            pe.sem_inc(tpx_ps, 4)
            pe.sem_inc(m_ps, 5)
            pe.wait_ge(ident1, 1)
            pe.wait_ge(w_in, 160)
            for c in range(CT):
                for k in range(KT):
                    last = pe.transpose(tpx[c][:, k * P:k * P + P], wi_nat[:, k, c * P:c * P + P], ident[:])
                last.then_inc(w_tp, 1)
            for k in range(KT):
                w = R + 2 * N
                last = pe.transpose(cps[:, k * w:k * w + w], xp_nat[:, k * P:k * P + P], ident[0:w, 0:w])
            last.then_inc(w_tp, 1)
            for k in range(KT):
                last = pe.transpose(kps[0:R, k * P:k * P + P], dp_nat[:, k, :], ident[:])
            last.then_inc(w_tp, 1)
            pe.wait_ge(w_sb, 4)
            pe.wait_ge(w_spl, 4)
            with pe.Fori(0, B) as b:
                for k in range(KT):
                    if k == 0:
                        pe.wait_ge(xn_ok, b * 4 + 4)
                    pe.wait_ge(xk_lo, b * 4 + k + 1)
                    for s in range(ST):
                        last = pe.transpose(tpx[k % 2][:, s * P:s * P + P], xn[:, s, k * P:k * P + P], ident[:])
                    last.then_inc(tpx_ps, 1)
                for k in range(CT):
                    if k == 0:
                        pe.wait_ge(c_in, b * 16 + 16)
                    pe.wait_ge(ct_ok, b * 2 + k + 1)
                    for s in range(ST):
                        last = pe.transpose(cps[:, s * P:s * P + P], c_nat[:, s, k * P:k * P + P], ident[:])
                    last.then_inc(c_ps, 1)
                pe.wait_ge(ct_ok, b * 2 + 2 + 1)
                for e in range(KT):
                    pe.wait_ge(xpad_ok, b * 4 + e + 1)
                    for k in range(CT):
                        last = pe.matmul(xps[e % 2][:], wi_t[:, k, e * P:e * P + P], c_t[:, k], start=k == 0, stop=k == CT - 1)
                    last.then_inc(x_ps, 1)
                pe.wait_ge(xk_lo, b * 4 + 4 + 2)
                rhs = [(xk[:, k], xk[:, 4 + k]) for k in range(KT)]
                pe.wait_ge(k_lo, b + 1)
                split_matmuls(pe, kps[:], [(wk_sp[:, HI, k], wk_sp[:, LO, k]) for k in range(KT)], rhs).then_inc(k_ps, 1)
                pe.wait_ge(v_sb, b * 2 + 1)
                split_matmuls(pe, vps[:], [(wv_sp[:, HI, k], wv_sp[:, LO, k]) for k in range(KT)], rhs).then_inc(v_ps, 1)
                pe.wait_ge(v_sb, b * 2 + 2)
                for s in range(ST):
                    last = pe.transpose(vps[:, s * P:s * P + P], v_t[:, s * P:s * P + P], ident[:])
                last.then_inc(v_ps, 1)
                pe.wait_ge(u_ok, b * 4 + 4 + 4)
                pe.wait_ge(dv, b * 4 + 1)
                for e in range(KT):
                    last = pe.matmul(mps[0:R + 2 * N, :], xp_t[:, e], u[:, e], start=e == 0, stop=e == KT - 1)
                last.then_inc(m_ps, 1)
                pe.wait_ge(xd_ok, b + 1)
                for e in range(KT):
                    if e:
                        pe.wait_ge(dv, b * 4 + e + 1)
                    pe.matmul(mps[:], dp_t[:, e * P:e * P + P], xdbl[0:R, :], start=True, stop=True).then_inc(m_ps, 1)


def attention_and_scan(nc, dm, g, x, scr):
    B, KT, ST, N, H, HD = dm.B, dm.KT, dm.ST, dm.N, dm.H, dm.HD
    GH = 4
    STEPS = GH * ST
    TPB = H // GH
    TURNS = B * TPB
    NG = N // TPB
    PIECES = NG * KT
    SCALE = float(HD) ** -0.5
    DA, HB, ADD_LAG = 4, 8, 4
    T_LAG, V_LAG = 5, 6
    OUT0 = V_LAG
    PROJECT = {0: [(1, 0)], 1: [(1, 1)], 2: [(1, 2), (1, 3)], 5: [(2, 0), (2, 1)], 6: [(2, 2), (2, 3)],
               10: [(3, k) for k in range(KT)], 12: [(4, 0)], 13: [(4, 1)], 14: [(4, 2), (4, 3)]}
    Q_OUT = {3: 1, 7: 2, 11: 3, 15: 4}
    SCANS = [1, 1, 1, 0, 0, 1, 2, 2, 2, 2, 1, 0, 1, 1, 1, 0]
    FIRST_SCAN = [sum(SCANS[:i]) for i in range(STEPS + 1)]
    with ExitStack() as ctx:
        sb = lambda n, s, d=F32: ctx.enter_context(nc.sbuf_tensor(n, s, d))
        ps = lambda n: ctx.enter_context(nc.psum_tensor(n, [P, T], F32))
        ident = g.ident
        xk_s = sb("xk_s", [P, 2, XK_ROWS, T], F32R)
        wq_s = sb("wq_s", [P, GH, 2, KT, HD], F32R)
        wo_s = sb("wo_s", [P, GH, 2, dm.D], F32R)
        v_s = sb("v_s", [P, T])
        q_s = sb("q_s", [P, 2, 2, T], F32R)
        p_s = sb("p_s", [P, 2, ST, T])
        pt_s = sb("pt_s", [P, 2, T])
        o_s = sb("o_s", [P, GH, 2, T], F32R)
        xa = sb("xa", [P, ST, T])
        mam_s = sb("mam_s", [P, 3, KT, T])
        d_a = sb("d_a", [P, DA, T])
        hb = sb("hb", [P, HB, T])
        bcs = sb("bcs", [P, 2, 2, T])
        nmax = sb("nmax", [P, STEPS])
        rsum = sb("rsum", [P, STEPS])
        rinv = sb("rinv", [P, STEPS])
        qps, ops = ps("qps"), ps("ops")
        sps = [ps("sps0"), ps("sps1")]
        tps = [ps("tps0"), ps("tps1")]
        ups = [ps("ups0"), ps("ups1")]
        names = ("xk_in wo_in x_in q_ps q_hi q_lo s_ps smax p_exp rc p_nrm t_ps pt_sb pv o_hi o_lo out_ps acc "
                 "m_da m_dbu m_scan m_prod m_add x1_st").split()
        (xk_in, wo_in, x_in, q_ps, q_hi, q_lo, s_ps, smax, p_exp, rc, p_nrm, t_ps, pt_sb, pv, o_hi, o_lo,
         out_ps, acc, m_da, m_dbu, m_scan, m_prod, m_add, x1_st) = [
            ctx.enter_context(nc.semaphore("a_" + n)) for n in names]
        several = lambda n, m: [ctx.enter_context(nc.semaphore(f"a_{n}{j}")) for j in range(m)]
        wq_in, bc_in, v_in = several("wq_in", GH), several("bc_in", 2), several("v_in", ST)
        dt_in, y_in, y_st = several("dt_in", KT), several("y_in", KT), several("y_st", KT)
        block = ctx.enter_context(nc.Block())

        @block.sync
        def _(sp):
            def load_xk(b):
                sp.dma_start(xk_s[:, b % 2].bitcast(F32), scr.xk[b]).then_inc(xk_in, 16)

            def load_wq(G):
                sp.dma_start(wq_s[:, G % GH].bitcast(F32), scr.wq[G % H]).then_inc(wq_in[G % GH], 16)

            def load_wo(it):
                h0 = it % TPB * GH
                sp.dma_start(wo_s[:].bitcast(F32), scr.wo[h0:h0 + GH].rearrange("h p two f -> p h two f"))\
                    .then_inc(wo_in, 16)

            def load_bc(n):
                sp.dma_start(bcs[:, n % 2], scr.bc[n // N, n % N].rearrange("(o t) c -> o t c", o=1)
                             .to_broadcast([P, 2, T])).then_inc(bc_in[n % 2], 16)

            def load_dt(b, k):
                sp.dma_start(mam_s[:, DT:DTU + 1, k], scr.mam[b, :, DT:DTU + 1, k]).then_inc(dt_in[k], 16)

            def load_y(b, k):
                sp.dma_start(mam_s[:, Y0, k], scr.mam[b, :, Y0, k]).then_inc(y_in[k], 16)

            def store_y(b, k):
                sp.dma_start(scr.y[b, :, k], mam_s[:, Y0, k]).then_inc(y_st[k], 16)

            def load_v(b, t):
                sp.dma_start(v_s[:, t * P:t * P + P], scr.v[b, :, t * P:t * P + P]).then_inc(v_in[t], 16)

            load_wq(0)
            load_xk(0)
            load_bc(0)
            for k in range(KT):
                load_dt(0, k)
            load_wq(1)
            load_bc(1)
            for k in range(KT):
                load_y(0, k)
            for G in range(2, GH):
                load_wq(G)
            for t in range(ST):
                load_v(0, t)
            sp.wait_ge(q_ps, 1)
            load_wq(GH)
            load_wo(0)
            sp.dma_start(xa[:], x[0].rearrange("(s p) f -> p s f", p=P)).then_inc(x_in, 16)
            for it in range(TURNS):
                b = it // TPB
                new = it % TPB == 0
                for j in range(GH):
                    G = it * GH + j
                    if new and j == 0 and b:
                        for k in range(KT):
                            sp.wait_ge(m_scan, it * PIECES - KT + k + 1 + DA)
                            load_dt(b, k)
                        for k in range(KT):
                            sp.wait_ge(m_add, it * PIECES - KT + k + 1 + HB)
                            store_y(b - 1, k)
                        for k in range(KT):
                            sp.wait_ge(y_st[k], 16 * b)
                            load_y(b, k)
                    if 2 <= G + 1 < TURNS * NG:
                        sp.wait_ge(m_prod, G * KT)
                        load_bc(G + 1)
                    if G + 1 + GH < B * H:
                        sp.wait_ge(q_ps, G + 2)
                        load_wq(G + 1 + GH)
                    if new and j == 1:
                        if b:
                            for t in range(ST):
                                sp.wait_ge(pv, it * STEPS - ST + t + 1 + 2)
                                load_v(b, t)
                        if b + 1 < B:
                            if b:
                                sp.wait_ge(s_ps, it * STEPS + 8)
                                sp.wait_ge(xk_in, 16 * (b + 1))
                            load_xk(b + 1)
                    if j == 2 and it:
                        sp.wait_ge(out_ps, it * ST + 4)
                        load_wo(it)
                    if j == 3 and new and b:
                        sp.wait_ge(acc, it * ST + 2)
                        sp.dma_start(scr.x1[b - 1], xa[:]).then_inc(x1_st, 16)
                        sp.wait_ge(x1_st, 16 * b)
                        sp.dma_start(xa[:], x[b].rearrange("(s p) f -> p s f", p=P)).then_inc(x_in, 16)
            for k in range(KT):
                sp.wait_ge(m_add, TURNS * PIECES - KT + k + 1 + HB)
                store_y(B - 1, k)
            sp.wait_ge(acc, TURNS * ST + 2)
            sp.dma_start(scr.x1[B - 1], xa[:]).then_inc(x1_st, 16)
            sp.wait_ge(x1_st, 16 * B)
            for k in range(KT):
                sp.wait_ge(y_st[k], 16 * B)

        class Turn:

            def __init__(self, it, g4, g16, first=False, final=False, tail=False):
                self.it, self.g4, self.g16, self.first, self.final, self.tail = it, g4, g16, first, final, tail

            def has(self, i):
                return not (self.first and i < 0) and not (self.tail and i >= 0) and not (self.final and i >= STEPS)

        def turns(eng, body):
            body(Turn(0, 0, 0, first=True))
            with eng.Fori(1, TURNS - 1) as it:
                body(Turn(it, eng.snap(it * GH), eng.snap(it * STEPS)))
            body(Turn(TURNS - 1, (TURNS - 1) * GH, (TURNS - 1) * STEPS, final=True))
            body(Turn(TURNS, TURNS * GH, TURNS * STEPS, tail=True))

        @block.tensor
        def _(pe):
            pe.sem_inc(s_ps, 8)
            pe.sem_inc(t_ps, 8)
            pe.sem_inc(pv, 2)
            pe.sem_inc(out_ps, 4)

            def project(u, slot, j, k):
                if k == 0:
                    pe.wait_ge(wq_in[j % GH], (u.it + j // GH) * 16 + 16)
                    pe.wait_ge(q_lo, u.g4 + (j + 1))
                last = split_matmul(pe, qps[:], wq_s[:, j % GH, HI, k], wq_s[:, j % GH, LO, k], xk_s[:, slot, k],
                                    xk_s[:, slot, 4 + k], k == 0, k == KT - 1)
                if k == KT - 1:
                    last.then_inc(q_ps, 1)

            def scores(u, slot, i):
                j, s = divmod(i, ST)
                if s == 0:
                    pe.wait_ge(q_lo, u.g4 + (j + 2))
                pe.wait_ge(p_exp, u.g16 + (i + 1))
                c = slice(s * P, s * P + P)
                split_matmul(pe, sps[s % 2][:], q_s[:, j % 2, HI, c], q_s[:, j % 2, LO, c], xk_s[:, slot, XK_KHI],
                             xk_s[:, slot, XK_KLO], True, True).then_inc(s_ps, 1)

            def transpose(u, i):
                j, t = i // ST, i % ST
                if t == 0:
                    pe.wait_ge(p_nrm, u.g16 + (i + ST))
                pe.wait_ge(pt_sb, u.g16 + (i + 1))
                for s in range(ST):
                    last = pe.transpose(tps[t % 2][:, s * P:s * P + P], p_s[:, j % 2, s, t * P:t * P + P], ident[:])
                last.then_inc(t_ps, 1)

            def values(u, i):
                j, t = i // ST, i % ST
                if j % GH == 0:
                    pe.wait_ge(v_in[t], (u.it + j // GH) // TPB * 16 + 16)
                if t == 0:
                    pe.wait_ge(o_lo, u.g4 + (j + 1))
                pe.wait_ge(pt_sb, u.g16 + (i + 3))
                pe.matmul(ops[:], v_s[:, t * P:t * P + P], pt_s[:, t % 2], start=t == 0, stop=t == ST - 1)\
                    .then_inc(pv, 1)

            def output(u, s):
                if s == 0:
                    pe.wait_ge(o_lo, u.g4 + 1)
                    pe.wait_ge(wo_in, u.it * 16)
                pe.wait_ge(acc, u.g4 + (s - ST + 1))
                c = slice(s * P, s * P + P)
                split_matmuls(pe, ups[s % 2][:], [(o_s[:, h, HI, c], o_s[:, h, LO, c]) for h in range(GH)],
                              [(wo_s[:, h, HI], wo_s[:, h, LO]) for h in range(GH)]).then_inc(out_ps, 1)

            def body(u):
                if u.first:
                    pe.wait_ge(xk_in, 16)
                    for k in range(KT):
                        project(u, 0, 0, k)
                if not u.tail:
                    slot = u.it // TPB % 2
                    slot = slot if u.first or u.final else pe.snap(slot)
                    after = (u.it + 1) // TPB % 2
                    after = after if u.first or u.final else pe.snap(after)
                for i in range(STEPS):
                    if u.has(i):
                        scores(u, slot, i)
                    if u.has(i - T_LAG):
                        transpose(u, i - T_LAG)
                    for j, k in PROJECT.get(i, ()):
                        if u.has(j * ST) and not u.tail:
                            if j == GH and k == 0:
                                pe.wait_ge(xk_in, (u.it + 1) // TPB * 16 + 16)
                            project(u, after if j == GH else slot, j, k)
                    if u.has(i - V_LAG):
                        values(u, i - V_LAG)
                    if not u.first and OUT0 <= i < OUT0 + ST:
                        output(u, i - OUT0)

            turns(pe, body)

        @block.scalar
        def _(act):
            act.sem_inc(p_exp, 2)
            act.sem_inc(pt_sb, 2)

            def q_high(u, j):
                act.wait_ge(q_ps, u.g4 + (j + 1))
                act.wait_ge(s_ps, u.g16 + (j * ST + 4))
                act.activation(q_s[:, j % 2, HI], qps[:], ACT.Copy, scale=SCALE).then_inc(q_hi, 1)

            def exps(u, i):
                j, s = divmod(i, ST)
                if s == 0:
                    act.wait_ge(t_ps, u.g16 + (i + 4))
                act.wait_ge(smax, u.g16 + (i + 1))
                act.activation(p_s[:, j % 2, s], sps[s % 2][:], ACT.Exp, bias=nmax[:, i:i + 1],
                               accum_out=rsum[:, i:i + 1]).then_inc(p_exp, 1)

            def pt_out(u, i):
                act.wait_ge(t_ps, u.g16 + (i + 1 + 8))
                act.wait_ge(pv, u.g16 + (i + 1))
                act.copy(pt_s[:, i % 2], tps[i % 2][:]).then_inc(pt_sb, 1)

            def o_high(u, j):
                act.wait_ge(out_ps, u.g4 + j // GH * ST + 4)
                act.wait_ge(pv, u.g16 + (j * ST + ST + 2))
                act.copy(o_s[:, j % GH, HI], ops[:]).then_inc(o_hi, 1)

            def decay(u, k):
                if k < KT:
                    act.wait_ge(dt_in[k], u.it // TPB * 16 + 16)
                act.wait_ge(m_scan, u.g16 + (k + 1))
                n = u.it % TPB * NG + k // KT
                act.activation(d_a[:, k % DA], mam_s[:, DT, k % KT], ACT.Exp,
                               scale=g.a_neg[:, n, k % KT:k % KT + 1]).then_inc(m_da, 1)

            def body(u):
                if u.first:
                    q_high(u, 0)
                for i in range(STEPS):
                    if i in Q_OUT and not u.tail and u.has(Q_OUT[i] * ST):
                        q_high(u, Q_OUT[i])
                    if i % ST == V_LAG % ST and u.has(i - V_LAG - ST):
                        o_high(u, (i - V_LAG - ST) // ST)
                    if not u.tail:
                        for k in range(FIRST_SCAN[i], FIRST_SCAN[i + 1]):
                            decay(u, k)
                        exps(u, i)
                    if u.has(i - T_LAG):
                        pt_out(u, i - T_LAG)

            turns(act, body)

        @block.vector
        def _(dve):
            dve.sem_inc(q_lo, 1)
            dve.sem_inc(o_lo, 1)
            dve.sem_inc(acc, 2)
            dve.sem_inc(m_scan, DA)

            def q_low(u, j):
                dve.wait_ge(q_hi, u.g4 + (j + 1))
                dve.scalar_tensor_tensor(q_s[:, j % 2, LO], qps[:], SCALE, q_s[:, j % 2, HI].bitcast(F32),
                                         ALU.mult, ALU.subtract).then_inc(q_lo, 1)

            def row_max(u, i):
                dve.wait_ge(s_ps, u.g16 + (i + 1 + 8))
                dve.tensor_reduce(nmax[:, i:i + 1], sps[i % 2][:], axis=AX_X, op=ALU.max, negate=True).then_inc(smax, 1)

            def normalise(u, i):
                s = i % ST
                dve.wait_ge(p_exp, u.g16 + (i + 1 + 2))
                dve.reciprocal(rinv[:, i % STEPS:i % STEPS + 1], rsum[:, i % STEPS:i % STEPS + 1]).then_inc(rc, 1)
                dve.wait_ge(rc, u.g16 + (i + 1))
                dve.tensor_scalar(p_s[:, i // ST % 2, s], p_s[:, i // ST % 2, s], rinv[:, i % STEPS:i % STEPS + 1], None,
                                  ALU.mult).then_inc(p_nrm, 1)

            def o_low(u, j):
                dve.wait_ge(o_hi, u.g4 + (j + 1))
                dve.tensor_tensor(o_s[:, j % GH, LO], ops[:], o_s[:, j % GH, HI].bitcast(F32), ALU.subtract)\
                    .then_inc(o_lo, 1)

            def add_out(u, s):
                if s == 0:
                    dve.wait_ge(x_in, (u.it - 1) // TPB * 16 + 16)
                dve.wait_ge(out_ps, u.g4 + (s + 1))
                dve.wait_ge(acc, u.g4 + (s - ST + 2))
                dve.tensor_tensor(xa[:, s], ups[s % 2][:], xa[:, s], ALU.add).then_inc(acc, 1)

            def scan(u, k):
                dve.wait_ge(m_da, u.g16 + (k + 1))
                dve.wait_ge(m_dbu, u.g16 + (k + 1))
                dve.tensor_tensor_scan(hb[:, k % HB], d_a[:, k % DA], hb[:, k % HB], 0.0, ALU.mult, ALU.add)\
                    .then_inc(m_scan, 1)

            def times_c(u, k):
                dve.wait_ge(m_scan, u.g16 + (k + 1 + DA))
                dve.tensor_tensor(hb[:, k % HB], hb[:, k % HB], bcs[:, k // KT % 2, 1], ALU.mult).then_inc(m_prod, 1)

            def body(u):
                if u.first:
                    q_low(u, 0)
                if u.tail:
                    normalise(u, -1)
                    times_c(u, -1)
                for i in range(STEPS):
                    if i in Q_OUT and not u.tail and u.has(Q_OUT[i] * ST):
                        q_low(u, Q_OUT[i])
                    if not u.tail:
                        row_max(u, i)
                    if i % ST == V_LAG % ST and u.has(i - V_LAG - ST):
                        o_low(u, (i - V_LAG - ST) // ST)
                    if not u.tail:
                        if u.has(i - 1):
                            normalise(u, i - 1)
                        for k in range(FIRST_SCAN[i], FIRST_SCAN[i + 1]):
                            scan(u, k)
                            if u.has(k - 1):
                                times_c(u, k - 1)
                    if not u.first and OUT0 <= i < OUT0 + ST:
                        add_out(u, i - OUT0)

            turns(dve, body)

        @block.gpsimd
        def _(pool):
            pool.sem_inc(m_add, HB)

            def dbu(u, k):
                n = k // KT
                if k < KT:
                    pool.wait_ge(dt_in[k], u.it // TPB * 16 + 16)
                if k % KT == 0:
                    pool.wait_ge(bc_in[n % 2], u.it * (NG // 2 * 16) + (n // 2 + 1) * 16)
                pool.wait_ge(m_add, u.g16 + (k + 1))
                pool.tensor_tensor(hb[:, k % HB], mam_s[:, DTU, k % KT], bcs[:, n % 2, 0], ALU.mult).then_inc(m_dbu, 1)

            def add_y(u, k):
                if 0 <= k < KT:
                    pool.wait_ge(y_in[k], u.it // TPB * 16 + 16)
                pool.wait_ge(m_prod, u.g16 + (k + 1))
                pool.wait_ge(m_add, u.g16 + (k - KT + 1 + HB))
                y = mam_s[:, Y0, k % KT]
                pool.tensor_tensor(y, y, hb[:, k % HB], ALU.add).then_inc(m_add, 1)

            def body(u):
                for k in range(PIECES):
                    if u.has(k):
                        dbu(u, k)
                    if u.has(k - ADD_LAG):
                        add_y(u, k - ADD_LAG)

            turns(pool, body)


def transposed_weights(nc, dm, g, gate_w, fc1_w, fc2_w, up_w, down_w):
    KT, E, L, S = dm.KT, dm.E, dm.L, dm.S
    LT, SJ = L // P, S // P
    with ExitStack() as ctx:
        sb = lambda n, s, d=F32: ctx.enter_context(nc.sbuf_tensor(n, s, d))
        ident = g.ident
        up_n = sb("up_n", [P, SJ, dm.D])
        dn_n = sb("dn_n", [P, KT, S])
        f1_n = sb("f1_n", [P, LT, dm.D])
        f2_n = sb("f2_n", [P, KT, L])
        gt_n = sb("gt_n", [E, dm.D])
        wps = [ctx.enter_context(nc.psum_tensor(f"wps{i}", [P, T], F32)) for i in range(4)]
        gt_in, f1_in, f2_in, up_in, dn_in, w_ps, w_hi, w_lo = [
            ctx.enter_context(nc.semaphore("w_" + n)) for n in "gt_in f1_in f2_in up_in dn_in w_ps w_hi w_lo".split()]
        block = ctx.enter_context(nc.Block())
        items = [(gt_in, [gt_n[:, k * P:k * P + P] for k in range(KT)], g.gate_t[:, HI], g.gate_t[:, LO])]
        for i in range(LT):
            items.append((f1_in, [f1_n[:, i, k * P:k * P + P] for k in range(KT)],
                          g.fc1_t[:, HI, :, i * P:i * P + P], g.fc1_t[:, LO, :, i * P:i * P + P]))
            items.append((f2_in, [f2_n[:, k, i * P:i * P + P] for k in range(KT)], g.fc2_t[:, HI, i], g.fc2_t[:, LO, i]))
        for j in range(SJ):
            items.append((up_in, [up_n[:, j, k * P:k * P + P] for k in range(KT)],
                          g.up_t[:, HI, :, j * P:j * P + P], g.up_t[:, LO, :, j * P:j * P + P]))
        for j in range(SJ):
            items.append((dn_in, [dn_n[:, k, j * P:j * P + P] for k in range(KT)], g.dn_t[:, HI, j], g.dn_t[:, LO, j]))

        def shaped(bank, blocks, like):
            w = blocks[0].shape[0]
            ap = bank[:, 0:len(blocks) * w]
            return ap.rearrange("p (k c) -> p k c", c=w) if len(like.shape) == 3 else ap

        @block.sync
        def _(sp):
            sp.dma_start(gt_n[:], gate_w).then_inc(gt_in, 16)
            sp.dma_start(f1_n[:], fc1_w.rearrange("(j p) f -> p j f", p=P)).then_inc(f1_in, 16)
            sp.dma_start(f2_n[:], fc2_w.rearrange("(j p) f -> p j f", p=P)).then_inc(f2_in, 16)
            sp.dma_start(up_n[:], up_w.rearrange("(j p) f -> p j f", p=P)).then_inc(up_in, 16)
            sp.dma_start(dn_n[:], down_w.rearrange("(j p) f -> p j f", p=P)).then_inc(dn_in, 16)

        @block.tensor
        def _(pe):
            for n, (loaded, blocks, hi, lo) in enumerate(items):
                pe.wait_ge(loaded, 16)
                if n >= 4:
                    pe.wait_ge(w_lo, n - 3)
                for k, blk in enumerate(blocks):
                    w = blk.shape[0]
                    last = pe.transpose(wps[n % 4][:, k * w:k * w + w], blk, ident[0:w, 0:w])
                last.then_inc(w_ps, 1)

        @block.scalar
        def _(act):
            for n, (loaded, blocks, hi, lo) in enumerate(items):
                act.wait_ge(w_ps, n + 1)
                act.copy(hi, shaped(wps[n % 4], blocks, hi)).then_inc(w_hi, 1)

        @block.vector
        def _(dve):
            for n, (loaded, blocks, hi, lo) in enumerate(items):
                dve.wait_ge(w_hi, n + 1)
                dve.tensor_tensor(lo, shaped(wps[n % 4], blocks, hi), hi.bitcast(F32), ALU.subtract).then_inc(w_lo, 1)


def gate_route_shared(nc, dm, g, gate_bias, scr):
    B, KT, ST, E, L, S = dm.B, dm.KT, dm.ST, dm.E, dm.L, dm.S
    LT, SJ = L // P, S // P
    G, TOPG, TOPK, ROUTED = 4, 2, 8, 2.5
    OUT = -1e30
    TAKEN = -3e38
    with ExitStack() as ctx:
        sb = lambda n, s, d=F32: ctx.enter_context(nc.sbuf_tensor(n, s, d))
        ps = lambda n: ctx.enter_context(nc.psum_tensor(n, [P, T], F32))
        ident = g.ident
        x2 = sb("x2", [P, ST, T])
        y_t = sb("y_t", [P, KT, T])
        xn = sb("xn3", [P, ST, T])
        stats = sb("stats3", [P, ST, 6])
        mv = sb("mv3", [P, ST, 2])
        sc = sb("sc3", [P, 6, ST])
        xt = sb("xt", [P, 2, KT, T], F32R)
        s_t = sb("s_t", [P, 2, SJ, T], F32R)
        hr = sb("hr", [P, 2, T])
        bias = sb("bias", [P, E])
        lower = sb("lower", [P, G, G])
        score = sb("score", [P, ST, E])
        sbias = sb("sbias", [P, ST, E])
        top = sb("top", [P, ST, G, 8])
        gs = sb("gs", [P, ST, G])
        gt = sb("gt", [P, ST, G, G])
        eq = sb("eq", [P, ST, G, G])
        rank = sb("rank", [P, ST, G])
        cand = sb("cand", [P, ST, E])
        top8 = sb("top8", [P, ST, 8])
        repl = sb("repl", [P, ST, E])
        cw = sb("cw3", [P, ST, E])
        wsum = sb("wsum", [P, ST])
        winv = sb("winv", [P, ST])
        cw_t = sb("cw_t", [E, T])
        tp = [ps("tp0"), ps("tp1")]
        lg, ct = ps("lg"), ps("ct")
        up = [ps("up0"), ps("up1")]
        dn = [ps("dn0"), ps("dn1")]
        names = ("c_in x_in y_in z_ok var1 std1 sz_ok yt_ps g1 x2_ok var2 std2 xn_ok t_ps xt_hi xt_lo l_ps sc_ok cw_ok "
                 "cwt_ps cwt_sb cw_st f_ps f_hi f_lo u_ps r_ok h_ok h_hi h_lo d_ps d_ok part_st chain low0 low1").split()
        (c_in, x_in, y_in, z_ok, var1, std1, sz_ok, yt_ps, g1, x2_ok, var2, std2, xn_ok, t_ps, xt_hi, xt_lo, l_ps, sc_ok,
         cw_ok, cwt_ps, cwt_sb, cw_st, f_ps, f_hi, f_lo, u_ps, r_ok, h_ok, h_hi, h_lo, d_ps, d_ok, part_st, chain, low0,
         low1) = [ctx.enter_context(nc.semaphore("g_" + n)) for n in names]
        block = ctx.enter_context(nc.Block())

        @block.sync
        def _(sp):
            sp.sem_inc(part_st, 16)
            sp.sem_inc(cw_st, 16)
            sp.dma_start(bias[:], gate_bias.rearrange("(o e) -> o e", o=1).to_broadcast([P, E])).then_inc(c_in, 16)
            for b in range(B):
                if b:
                    sp.wait_ge(part_st, b * 16 + 16)
                sp.dma_start(x2[:], scr.x1[b]).then_inc(x_in, 16)
                if b:
                    sp.wait_ge(yt_ps, b * ST)
                sp.dma_start(y_t[:], scr.y[b]).then_inc(y_in, 16)
                sp.wait_ge(cwt_sb, b + 1)
                sp.dma_start(scr.cw.rearrange("e (b t) -> b e t", b=B)[b], cw_t[:]).then_inc(cw_st, 16)
                sp.wait_ge(d_ok, (b + 1) * ST + 2)
                sp.dma_start(scr.part[b], x2[:]).then_inc(part_st, 16)
            sp.wait_ge(part_st, B * 16 + 16)
            sp.wait_ge(cw_st, B * 16 + 16)

        @block.gpsimd
        def _(pool):
            pool.sem_inc(h_lo, 2)
            pool.memset(lower[:], 1.0).then_inc(low0, 1)
            pool.wait_ge(low0, 1)
            pool.affine_select(out=lower[:], in_=lower[:], compare_op=ALU.is_gt, fill=0.0, base=0,
                               pattern=[[1, G], [-1, G]], channel_multiplier=0).then_inc(low1, 1)
            with pool.Fori(0, B) as b:
                for j in range(SJ):
                    pool.wait_ge(h_hi, b * SJ + j + 1)
                    pool.tensor_tensor(s_t[:, LO, j], hr[:, j % 2], s_t[:, HI, j].bitcast(F32), ALU.subtract)\
                        .then_inc(h_lo, 1)

        @block.scalar
        def _(act):
            act.sem_inc(r_ok, 2)
            with act.Fori(0, B) as b:
                act.wait_ge(var1, b + 1)
                act.activation(sc[:, 1], sc[:, 0], ACT.Sqrt).then_inc(std1, 1)
                for s in range(ST):
                    act.wait_ge(z_ok, b * ST + s + 1)
                    act.activation(xn[:, s], xn[:, s], ACT.Silu).then_inc(sz_ok, 1)
                act.wait_ge(var2, b + 1)
                act.activation(sc[:, 1], sc[:, 0], ACT.Sqrt).then_inc(std2, 1)
                for k in range(KT):
                    act.wait_ge(t_ps, b * KT + k + 1)
                    if k == 0:
                        act.wait_ge(u_ps, b * SJ + 8)
                    act.copy(xt[:, HI, k], tp[k % 2][:]).then_inc(xt_hi, 1)
                act.wait_ge(l_ps, b + 1)
                act.activation(score[:], lg[:, 0:ST * E], ACT.Sigmoid).then_inc(sc_ok, 1)
                for i in range(LT):
                    act.wait_ge(f_ps, b * LT + i + 1)
                    act.copy(g.xl[:, HI, i, bass.ds(b * T, T)], dn[i % 2][:]).then_inc(f_hi, 1)
                def relu(j):
                    act.wait_ge(u_ps, b * SJ + j + 1 + 8)
                    act.wait_ge(h_lo, b * SJ + j + 1)
                    act.activation(hr[:, j % 2], up[j % 2][:], ACT.Relu).then_inc(r_ok, 1)

                def high(j):
                    if j == 0:
                        act.wait_ge(d_ps, b * ST + 4)
                    act.wait_ge(h_ok, b * SJ + j + 1)
                    act.copy(s_t[:, HI, j], hr[:, j % 2]).then_inc(h_hi, 1)

                for j in range(SJ):
                    relu(j)
                    if j:
                        high(j - 1)
                high(SJ - 1)
                act.wait_ge(cwt_ps, b + 1)
                act.wait_ge(cw_st, b * 16 + 16)
                act.copy(cw_t[:], ct[0:E, :]).then_inc(cwt_sb, 1)

        @block.vector
        def _(dve):
            dve.sem_inc(x2_ok, 2)
            dve.sem_inc(xt_lo, 2)
            dve.sem_inc(d_ok, 2)
            dve.sem_inc(f_lo, 2)
            dve.wait_ge(c_in, 16)
            dve.wait_ge(low1, 1)
            with dve.Fori(0, B) as b:
                dve.wait_ge(x_in, b * 16 + 16)
                n = layer_norm(dve, chain, 0, x2, xn, stats, mv, sc, var1, std1, b + 1, lambda i: i.then_inc(z_ok, 1))
                dve.wait_ge(chain, n)
                dve.wait_ge(y_in, b * 16 + 16)
                for s in range(ST):
                    dve.wait_ge(sz_ok, b * ST + s + 1)
                    dve.tensor_tensor(y_t[:, s], y_t[:, s], xn[:, s], ALU.mult).then_inc(g1, 1)
                for s in range(ST):
                    dve.wait_ge(yt_ps, b * ST + s + 1)
                    dve.tensor_tensor(x2[:, s], x2[:, s], tp[s % 2][:], ALU.add).then_inc(x2_ok, 1)
                dve.wait_ge(x2_ok, b * ST + ST + 2)
                n2 = layer_norm(dve, chain, n, x2, xn, stats, mv, sc, var2, std2, b + 1, lambda i: i.then_inc(xn_ok, 1))
                for k in range(KT):
                    dve.wait_ge(xt_hi, b * KT + k + 1)
                    dve.tensor_tensor(xt[:, LO, k], tp[k % 2][:], xt[:, HI, k].bitcast(F32), ALU.subtract).then_inc(xt_lo, 1)

                m = [n2]

                def step(ins, *waits):
                    m[0] += 1
                    ins.then_inc(chain, 1)

                def settled():
                    dve.wait_ge(chain, m[0])

                settled()
                dve.wait_ge(sc_ok, b + 1)
                step(dve.tensor_tensor(sbias[:], score[:], bias[:].unsqueeze(1).to_broadcast([P, ST, E]), ALU.add))
                settled()
                for s in range(ST):
                    for q in range(G):
                        step(dve.max(top[:, s, q], sbias[:, s, q * (E // G):(q + 1) * (E // G)]))
                settled()
                step(dve.tensor_tensor(gs[:], top[:, :, :, 0], top[:, :, :, 1], ALU.add))
                settled()
                for s in range(ST):
                    mine = gs[:, s].unsqueeze(2).to_broadcast([P, G, G])
                    other = gs[:, s].unsqueeze(1).to_broadcast([P, G, G])
                    step(dve.tensor_tensor(gt[:, s], other, mine, ALU.is_gt))
                    step(dve.tensor_tensor(eq[:, s], other, mine, ALU.is_equal))
                settled()
                for s in range(ST):
                    step(dve.tensor_tensor(eq[:, s], eq[:, s], lower[:], ALU.mult))
                settled()
                step(dve.tensor_tensor(gt[:], gt[:], eq[:], ALU.add))
                settled()
                step(dve.tensor_reduce(rank[:], gt[:], axis=AX_X, op=ALU.add))
                settled()
                step(dve.tensor_scalar(rank[:], rank[:], TOPG - 0.5, OUT, ALU.is_gt, ALU.mult))
                settled()
                for s in range(ST):
                    step(dve.tensor_tensor(cand[:, s].rearrange("p (g e) -> p g e", g=G),
                                           sbias[:, s].rearrange("p (g e) -> p g e", g=G),
                                           rank[:, s].unsqueeze(2).to_broadcast([P, G, E // G]), ALU.add))
                settled()
                for s in range(ST):
                    step(dve.max(top8[:, s], cand[:, s]))
                settled()
                for s in range(ST):
                    step(dve.match_replace(repl[:, s], top8[:, s], cand[:, s], TAKEN))
                settled()
                step(dve.scalar_tensor_tensor(cw[:], repl[:], TAKEN, score[:], ALU.is_equal, ALU.mult))
                settled()
                step(dve.tensor_reduce(wsum[:], cw[:], axis=AX_X, op=ALU.add))
                settled()
                step(dve.reciprocal(winv[:], wsum[:]))
                settled()
                for s in range(ST):
                    step(dve.tensor_scalar(cw[:, s], cw[:, s], winv[:, s:s + 1], ROUTED, ALU.mult, ALU.mult))
                settled()
                dve.sem_clear(chain)
                dve.sem_inc(cw_ok, 1)

                for i in range(LT):
                    dve.wait_ge(f_hi, b * LT + i + 1)
                    dve.tensor_tensor(g.xl[:, LO, i, bass.ds(b * T, T)], dn[i % 2][:],
                                      g.xl[:, HI, i, bass.ds(b * T, T)].bitcast(F32), ALU.subtract).then_inc(f_lo, 1)
                for j in range(SJ):
                    dve.wait_ge(r_ok, b * SJ + j + 1 + 2)
                    dve.tensor_tensor(hr[:, j % 2], hr[:, j % 2], hr[:, j % 2], ALU.mult).then_inc(h_ok, 1)
                for s in range(ST):
                    dve.wait_ge(d_ps, b * ST + s + 1 + 4)
                    dve.tensor_tensor(x2[:, s], x2[:, s], dn[s % 2][:], ALU.add).then_inc(d_ok, 1)

        @block.tensor
        def _(pe):
            pe.sem_inc(u_ps, 8)
            pe.sem_inc(d_ps, 4)
            with pe.Fori(0, B) as b:
                for s in range(ST):
                    if s == 0:
                        pe.wait_ge(g1, b * ST + ST)
                        pe.wait_ge(xt_lo, b * KT + 2)
                    pe.wait_ge(x2_ok, b * ST + s + 1)
                    for k in range(KT):
                        last = pe.transpose(tp[s % 2][:, k * P:k * P + P], y_t[:, k, s * P:s * P + P], ident[:])
                    last.then_inc(yt_ps, 1)
                for k in range(KT):
                    if k == 0:
                        pe.wait_ge(xn_ok, b * ST + ST)
                    pe.wait_ge(xt_lo, b * KT + k + 1)
                    for s in range(ST):
                        last = pe.transpose(tp[k % 2][:, s * P:s * P + P], xn[:, s, k * P:k * P + P], ident[:])
                    last.then_inc(t_ps, 1)
                pe.wait_ge(xt_lo, b * KT + KT + 2)
                for s in range(ST):
                    c = slice(s * P, s * P + P)
                    last = split_matmuls(pe, lg[:, s * E:s * E + E], [(xt[:, HI, k, c], xt[:, LO, k, c]) for k in range(KT)],
                                         [(g.gate_t[:, HI, k * E:k * E + E], g.gate_t[:, LO, k * E:k * E + E])
                                          for k in range(KT)])
                last.then_inc(l_ps, 1)
                x_t = [(xt[:, HI, k], xt[:, LO, k]) for k in range(KT)]
                for i in range(LT):
                    pe.wait_ge(d_ok, b * ST + 2)
                    c = slice(i * P, i * P + P)
                    split_matmuls(pe, dn[i % 2][:], [(g.fc1_t[:, HI, k, c], g.fc1_t[:, LO, k, c]) for k in range(KT)],
                                  x_t).then_inc(f_ps, 1)
                for j in range(SJ):
                    pe.wait_ge(r_ok, b * SJ + j + 1)
                    c = slice(j * P, j * P + P)
                    split_matmuls(pe, up[j % 2][:], [(g.up_t[:, HI, k, c], g.up_t[:, LO, k, c]) for k in range(KT)],
                                  x_t).then_inc(u_ps, 1)
                pe.wait_ge(cw_ok, b + 1)
                for s in range(ST):
                    last = pe.transpose(ct[0:E, s * P:s * P + P], cw[:, s], ident[:])
                last.then_inc(cwt_ps, 1)
                pe.wait_ge(h_lo, b * SJ + SJ + 2)
                pe.wait_ge(f_lo, b * LT + LT + 2)
                for s in range(ST):
                    pe.wait_ge(d_ok, b * ST + s + 1)
                    c = slice(s * P, s * P + P)
                    split_matmuls(pe, dn[s % 2][:], [(s_t[:, HI, j, c], s_t[:, LO, j, c]) for j in range(SJ)],
                                  [(g.dn_t[:, HI, j], g.dn_t[:, LO, j]) for j in range(SJ)]).then_inc(d_ps, 1)


def routed_experts(nc, dm, g, w1, w2, scr):
    E, I, L, B = dm.E, dm.I, dm.L, dm.B
    IT, LT = I // P, L // P
    HALVES = 2
    HTOK = B * T // HALVES
    TC = HTOK // T
    TILES = TC * IT
    with ExitStack() as ctx:
        sb = lambda n, s, d=F32: ctx.enter_context(nc.sbuf_tensor(n, s, d))
        ps = lambda n: ctx.enter_context(nc.psum_tensor(n, [P, T], F32))
        ident = g.ident
        w_nat = sb("w_nat", [P, 2, 2, IT * L])
        w_s = sb("w_s", [P, 2, 2, 2, T], F32R)
        cwb = sb("cwb", [P, 2, HTOK])
        rt = sb("rt", [P, 2, T])
        rc = sb("rc", [P, 2, T])
        hf = sb("hf", [P, TILES, T])
        h_s = sb("h_s", [P, TILES, 2, T], F32R)
        yps = [[ps(f"y{l}{c}") for c in range(TC)] for l in range(LT)]
        zps = [ps("z0"), ps("z1")]
        wps = [ps("wt0"), ps("wt1")]
        names = "wt_ps w_hi w_lo z_ps r_ok c_ok h_ok hh_ok hl_ok y_ps ye_hi ye_lo".split()
        (wt_ps, w_hi, w_lo, z_ps, r_ok, c_ok, h_ok, hh_ok, hl_ok, y_ps, ye_hi, ye_lo) = [
            ctx.enter_context(nc.semaphore("e_" + n)) for n in names]
        w_in = [ctx.enter_context(nc.semaphore(f"e_w_in{q}")) for q in range(2)]
        cw_in = [ctx.enter_context(nc.semaphore(f"e_cw_in{q}")) for q in range(2)]
        block = ctx.enter_context(nc.Block())

        @block.sync
        def _(sp):
            for X in range(HALVES * E):
                q, e, half = X % 2, X % E, X // E
                if X >= 2:
                    sp.wait_ge(wt_ps, 2 * (X - 2) + 2)
                for m, w in ((0, w1), (1, w2)):
                    sp.dma_start(w_nat[:, q, m], w[e].rearrange("(a p) c -> p a c", p=P)).then_inc(w_in[q], 16)
                if X >= 2:
                    sp.wait_ge(c_ok, TILES * (X - 2) + TILES)
                sp.dma_start(cwb[:, q], scr.cw[e:e + 1, half * HTOK:(half + 1) * HTOK].to_broadcast([P, HTOK]))\
                    .then_inc(cw_in[q], 16)

        def halves(eng, expert, finish):
            for half in range(HALVES):
                X0 = half * E
                for q in range(2):
                    expert(X0 + q, q, half, 2 * (X0 + q), TILES * (X0 + q), half * (E // 2), q == 0)
                with eng.Fori(1, E // 2) as pair:
                    x2_, x4_ = eng.snap(pair * 4 + 2 * X0), eng.snap(pair * (2 * TILES) + TILES * X0)
                    for q in range(2):
                        expert(None, q, half, x2_ + 2 * q, x4_ + TILES * q, pair + half * (E // 2), False)
                finish(half, X0 + E)

        @block.tensor
        def _(pe):
            pe.sem_inc(y_ps, 8)

            def down(q, n2, n4, first, last):
                pe.wait_ge(w_lo, n2 + (2 + 2))
                for c in range(TC):
                    for i in range(IT):
                        n = c * IT + i
                        pe.wait_ge(hl_ok, n4 + (n + 1 + TILES))
                        for l in range(LT):
                            col = slice(i * L + l * P, i * L + l * P + P)
                            ins = split_matmul(pe, yps[l][c][:], w_s[:, q, 1, HI, col], w_s[:, q, 1, LO, col],
                                               h_s[:, n, HI], h_s[:, n, LO], first and i == 0, last and i == IT - 1)
                        ins.then_inc(y_ps, 1)

            def expert(X, q, half, n2, n4, pair, first):
                pe.wait_ge(w_in[q], pair * 32 + 32)
                for m in range(2):
                    pe.wait_ge(w_lo, n2 + (m + 1))
                    for a in range(2):
                        for c in range(2):
                            col = a * 2 * P + c * P
                            last = pe.transpose(wps[m][:, col:col + P],
                                                w_nat[:, q, m, c * 2 * P + a * P:c * 2 * P + a * P + P], ident[:])
                    last.then_inc(wt_ps, 1)
                if not first:
                    is_first = X is not None and X % E == 1
                    if is_first and half:
                        pe.wait_ge(ye_lo, half * LT * TC)
                    down(1 - q, n2 - 2, n4 - TILES, is_first, False)
                pe.wait_ge(w_lo, n2 + (1 + 2))
                for c in range(TC):
                    for i in range(IT):
                        n = c * IT + i
                        pe.wait_ge(r_ok, n4 + (n + 1))
                        tok = slice(half * HTOK + c * T, half * HTOK + c * T + T)
                        split_matmuls(pe, zps[n % 2][:],
                                      [(w_s[:, q, 0, HI, l * I + i * P:l * I + i * P + P],
                                        w_s[:, q, 0, LO, l * I + i * P:l * I + i * P + P]) for l in range(LT)],
                                      [(g.xl[:, HI, l, tok], g.xl[:, LO, l, tok]) for l in range(LT)]).then_inc(z_ps, 1)

            def finish(half, X):
                down(1, 2 * X - 2, TILES * X - TILES, False, True)

            halves(pe, expert, finish)

        @block.scalar
        def _(act):
            act.sem_inc(r_ok, 2)

            def expert(X, q, half, n2, n4, pair, first):
                for m in range(2):
                    act.wait_ge(wt_ps, n2 + (m + 1))
                    if m == 0:
                        act.wait_ge(y_ps, n4 + 4)
                    act.copy(w_s[:, q, m, HI], wps[m][:]).then_inc(w_hi, 1)
                for n in range(TILES + 1):
                    if n < TILES:
                        act.wait_ge(z_ps, n4 + (n + 1))
                        act.wait_ge(h_ok, n4 + (n + 1))
                        act.activation(rt[:, n % 2], zps[n % 2][:], ACT.Relu).then_inc(r_ok, 1)
                    if n:
                        act.wait_ge(h_ok, n4 + (n + 2))
                        act.wait_ge(y_ps, n4 + (n - 1 + 5))
                        act.copy(h_s[:, n - 1, HI], hf[:, n - 1]).then_inc(hh_ok, 1)

            def finish(half, X):
                for l in range(LT):
                    for c in range(TC):
                        act.wait_ge(y_ps, TILES * X + 8)
                        tok = slice(half * HTOK + c * T, half * HTOK + c * T + T)
                        act.copy(g.yl[:, HI, l, tok], yps[l][c][:]).then_inc(ye_hi, 1)

            halves(act, expert, finish)

        @block.gpsimd
        def _(pool):
            def expert(X, q, half, n2, n4, pair, first):
                pool.wait_ge(cw_in[q], pair * 16 + 16)
                for n in range(TILES):
                    c = n // IT
                    pool.wait_ge(r_ok, n4 + (n + 1 + 2))
                    pool.wait_ge(h_ok, n4 + (n + 1))
                    pool.tensor_tensor(rc[:, n % 2], rt[:, n % 2], cwb[:, q, c * T:c * T + T], ALU.mult).then_inc(c_ok, 1)

            halves(pool, expert, lambda half, X: None)

        @block.vector
        def _(dve):
            dve.sem_inc(w_lo, 2)
            dve.sem_inc(h_ok, 2)
            dve.sem_inc(hl_ok, TILES)

            def expert(X, q, half, n2, n4, pair, first):
                for m in range(2):
                    dve.wait_ge(w_hi, n2 + (m + 1))
                    dve.tensor_tensor(w_s[:, q, m, LO], wps[m][:], w_s[:, q, m, HI].bitcast(F32), ALU.subtract)\
                        .then_inc(w_lo, 1)
                for n in range(TILES + 1):
                    if n < TILES:
                        dve.wait_ge(c_ok, n4 + (n + 1))
                        dve.wait_ge(hl_ok, n4 + (n + 1))
                        dve.tensor_tensor(hf[:, n], rc[:, n % 2], rt[:, n % 2], ALU.mult).then_inc(h_ok, 1)
                    if n:
                        dve.wait_ge(hh_ok, n4 + n)
                        dve.tensor_tensor(h_s[:, n - 1, LO], hf[:, n - 1], h_s[:, n - 1, HI].bitcast(F32),
                                          ALU.subtract).then_inc(hl_ok, 1)

            def finish(half, X):
                for l in range(LT):
                    for c in range(TC):
                        dve.wait_ge(ye_hi, half * LT * TC + l * TC + c + 1)
                        tok = slice(half * HTOK + c * T, half * HTOK + c * T + T)
                        dve.tensor_tensor(g.yl[:, LO, l, tok], yps[l][c][:], g.yl[:, HI, l, tok].bitcast(F32),
                                          ALU.subtract).then_inc(ye_lo, 1)

            halves(dve, expert, finish)


def routed_output(nc, dm, g, scr, out):
    B, ST, LT = dm.B, dm.ST, dm.L // P
    with ExitStack() as ctx:
        part = ctx.enter_context(nc.sbuf_tensor("part", [P, B, ST, T], F32))
        ops = [ctx.enter_context(nc.psum_tensor(f"o{i}", [P, T], F32)) for i in range(4)]
        o_ps, o_ok, o_st = [ctx.enter_context(nc.semaphore("o_" + n)) for n in "ps ok st".split()]
        p_in = [ctx.enter_context(nc.semaphore(f"o_in{b}")) for b in range(B)]
        block = ctx.enter_context(nc.Block())

        @block.sync
        def _(sp):
            for b in range(B):
                sp.dma_start(part[:, b], scr.part[b]).then_inc(p_in[b], 16)
            for b in range(B):
                sp.wait_ge(o_ok, (b + 1) * ST)
                sp.dma_start(out[b].rearrange("(s p) f -> p s f", p=P), part[:, b]).then_inc(o_st, 16)
            sp.wait_ge(o_st, 16 * B)

        @block.tensor
        def _(pe):
            for n in range(B * ST):
                if n >= 4:
                    pe.wait_ge(o_ok, n - 3)
                c = slice(n * P, n * P + P)
                split_matmuls(pe, ops[n % 4][:], [(g.yl[:, HI, l, c], g.yl[:, LO, l, c]) for l in range(LT)],
                              [(g.fc2_t[:, HI, l], g.fc2_t[:, LO, l]) for l in range(LT)]).then_inc(o_ps, 1)

        @block.vector
        def _(dve):
            for n in range(B * ST):
                b, s = n // ST, n % ST
                if s == 0:
                    dve.wait_ge(p_in[b], 16)
                dve.wait_ge(o_ps, n + 1)
                dve.tensor_tensor(part[:, b, s], part[:, b, s], ops[n % 4][:], ALU.add).then_inc(o_ok, 1)


class Held:
    pass


class Scratch:
    pass


def program(nc, a, out):
    dm = Dims(a["x"], a["ctx_1024"], a["L0_attn_Wq"], a["L0_attn_Wk"], a["L0_xattn_in_proj_w"], a["L0_xattn_x_proj_w"],
              a["L0_xattn_dt_proj_w"], a["L0_xattn_A_log"], a["L0_ffn_w1"])
    dm.S = a["L0_ffn_shared_up_w"].shape[0]
    scr = Scratch()
    dram = lambda n, s, d=F32: nc.dram_tensor("s_" + n, s, d, kind="Internal").ap()
    scr.wq = dram("wq", [dm.H, P, 2, dm.KT, dm.HD])
    scr.wo = dram("wo", [dm.H, P, 2, dm.D])
    scr.xk = dram("xk", [dm.B, P, XK_ROWS, T])
    scr.v = dram("v", [dm.B, P, T])
    scr.mam = dram("mam", [dm.B, P, 3, dm.KT, T])
    scr.bc = dram("bc", [dm.B, dm.N, 2, T])
    scr.x1 = dram("x1", [dm.B, P, dm.ST, dm.D])
    scr.part = dram("part", [dm.B, P, dm.ST, dm.D])
    scr.cw = dram("cw", [dm.E, dm.B * T])
    scr.y = dram("y", [dm.B, P, dm.KT, T])
    with ExitStack() as ctx:
        g = Held()
        g.ident = ctx.enter_context(nc.sbuf_tensor("ident", [P, P], F32))
        g.a_neg = ctx.enter_context(nc.sbuf_tensor("a_neg", [P, dm.N, dm.KT], F32))
        prepare(nc, dm, g, a["x"], a["ctx_1024"], a["L0_attn_Wq"], a["L0_attn_Wk"], a["L0_attn_Wv"],
                a["L0_attn_Wo"],
                a["L0_xattn_in_proj_w"], a["L0_xattn_conv_w"], a["L0_xattn_conv_b"], a["L0_xattn_x_proj_w"],
                a["L0_xattn_dt_proj_w"], a["L0_xattn_dt_proj_b"], a["L0_xattn_A_log"], a["L0_xattn_D"], scr)
        attention_and_scan(nc, dm, g, a["x"], scr)
        held = lambda n, s: ctx.enter_context(nc.sbuf_tensor(n, s, F32R))
        g.fc2_t = held("fc2_t", [P, 2, dm.L // P, dm.D])
        g.xl = held("xl", [P, 2, dm.L // P, dm.B * T])
        with ExitStack() as shared:
            held = lambda n, s: shared.enter_context(nc.sbuf_tensor(n, s, F32R))
            g.gate_t = held("gate_t", [P, 2, dm.KT * dm.E])
            g.fc1_t = held("fc1_t", [P, 2, dm.KT, dm.L])
            g.up_t = held("up_t", [P, 2, dm.KT, dm.S])
            g.dn_t = held("dn_t", [P, 2, dm.S // P, dm.D])
            transposed_weights(nc, dm, g, a["L0_ffn_gate_w"], a["L0_ffn_fc1_w"], a["L0_ffn_fc2_w"],
                               a["L0_ffn_shared_up_w"], a["L0_ffn_shared_down_w"])
            gate_route_shared(nc, dm, g, a["L0_ffn_gate_bias"], scr)
        g.yl = ctx.enter_context(nc.sbuf_tensor("yl", [P, 2, dm.L // P, dm.B * T], F32R))
        routed_experts(nc, dm, g, a["L0_ffn_w1"], a["L0_ffn_w2"], scr)
        routed_output(nc, dm, g, scr, out)


_INS = ['x', 'ctx_1024', 'L0_attn_Wq', 'L0_attn_Wk', 'L0_attn_Wv', 'L0_attn_Wo', 'L0_xattn_in_proj_w',
        'L0_xattn_conv_w', 'L0_xattn_conv_b', 'L0_xattn_x_proj_w', 'L0_xattn_dt_proj_w', 'L0_xattn_dt_proj_b',
        'L0_xattn_A_log', 'L0_xattn_D', 'L0_ffn_gate_w', 'L0_ffn_gate_bias', 'L0_ffn_fc1_w', 'L0_ffn_fc2_w',
        'L0_ffn_w1', 'L0_ffn_w2', 'L0_ffn_shared_up_w', 'L0_ffn_shared_down_w']


def kernel(**inputs):
    import numpy as np
    import concourse.bacc as bacc
    from concourse.bass_utils import run_bass_kernel_spmd

    nc = bacc.Bacc("TRN2", target_bir_lowering=False, num_devices=1)
    arrays, a = {}, {}
    for name in _INS:
        arrays["in_" + name] = v = np.ascontiguousarray(inputs[name])
        a[name] = nc.dram_tensor("in_" + name, v.shape, mybir.dt.from_np(v.dtype), kind="ExternalInput").ap()
    out = nc.dram_tensor("out_0", inputs["x"].shape, F32, kind="ExternalOutput").ap()
    program(nc, a, out)
    r = run_bass_kernel_spmd(nc, [arrays], core_ids=[0])
    return r.results[0]["out_0"]
```

```python
from contextlib import ExitStack

import concourse.bass as bass
from concourse import mybir

F32 = mybir.dt.float32
F32R = mybir.dt.float32r
ACT = mybir.ActivationFunctionType
ALU = mybir.AluOpType
AX_X = mybir.AxisListType.X
P = 128
T = 512
HI, LO = 0, 1
XK_KHI, XK_KLO, XK_ROWS = 8, 9, 10
DT, DTU, Y0 = 0, 1, 2
EPS = 1e-5


class Dims:
    def __init__(self, x, ctx_in, wq, wk, in_proj, xproj, dtproj, a_log, w1):
        self.B, _, self.D = x.shape
        self.C = ctx_in.shape[2]
        self.HD = wk.shape[1]
        self.H = wq.shape[1] // self.HD
        self.KT = self.D // P
        self.CT = self.C // P
        self.ST = T // P
        self.R = dtproj.shape[1]
        self.N = a_log.shape[1]
        self.E, self.I, self.L = w1.shape


def split_matmul(pe, out, lhs_hi, lhs_lo, rhs_hi, rhs_lo, start, stop):
    pe.matmul(out, lhs_hi, rhs_hi, start=start, stop=False)
    pe.matmul(out, lhs_hi, rhs_lo, start=False, stop=False)
    return pe.matmul(out, lhs_lo, rhs_hi, start=False, stop=stop)


def split_matmuls(pe, out, lhs, rhs):
    n = len(lhs)
    for k in range(n):
        last = split_matmul(pe, out, *lhs[k], *rhs[k], k == 0, k == n - 1)
    return last


def free_semaphores(nc, sems):
    nc.clear_and_free_semaphores(sems)
    nc.all_engine_barrier()


def layer_norm(dve, chain, n0, src, dst, stats, mv, sc, var_ok, std_ok, std_count, done):
    tiles = src.shape[1]
    for s in range(tiles):
        dve.bn_stats(stats[:, s], src[:, s]).then_inc(chain, 1)
    for s in range(tiles):
        dve.wait_ge(chain, n0 + s + 1)
        dve.bn_aggr(mv[:, s], stats[:, s]).then_inc(chain, 1)
    n = n0 + 2 * tiles
    dve.wait_ge(chain, n)
    dve.tensor_scalar(sc[:, 0], mv[:, :, 1], EPS, None, ALU.add).then_inc(var_ok, 1)
    dve.wait_ge(std_ok, std_count)
    dve.reciprocal(sc[:, 2], sc[:, 1]).then_inc(chain, 1)
    dve.wait_ge(chain, n + 1)
    dve.tensor_tensor(sc[:, 3], sc[:, 0], sc[:, 2], ALU.mult).then_inc(chain, 1)
    dve.wait_ge(chain, n + 2)
    dve.tensor_tensor(sc[:, 4], sc[:, 1], sc[:, 3], ALU.add).then_inc(chain, 1)
    dve.wait_ge(chain, n + 3)
    dve.tensor_scalar(sc[:, 3], sc[:, 4], 0.5, None, ALU.mult).then_inc(chain, 1)
    dve.wait_ge(chain, n + 4)
    dve.reciprocal(sc[:, 5], sc[:, 3]).then_inc(chain, 1)
    dve.wait_ge(chain, n + 5)
    for s in range(tiles):
        done(dve.tensor_scalar(dst[:, s], src[:, s], mv[:, s, 0:1], sc[:, 5, s:s + 1], ALU.subtract, ALU.mult))
    return n + 5


def prepare(nc, dm, g, x, ctx_in, Wq, Wk, Wv, Wo, in_proj, conv_w, conv_b, xproj, dtproj, dt_b, a_log, d_skip, scr):
    B, KT, ST, CT, N, R, H, HD = dm.B, dm.KT, dm.ST, dm.CT, dm.N, dm.R, dm.H, dm.HD
    with ExitStack() as ctx:
        sb = lambda n, s, d=F32: ctx.enter_context(nc.sbuf_tensor(n, s, d))
        ps = lambda n: ctx.enter_context(nc.psum_tensor(n, [P, T], F32))
        ident = g.ident
        wk_sp = sb("wk_sp", [P, 2, KT, HD], F32R)
        wv_sp = sb("wv_sp", [P, 2, KT, HD], F32R)
        wi_t = sb("wi_t", [P, CT, dm.D])
        xp_nat = sb("xp_nat", [R + 2 * N, dm.D])
        xp_t = sb("xp_t", [P, KT, R + 2 * N])
        dp_nat = sb("dp_nat", [P, KT, R])
        dp_t = sb("dp_t", [R, dm.D])
        cw = sb("cw", [P, KT, 4])
        cb = sb("cb", [P, KT])
        db = sb("db", [P, KT])
        dsk = sb("dsk", [P, KT])
        alog = sb("alog", [P, KT, N])
        wq_in = sb("wq_in", [P, H * HD])
        wq_hi = sb("wq_hi", [P, H * HD], F32R)
        wq_lo = sb("wq_lo", [P, H * HD], F32R)
        wo_in = sb("wo_in", [P, H // B, dm.D])
        wo_sp = sb("wo_sp", [P, H // B, 2, dm.D], F32R)

        x_nat = sb("x_nat", [P, ST, T])
        xn = sb("xn", [P, ST, T])
        stats = sb("stats", [P, ST, 6])
        mv = sb("mv", [P, ST, 2])
        sc = sb("sc", [P, 6, ST])
        xk = sb("xk", [P, XK_ROWS, T], F32R)
        v_t = sb("v_t", [P, T])
        v_nat = sb("v_nat", [P, T])
        c_nat = sb("c_nat", [P, ST, dm.C])
        c_t = sb("c_t", [P, CT, T])
        x_pad = sb("x_pad", [P, KT, T + 4])
        acc = sb("acc", [P, KT, T])
        u = sb("u", [P, KT, T])
        u_kept = sb("u_kept", [P, KT, T])
        wraw, wi_nat = u_kept[:, :, 0:HD * 2], u_kept[:, :, T - dm.C:]
        xdbl = sb("xdbl", [R + 2 * N, T])
        vraw = sb("vraw", [P, KT, T])
        ea = sb("ea", [P, KT, T])
        el = sb("el", [P, KT, T])
        ew = sb("ew", [P, KT, T])
        mam = sb("mam", [P, 3, KT, T])

        tpx = [ps("tpx0"), ps("tpx1")]
        cps, kps, vps, mps = ps("cps"), ps("kps"), ps("vps"), ps("mps")
        xps = [ps("xps0"), ps("xps1")]
        dps = [mps, cps]

        names = ("w_in wq_ld wq_h wq_l wq_st ident0 ident1 w_tp w_sb w_spl zpad a_ok x_in c_in xn_ok var_ok "
                 "std_ok tpx_ps xk_hi xk_lo k_ps k_hi k_lo v_ps v_sb c_ps ct_ok x_ps xpad_ok conv u_ok m_ps "
                 "xd_ok dv av e_ok l_ok w_ok r_ok cor_ok dt_ok dtu_ok y0_ok chain xk_st v_st mam_st bc_st lmin wo_ld wo_h wo_l wo_st kt_st kept").split()
        (w_in, wq_ld, wq_h, wq_l, wq_st, ident0, ident1, w_tp, w_sb, w_spl, zpad, a_ok, x_in, c_in, xn_ok, var_ok,
         std_ok, tpx_ps, xk_hi, xk_lo, k_ps, k_hi, k_lo, v_ps, v_sb, c_ps, ct_ok, x_ps, xpad_ok, conv, u_ok, m_ps,
         xd_ok, dv, av, e_ok, l_ok, w_ok, r_ok, cor_ok, dt_ok, dtu_ok, y0_ok, chain, xk_st, v_st, mam_st,
         bc_st, lmin, wo_ld, wo_h, wo_l, wo_st, kt_st, kept) = sems = [nc.alloc_semaphore("p_" + n) for n in names]
        ctx.callback(free_semaphores, nc, sems)
        block = ctx.enter_context(nc.Block())
        bc_v = scr.bc.rearrange("b n two t -> b two n t")
        wo_v = scr.wo.rearrange("(b h) p two f -> b p h two f", b=B)
        wq_v = scr.wq.rearrange("h p two k c -> k two p h c")

        @block.sync
        def _(sp):
            sp.sem_inc(xk_st, 16)
            sp.sem_inc(v_st, 16)
            sp.sem_inc(mam_st, 80)
            sp.sem_inc(bc_st, 32)
            sp.sem_inc(wq_st, 32)
            sp.dma_start(x_nat[:], x[0].rearrange("(s p) f -> p s f", p=P)).then_inc(x_in, 16)
            sp.dma_start(c_nat[:], ctx_in[0].rearrange("(s p) f -> p s f", p=P)).then_inc(c_in, 16)
            for dst, src in ((wi_nat[:], in_proj.rearrange("(k p) c -> p k c", p=P)), (xp_nat[:], xproj),
                             (dp_nat[:], dtproj.rearrange("(k p) r -> p k r", p=P)),
                             (wraw[:, :, 0:HD], Wk.rearrange("(k p) d -> p k d", p=P)),
                             (wraw[:, :, HD:2 * HD], Wv.rearrange("(k p) d -> p k d", p=P)),
                             (cw[:], conv_w.rearrange("(k p) o j -> p k (o j)", p=P)),
                             (cb[:], conv_b.rearrange("(k p) -> p k", p=P)),
                             (db[:], dt_b.rearrange("(k p) -> p k", p=P)),
                             (dsk[:], d_skip.rearrange("(k p) -> p k", p=P)),
                             (alog[:], a_log.rearrange("(k p) n -> p k n", p=P))):
                sp.dma_start(dst, src, allow_slow_non_contiguous=True).then_inc(w_in, 16)

            sp.sem_inc(wo_st, 16)
            sp.sem_inc(kt_st, 16)

            def weights(f):
                sp.wait_ge(wq_st, f * 32 + 32)
                sp.dma_start(wq_in[:], Wq.rearrange("(k p) n -> k p n", p=P)[f]).then_inc(wq_ld, 16)
                sp.wait_ge(wo_st, f * 16 + 16)
                sp.dma_start(wo_in[:], Wo.rearrange("(b h p) f -> b p h f", p=P, b=B)[f]).then_inc(wo_ld, 16)

            def body(g_, f):
                if f == 0:
                    weights(0)
                if f is not None and f + 1 < B:
                    sp.wait_ge(c_ps, f * 2 + 2)
                    sp.dma_start(c_nat[:], ctx_in[f + 1].rearrange("(s p) f -> p s f", p=P)).then_inc(c_in, 16)
                    sp.wait_ge(xn_ok, f * 4 + 4)
                    sp.dma_start(x_nat[:], x[f + 1].rearrange("(s p) f -> p s f", p=P)).then_inc(x_in, 16)
                if g_ is not None:
                    sp.wait_ge(xd_ok, g_ + 1)
                    for two in range(2):
                        sp.dma_start(bc_v[g_, two], xdbl[R + two * N:R + (two + 1) * N, :]).then_inc(bc_st, 16)
                if f is not None:
                    sp.wait_ge(wq_h, f + 1)
                    sp.dma_start(wq_v[f, HI], wq_hi[:].bitcast(F32).rearrange("p (h c) -> p h c", c=HD))\
                        .then_inc(wq_st, 16)
                    sp.wait_ge(wq_l, f + 1)
                    sp.dma_start(wq_v[f, LO], wq_lo[:].bitcast(F32).rearrange("p (h c) -> p h c", c=HD))\
                        .then_inc(wq_st, 16)
                    sp.wait_ge(wo_l, f + 1)
                    sp.dma_start(wo_v[f], wo_sp[:].bitcast(F32)).then_inc(wo_st, 16)
                    sp.wait_ge(xk_lo, f * 4 + 4 + 2)
                    sp.dma_start(scr.xk[f, :, 0:XK_KHI], xk[:, 0:XK_KHI].bitcast(F32)).then_inc(xk_st, 16)
                    if f + 1 < B:
                        weights(f + 1)
                    sp.wait_ge(v_sb, f * 2 + 3)
                    sp.dma_start(scr.v[f], v_nat[:]).then_inc(v_st, 16)
                    sp.wait_ge(k_lo, f + 2)
                    sp.dma_start(scr.xk[f, :, XK_KHI:XK_ROWS], xk[:, XK_KHI:XK_ROWS].bitcast(F32)).then_inc(kt_st, 16)
                if g_ is not None:
                    sp.wait_ge(y0_ok, g_ * 4 + 4 + 4)
                    sp.dma_start(scr.mam[g_, :, Y0], mam[:, Y0]).then_inc(mam_st, 16)
                    for e in range(KT):
                        sp.wait_ge(dtu_ok, g_ * 4 + e + 1 + 4)
                        sp.dma_start(scr.mam[g_, :, DT:DTU + 1, e], mam[:, DT:DTU + 1, e]).then_inc(mam_st, 16)

            for b in range(B + 1):
                body(b - 1 if b else None, b if b < B else None)
            sp.wait_ge(wq_st, 32 * B + 32)
            sp.wait_ge(wo_st, 16 * B + 16)
            sp.wait_ge(mam_st, 80 * B + 80)
            sp.wait_ge(xk_st, 16 * B + 16)
            sp.wait_ge(kt_st, 16 * B + 16)
            sp.wait_ge(v_st, 16 * B + 16)
            sp.wait_ge(bc_st, 32 * B + 32)

        def correct(eng, g_, e):
            eng.wait_ge(lmin, g_ * 4 + e + 1)
            eng.tensor_tensor(ew[:, e], ea[:, e], ew[:, e], ALU.subtract).then_inc(cor_ok, 1)

        def sum_dt(eng, g_, e):
            eng.wait_ge(r_ok, g_ * 4 + e + 1 + 4)
            eng.wait_ge(cor_ok, g_ * 4 + e + 1 + 4)
            eng.wait_ge(mam_st, g_ * 80 + 80)
            eng.tensor_tensor(mam[:, DT, e], vraw[:, e], ew[:, e], ALU.add).then_inc(dt_ok, 1)

        def batches(eng, body):
            body(None, 0)
            with eng.Fori(0, B - 1) as b:
                body(b, eng.snap(b + 1))
            body(B - 1, None)

        @block.gpsimd
        def _(pool):
            pool.sem_inc(cor_ok, 4)
            pool.sem_inc(dt_ok, 4)
            pool.sem_inc(dtu_ok, 4)
            pool.memset(ident[:], 0.0).then_inc(ident0, 1)
            pool.memset(x_pad[:, :, 0:3], 0.0).then_inc(zpad, 1)
            pool.wait_ge(ident0, 1)
            pool.affine_select(out=ident[:], in_=ident[:], compare_op=ALU.not_equal, fill=1.0, base=0,
                               pattern=[[-1, P]], channel_multiplier=1).then_inc(ident1, 1)

            def body(g_, f):
                if f is not None:
                    pool.wait_ge(wq_h, f + 1)
                    pool.tensor_tensor(wq_lo[:], wq_in[:], wq_hi[:].bitcast(F32), ALU.subtract).then_inc(wq_l, 1)
                    pool.wait_ge(wo_h, f + 1)
                    pool.tensor_tensor(wo_sp[:, :, LO], wo_in[:], wo_sp[:, :, HI].bitcast(F32), ALU.subtract)\
                        .then_inc(wo_l, 1)
                if g_ is not None:
                    for e in range(KT):
                        correct(pool, g_, e)
                        if f is not None:
                            sum_dt(pool, g_, e)
                            times_u(g_, e)
                    if f is None:
                        for e in range(KT):
                            times_u(g_, e)

            def times_u(g_, e):
                pool.wait_ge(dt_ok, g_ * 4 + e + 1 + 4)
                pool.wait_ge(kept, g_ * 4 + e + 1 + 4)
                pool.tensor_tensor(mam[:, DTU, e], mam[:, DT, e], u_kept[:, e], ALU.mult).then_inc(dtu_ok, 1)

            batches(pool, body)

        @block.scalar
        def _(act):
            act.sem_inc(ct_ok, 1)
            act.sem_inc(xpad_ok, 2)
            act.sem_inc(u_ok, 4)
            act.sem_inc(v_sb, 1)
            act.sem_inc(y0_ok, 4)
            act.wait_ge(w_tp, 1)
            act.copy(wi_t[:, 0], tpx[0][:]).then_inc(w_sb, 1)
            act.wait_ge(w_tp, 2)
            act.copy(wi_t[:, 1], tpx[1][:]).then_inc(w_sb, 1)
            act.wait_ge(w_tp, 3)
            act.copy(xp_t[:], cps[:, 0:KT * (R + 2 * N)]).then_inc(w_sb, 1)
            act.wait_ge(w_tp, 4)
            act.copy(dp_t[:], kps[0:R, :]).then_inc(w_sb, 1)
            act.wait_ge(w_in, 160)
            act.activation(alog[:], alog[:], ACT.Exp).then_inc(a_ok, 1)

            def body(g_, f):
                if f is not None:
                    for k in range(CT):
                        act.wait_ge(c_ps, f * 2 + k + 1)
                        act.copy(c_t[:, k], cps[:]).then_inc(ct_ok, 1)
                    act.wait_ge(var_ok, f + 1)
                    act.activation(sc[:, 1], sc[:, 0], ACT.Sqrt).then_inc(std_ok, 1)
                    for e in range(KT):
                        act.wait_ge(x_ps, f * 4 + e + 1)
                        act.wait_ge(conv, f * 16 + 13 + e)
                        act.copy(x_pad[:, e, 3:3 + T], xps[e % 2][:]).then_inc(xpad_ok, 1)
                if g_ is not None:
                    act.wait_ge(m_ps, g_ * 5 + 1 + 5)
                    act.wait_ge(bc_st, g_ * 32 + 32)
                    act.copy(xdbl[:], mps[0:R + 2 * N, :]).then_inc(xd_ok, 1)
                if f is not None:
                    act.wait_ge(wo_ld, f * 16 + 16)
                    act.wait_ge(wo_st, f * 16 + 16)
                    act.copy(wo_sp[:, :, HI], wo_in[:]).then_inc(wo_h, 1)
                    for k in range(KT):
                        if k == 0:
                            act.wait_ge(xk_st, f * 16 + 16)
                        act.wait_ge(tpx_ps, f * 4 + k + 1 + 4)
                        act.copy(xk[:, k], tpx[k % 2][:]).then_inc(xk_hi, 1)
                    for e in range(KT):
                        if e == 0:
                            act.wait_ge(m_ps, f * 5 + 1)
                        act.wait_ge(kept, f * 4 + e + 1)
                        act.wait_ge(conv, f * 16 + 12 + e + 1 + 16)
                        act.activation(u[:, e], acc[:, e], ACT.Silu).then_inc(u_ok, 1)
                if g_ is not None:
                    for e in range(KT):
                        act.wait_ge(av, g_ * 4 + e + 1)
                        act.activation(ea[:, e], ea[:, e], ACT.Exp).then_inc(e_ok, 1)
                    for e in range(KT):
                        act.wait_ge(e_ok, g_ * 4 + e + 1)
                        act.wait_ge(r_ok, g_ * 4 + e + 1)
                        act.activation(el[:, e], ea[:, e], ACT.Ln, bias=1.0).then_inc(l_ok, 1)
                if f is not None:
                    act.wait_ge(k_ps, f + 1)
                    act.wait_ge(kt_st, f * 16 + 16)
                    act.copy(xk[:, XK_KHI], kps[:]).then_inc(k_hi, 1)
                    act.wait_ge(v_ps, f * 2 + 1)
                    act.copy(v_t[:], vps[:]).then_inc(v_sb, 1)
                    act.wait_ge(v_ps, f * 2 + 2)
                    act.wait_ge(v_st, f * 16 + 16)
                    act.copy(v_nat[:], vps[:]).then_inc(v_sb, 1)
                if g_ is not None:
                    act.wait_ge(mam_st, g_ * 80 + 80)
                    for e in range(KT):
                        act.wait_ge(kept, g_ * 4 + e + 1 + 4)
                        act.activation(mam[:, Y0, e], u_kept[:, e], ACT.Copy, scale=dsk[:, e:e + 1]).then_inc(y0_ok, 1)

            batches(act, body)

        @block.vector
        def _(dve):
            dve.sem_inc(xk_lo, 2)
            dve.sem_inc(k_lo, 1)
            dve.sem_inc(conv, 16)
            dve.sem_inc(dv, 1)
            dve.sem_inc(r_ok, 4)
            dve.sem_inc(kept, 4)
            dve.wait_ge(w_in, 160)
            dve.tensor_copy(wk_sp[:, HI], wraw[:, :, 0:HD]).then_inc(w_spl, 1)
            dve.tensor_copy(wv_sp[:, HI], wraw[:, :, HD:2 * HD]).then_inc(w_spl, 1)
            dve.wait_ge(w_spl, 2)
            dve.tensor_tensor(wk_sp[:, LO], wraw[:, :, 0:HD], wk_sp[:, HI].bitcast(F32), ALU.subtract).then_inc(w_spl, 1)
            dve.tensor_tensor(wv_sp[:, LO], wraw[:, :, HD:2 * HD], wv_sp[:, HI].bitcast(F32),
                              ALU.subtract).then_inc(w_spl, 1)
            dve.wait_ge(a_ok, 1)
            dve.tensor_scalar(g.a_neg[:].rearrange("p n k -> p k n"), alog[:], -1.0, None, ALU.mult).then_inc(a_ok, 1)
            dve.wait_ge(zpad, 1)

            def convolve(f, j):
                for e in range(KT):
                    if j == 0:
                        dve.wait_ge(xpad_ok, f * 4 + e + 1 + 2)
                        dve.wait_ge(u_ok, f * 4 + e + 1)
                        ins = dve.tensor_scalar(acc[:, e], x_pad[:, e, 3:3 + T], cw[:, e, 3:4], cb[:, e:e + 1],
                                                ALU.mult, ALU.add)
                    else:
                        dve.wait_ge(conv, f * 16 + (j - 1) * 4 + e + 1 + 16)
                        ins = dve.scalar_tensor_tensor(acc[:, e], x_pad[:, e, 3 - j:3 - j + T],
                                                       cw[:, e, 3 - j:4 - j], acc[:, e], ALU.mult, ALU.add)
                    ins.then_inc(conv, 1)

            def x_low(f, k):
                dve.wait_ge(xk_hi, f * 4 + k + 1)
                dve.tensor_tensor(xk[:, 4 + k], tpx[k % 2][:], xk[:, k].bitcast(F32), ALU.subtract).then_inc(xk_lo, 1)

            def dt_raw(g_, e):
                dve.wait_ge(m_ps, g_ * 5 + e + 2 + 5)
                dve.wait_ge(dt_ok, g_ * 4 + e + 1)
                dve.tensor_scalar(vraw[:, e], dps[e % 2][:], db[:, e:e + 1], None, ALU.add).then_inc(dv, 1)

            def body(g_, f):
                if f is not None:
                    dve.wait_ge(x_in, f * 16 + 16)
                    dve.wait_ge(tpx_ps, f * 4 + 4)
                    n = layer_norm(dve, chain, 0, x_nat, xn, stats, mv, sc, var_ok, std_ok, f + 1,
                                   lambda ins: ins.then_inc(xn_ok, 1))
                    dve.wait_ge(chain, n)
                    dve.wait_ge(xn_ok, f * 4 + 4)
                    dve.sem_clear(chain)
                    dve.wait_ge(wq_ld, f * 16 + 16)
                    dve.wait_ge(wq_st, f * 32 + 32)
                    dve.tensor_copy(wq_hi[:], wq_in[:]).then_inc(wq_h, 1)
                    if g_ is not None:
                        for j in range(4):
                            convolve(f, j)
                if g_ is not None:
                    for e in range(KT):
                        dve.wait_ge(u_ok, g_ * 4 + e + 1 + 4)
                        dve.wait_ge(dtu_ok, g_ * 4 + e + 1)
                        dve.wait_ge(y0_ok, g_ * 4 + e + 1)
                        dve.tensor_copy(u_kept[:, e], u[:, e]).then_inc(kept, 1)
                for kind, k in (("dt", 0), ("dt", 1), ("x", 0), ("dt", 2), ("x", 1), ("dt", 3), ("x", 2), ("x", 3)):
                    if kind == "dt" and g_ is not None:
                        dt_raw(g_, k)
                    if kind == "x" and f is not None:
                        x_low(f, k)
                if f is not None and g_ is None:
                    for j in range(4):
                        convolve(f, j)
                if g_ is not None:
                    for e in range(KT):
                        dve.wait_ge(dv, g_ * 4 + e + 1 + 1)
                        dve.wait_ge(cor_ok, g_ * 4 + e + 1)
                        dve.scalar_tensor_tensor(ea[:, e], vraw[:, e], -1.0, vraw[:, e], ALU.mult, ALU.min)\
                            .then_inc(av, 1)
                    for e in range(KT):
                        dve.wait_ge(e_ok, g_ * 4 + e + 1)
                        dve.tensor_scalar(ew[:, e], ea[:, e], 1.0, -1.0, ALU.add, ALU.add).then_inc(w_ok, 1)
                    for e in range(KT):
                        dve.wait_ge(l_ok, g_ * 4 + e + 1)
                        dve.wait_ge(w_ok, g_ * 4 + e + 1)
                        dve.tensor_tensor(el[:, e], el[:, e], ew[:, e], ALU.min).then_inc(lmin, 1)
                    for e in range(KT):
                        dve.wait_ge(lmin, g_ * 4 + e + 1)
                        dve.scalar_tensor_tensor(vraw[:, e], vraw[:, e], 0.0, el[:, e], ALU.max, ALU.add).then_inc(r_ok, 1)
                        if f is None:
                            sum_dt(dve, g_, e)
                if f is not None:
                    dve.wait_ge(k_hi, f + 1)
                    dve.tensor_tensor(xk[:, XK_KLO], kps[:], xk[:, XK_KHI].bitcast(F32), ALU.subtract).then_inc(k_lo, 1)

            batches(dve, body)

        @block.tensor
        def _(pe):
            pe.sem_inc(tpx_ps, 4)
            pe.sem_inc(m_ps, 5)
            pe.wait_ge(ident1, 1)
            pe.wait_ge(w_in, 160)
            for c in range(CT):
                for k in range(KT):
                    last = pe.transpose(tpx[c][:, k * P:k * P + P], wi_nat[:, k, c * P:c * P + P], ident[:])
                last.then_inc(w_tp, 1)
            for k in range(KT):
                w = R + 2 * N
                last = pe.transpose(cps[:, k * w:k * w + w], xp_nat[:, k * P:k * P + P], ident[0:w, 0:w])
            last.then_inc(w_tp, 1)
            for k in range(KT):
                last = pe.transpose(kps[0:R, k * P:k * P + P], dp_nat[:, k, :], ident[:])
            last.then_inc(w_tp, 1)
            pe.wait_ge(w_sb, 4)
            pe.wait_ge(w_spl, 4)

            def x_transpose(f, k):
                if k == 0:
                    pe.wait_ge(xn_ok, f * 4 + 4)
                pe.wait_ge(xk_lo, f * 4 + k + 1)
                for s in range(ST):
                    last = pe.transpose(tpx[k % 2][:, s * P:s * P + P], xn[:, s, k * P:k * P + P], ident[:])
                last.then_inc(tpx_ps, 1)

            def dt_project(g_, e):
                if e >= 2:
                    pe.wait_ge(dv, g_ * 4 + e)
                pe.matmul(dps[e % 2][:], dp_t[:, e * P:e * P + P], xdbl[0:R, :], start=True, stop=True).then_inc(m_ps, 1)

            def context(g_, f):
                for k in range(CT):
                    if k == 0:
                        if g_ is not None:
                            pe.wait_ge(dv, g_ * 4 + 1)
                        pe.wait_ge(c_in, f * 16 + 16)
                    pe.wait_ge(ct_ok, f * 2 + k + 1)
                    for s in range(ST):
                        last = pe.transpose(cps[:, s * P:s * P + P], c_nat[:, s, k * P:k * P + P], ident[:])
                    last.then_inc(c_ps, 1)
                pe.wait_ge(ct_ok, f * 2 + 2 + 1)
                for e in range(KT):
                    pe.wait_ge(xpad_ok, f * 4 + e + 1)
                    for k in range(CT):
                        last = pe.matmul(xps[e % 2][:], wi_t[:, k, e * P:e * P + P], c_t[:, k], start=k == 0, stop=k == CT - 1)
                    last.then_inc(x_ps, 1)
            def body(g_, f):
                if f is not None:
                    context(g_, f)
                if g_ is not None:
                    pe.wait_ge(u_ok, g_ * 4 + 4 + 4)
                    pe.wait_ge(dv, g_ * 4 + 1)
                    for e in range(KT):
                        last = pe.matmul(mps[0:R + 2 * N, :], xp_t[:, e], u[:, e], start=e == 0, stop=e == KT - 1)
                    last.then_inc(m_ps, 1)
                    pe.wait_ge(xd_ok, g_ + 1)
                for kind, k in (("dt", 0), ("dt", 1), ("x", 0), ("dt", 2), ("x", 1), ("dt", 3), ("x", 2), ("x", 3)):
                    if kind == "dt" and g_ is not None:
                        dt_project(g_, k)
                    if kind == "x" and f is not None:
                        x_transpose(f, k)
                if f is None:
                    return
                pe.wait_ge(xk_lo, f * 4 + 4 + 2)
                rhs = [(xk[:, k], xk[:, 4 + k]) for k in range(KT)]
                pe.wait_ge(k_lo, f + 1)
                split_matmuls(pe, kps[:], [(wk_sp[:, HI, k], wk_sp[:, LO, k]) for k in range(KT)], rhs).then_inc(k_ps, 1)
                pe.wait_ge(v_sb, f * 2 + 1)
                split_matmuls(pe, vps[:], [(wv_sp[:, HI, k], wv_sp[:, LO, k]) for k in range(KT)], rhs).then_inc(v_ps, 1)
                pe.wait_ge(v_sb, f * 2 + 2)
                for s in range(ST):
                    last = pe.transpose(vps[:, s * P:s * P + P], v_t[:, s * P:s * P + P], ident[:])
                last.then_inc(v_ps, 1)

            batches(pe, body)


def attention_and_scan(nc, dm, g, x, scr):
    B, KT, ST, N, H, HD = dm.B, dm.KT, dm.ST, dm.N, dm.H, dm.HD
    GH = 4
    STEPS = GH * ST
    TPB = H // GH
    TURNS = B * TPB
    NG = N // TPB
    PIECES = NG * KT
    SCALE = float(HD) ** -0.5
    DA, HB, ADD_LAG = 4, 8, 4
    T_LAG, V_LAG = 5, 6
    OUT0 = V_LAG
    PROJECT = {0: [(1, 0)], 1: [(1, 1)], 2: [(1, 2), (1, 3)], 5: [(2, 0), (2, 1)], 6: [(2, 2), (2, 3)],
               10: [(3, k) for k in range(KT)], 12: [(4, 0)], 13: [(4, 1)], 14: [(4, 2), (4, 3)]}
    Q_OUT = {3: 1, 7: 2, 11: 3, 15: 4}
    SCANS = [0, 0, 1, 1, 0, 1, 2, 2, 2, 2, 2, 1, 1, 1, 0, 0]
    FIRST_SCAN = [sum(SCANS[:i]) for i in range(STEPS + 1)]
    with ExitStack() as ctx:
        sb = lambda n, s, d=F32: ctx.enter_context(nc.sbuf_tensor(n, s, d))
        ps = lambda n: ctx.enter_context(nc.psum_tensor(n, [P, T], F32))
        ident = g.ident
        xk_s = sb("xk_s", [P, 2, XK_ROWS, T], F32R)
        wq_s = sb("wq_s", [P, GH, 2, KT, HD], F32R)
        wo_s = sb("wo_s", [P, GH, 2, dm.D], F32R)
        v_s = sb("v_s", [P, T])
        q_s = sb("q_s", [P, 2, 2, T], F32R)
        p_s = sb("p_s", [P, 2, ST, T])
        pt_s = sb("pt_s", [P, 2, T])
        o_s = sb("o_s", [P, GH, 2, T], F32R)
        xa = sb("xa", [P, ST, T])
        mam_s = sb("mam_s", [P, 3, KT, T])
        d_a = sb("d_a", [P, DA, T])
        hb = sb("hb", [P, HB, T])
        bcs = sb("bcs", [P, 2, 2, T])
        nmax = sb("nmax", [P, STEPS])
        rsum = sb("rsum", [P, STEPS])
        rinv = sb("rinv", [P, STEPS])
        qps, ops = ps("qps"), ps("ops")
        sps = [ps("sps0"), ps("sps1")]
        tps = [ps("tps0"), ps("tps1")]
        ups = [ps("ups0"), ps("ups1")]
        names = ("xk_in wo_in x_in q_ps q_hi q_lo s_ps smax p_exp rc p_nrm t_ps pt_sb pv o_hi o_lo out_ps acc "
                 "m_da m_dbu m_scan m_prod m_add x1_st").split()
        (xk_in, wo_in, x_in, q_ps, q_hi, q_lo, s_ps, smax, p_exp, rc, p_nrm, t_ps, pt_sb, pv, o_hi, o_lo,
         out_ps, acc, m_da, m_dbu, m_scan, m_prod, m_add, x1_st) = [
            ctx.enter_context(nc.semaphore("a_" + n)) for n in names]
        several = lambda n, m: [ctx.enter_context(nc.semaphore(f"a_{n}{j}")) for j in range(m)]
        wq_in, bc_in, v_in = several("wq_in", GH), several("bc_in", 2), several("v_in", ST)
        dt_in, y_in, y_st = several("dt_in", KT), several("y_in", KT), several("y_st", KT)
        xt_in = several("xt_in", KT)
        block = ctx.enter_context(nc.Block())

        @block.sync
        def _(sp):
            def load_xk(b):
                sp.dma_start(xk_s[:, b % 2].bitcast(F32), scr.xk[b]).then_inc(xk_in, 16)

            def load_wq(G):
                sp.dma_start(wq_s[:, G % GH].bitcast(F32), scr.wq[G % H]).then_inc(wq_in[G % GH], 16)

            def load_wo(it):
                h0 = it % TPB * GH
                sp.dma_start(wo_s[:].bitcast(F32), scr.wo[h0:h0 + GH].rearrange("h p two f -> p h two f"))\
                    .then_inc(wo_in, 16)

            def load_bc(n):
                sp.dma_start(bcs[:, n % 2], scr.bc[n // N, n % N].rearrange("(o t) c -> o t c", o=1)
                             .to_broadcast([P, 2, T])).then_inc(bc_in[n % 2], 16)

            def load_dt(b, k):
                sp.dma_start(mam_s[:, DT:DTU + 1, k], scr.mam[b, :, DT:DTU + 1, k]).then_inc(dt_in[k], 16)

            def load_y(b, k):
                sp.dma_start(mam_s[:, Y0, k], scr.mam[b, :, Y0, k]).then_inc(y_in[k], 16)

            def store_y(b, k):
                sp.dma_start(scr.y[b, :, k], mam_s[:, Y0, k]).then_inc(y_st[k], 16)

            def load_v(b, t):
                sp.dma_start(v_s[:, t * P:t * P + P], scr.v[b, :, t * P:t * P + P]).then_inc(v_in[t], 16)

            load_wq(0)
            for k in range(KT):
                hi_lo = slice(k, k + KT + 1, KT)
                sp.dma_start(xk_s[:, 0, hi_lo].bitcast(F32), scr.xk[0, :, hi_lo]).then_inc(xt_in[k], 16)
            sp.dma_start(xk_s[:, 0, XK_KHI:].bitcast(F32), scr.xk[0, :, XK_KHI:]).then_inc(xk_in, 16)
            load_bc(0)
            load_dt(0, 0)
            load_wq(1)
            for k in range(1, KT):
                load_dt(0, k)
            load_bc(1)
            for t in range(ST):
                load_v(0, t)
            for G in range(2, GH):
                load_wq(G)
            for k in range(KT):
                load_y(0, k)
            sp.wait_ge(q_ps, 1)
            load_wq(GH)
            load_wo(0)
            sp.dma_start(xa[:], x[0].rearrange("(s p) f -> p s f", p=P)).then_inc(x_in, 16)
            for it in range(TURNS):
                b = it // TPB
                new = it % TPB == 0
                for j in range(GH):
                    G = it * GH + j
                    if new and j == 0 and b:
                        for k in range(KT):
                            sp.wait_ge(m_scan, it * PIECES - KT + k + 1 + DA)
                            load_dt(b, k)
                        for k in range(KT):
                            sp.wait_ge(m_add, it * PIECES - KT + k + 1 + HB)
                            store_y(b - 1, k)
                        for k in range(KT):
                            sp.wait_ge(y_st[k], 16 * b)
                            load_y(b, k)
                    if new and j == 1 and b:
                        for t in range(ST):
                            sp.wait_ge(pv, it * STEPS - ST + t + 1 + 2)
                            load_v(b, t)
                    if 2 <= G + 1 < TURNS * NG:
                        sp.wait_ge(m_prod, G * KT)
                        load_bc(G + 1)
                    if G + 1 + GH < B * H:
                        sp.wait_ge(q_ps, G + 2)
                        load_wq(G + 1 + GH)
                    if new and j == 1:
                        if b + 1 < B:
                            if b:
                                sp.wait_ge(s_ps, it * STEPS + 8)
                                sp.wait_ge(xk_in, 16 * (b + 1))
                            load_xk(b + 1)
                    if j == 2 and it:
                        sp.wait_ge(out_ps, it * ST + 4)
                        load_wo(it)
                    if j == 3 and new and b:
                        sp.wait_ge(acc, it * ST + 2)
                        sp.dma_start(scr.x1[b - 1], xa[:]).then_inc(x1_st, 16)
                        sp.wait_ge(x1_st, 16 * b)
                        sp.dma_start(xa[:], x[b].rearrange("(s p) f -> p s f", p=P)).then_inc(x_in, 16)
            for k in range(KT):
                sp.wait_ge(m_add, TURNS * PIECES - KT + k + 1 + HB)
                store_y(B - 1, k)
            sp.wait_ge(acc, TURNS * ST + 2)
            sp.dma_start(scr.x1[B - 1], xa[:]).then_inc(x1_st, 16)
            sp.wait_ge(x1_st, 16 * B)
            for k in range(KT):
                sp.wait_ge(y_st[k], 16 * B)

        class Turn:

            def __init__(self, it, g4, g16, first=False, final=False, tail=False):
                self.it, self.g4, self.g16, self.first, self.final, self.tail = it, g4, g16, first, final, tail

            def has(self, i):
                return not (self.first and i < 0) and not (self.tail and i >= 0) and not (self.final and i >= STEPS)

        def turns(eng, body):
            body(Turn(0, 0, 0, first=True))
            with eng.Fori(1, TURNS - 1) as it:
                body(Turn(it, eng.snap(it * GH), eng.snap(it * STEPS)))
            body(Turn(TURNS - 1, (TURNS - 1) * GH, (TURNS - 1) * STEPS, final=True))
            body(Turn(TURNS, TURNS * GH, TURNS * STEPS, tail=True))

        @block.tensor
        def _(pe):
            pe.sem_inc(s_ps, 8)
            pe.sem_inc(t_ps, 8)
            pe.sem_inc(pv, 2)
            pe.sem_inc(out_ps, 4)

            def project(u, slot, j, k):
                if k == 0:
                    pe.wait_ge(wq_in[j % GH], (u.it + j // GH) * 16 + 16)
                    pe.wait_ge(q_lo, u.g4 + (j + 1))
                last = split_matmul(pe, qps[:], wq_s[:, j % GH, HI, k], wq_s[:, j % GH, LO, k], xk_s[:, slot, k],
                                    xk_s[:, slot, 4 + k], k == 0, k == KT - 1)
                if k == KT - 1:
                    last.then_inc(q_ps, 1)

            def scores(u, slot, i):
                j, s = divmod(i, ST)
                if s == 0:
                    pe.wait_ge(q_lo, u.g4 + (j + 2))
                pe.wait_ge(p_exp, u.g16 + (i + 1))
                c = slice(s * P, s * P + P)
                split_matmul(pe, sps[s % 2][:], q_s[:, j % 2, HI, c], q_s[:, j % 2, LO, c], xk_s[:, slot, XK_KHI],
                             xk_s[:, slot, XK_KLO], True, True).then_inc(s_ps, 1)

            def transpose(u, i):
                j, t = i // ST, i % ST
                if t == 0:
                    pe.wait_ge(p_nrm, u.g16 + (i + ST))
                pe.wait_ge(pt_sb, u.g16 + (i + 1))
                for s in range(ST):
                    last = pe.transpose(tps[t % 2][:, s * P:s * P + P], p_s[:, j % 2, s, t * P:t * P + P], ident[:])
                last.then_inc(t_ps, 1)

            def values(u, i):
                j, t = i // ST, i % ST
                if j % GH == 0:
                    pe.wait_ge(v_in[t], (u.it + j // GH) // TPB * 16 + 16)
                if t == 0:
                    pe.wait_ge(o_lo, u.g4 + (j + 1))
                pe.wait_ge(pt_sb, u.g16 + (i + 3))
                pe.matmul(ops[:], v_s[:, t * P:t * P + P], pt_s[:, t % 2], start=t == 0, stop=t == ST - 1)\
                    .then_inc(pv, 1)

            def output(u, s):
                if s == 0:
                    pe.wait_ge(o_lo, u.g4 + 1)
                    pe.wait_ge(wo_in, u.it * 16)
                pe.wait_ge(acc, u.g4 + (s - ST + 1))
                c = slice(s * P, s * P + P)
                split_matmuls(pe, ups[s % 2][:], [(o_s[:, h, HI, c], o_s[:, h, LO, c]) for h in range(GH)],
                              [(wo_s[:, h, HI], wo_s[:, h, LO]) for h in range(GH)]).then_inc(out_ps, 1)

            def body(u):
                if u.first:
                    for k in range(KT):
                        pe.wait_ge(xt_in[k], 16)
                        project(u, 0, 0, k)
                    pe.wait_ge(xk_in, 16)
                if not u.tail:
                    slot = u.it // TPB % 2
                    slot = slot if u.first or u.final else pe.snap(slot)
                    after = (u.it + 1) // TPB % 2
                    after = after if u.first or u.final else pe.snap(after)
                for i in range(STEPS):
                    if u.has(i):
                        scores(u, slot, i)
                    if u.has(i - T_LAG):
                        transpose(u, i - T_LAG)
                    for j, k in PROJECT.get(i, ()):
                        if u.has(j * ST) and not u.tail:
                            if j == GH and k == 0:
                                pe.wait_ge(xk_in, (u.it + 1) // TPB * 16 + 16)
                            project(u, after if j == GH else slot, j, k)
                    if u.has(i - V_LAG):
                        values(u, i - V_LAG)
                    if not u.first and OUT0 <= i < OUT0 + ST:
                        output(u, i - OUT0)

            turns(pe, body)

        @block.scalar
        def _(act):
            act.sem_inc(p_exp, 2)
            act.sem_inc(pt_sb, 2)

            def q_high(u, j):
                act.wait_ge(q_ps, u.g4 + (j + 1))
                act.wait_ge(s_ps, u.g16 + (j * ST + 4))
                act.activation(q_s[:, j % 2, HI], qps[:], ACT.Copy, scale=SCALE).then_inc(q_hi, 1)

            def exps(u, i):
                j, s = divmod(i, ST)
                if s == 0:
                    act.wait_ge(t_ps, u.g16 + (i + 4))
                act.wait_ge(smax, u.g16 + (i + 1))
                act.activation(p_s[:, j % 2, s], sps[s % 2][:], ACT.Exp, bias=nmax[:, i:i + 1],
                               accum_out=rsum[:, i:i + 1]).then_inc(p_exp, 1)

            def pt_out(u, i):
                act.wait_ge(t_ps, u.g16 + (i + 1 + 8))
                act.wait_ge(pv, u.g16 + (i + 1))
                act.copy(pt_s[:, i % 2], tps[i % 2][:]).then_inc(pt_sb, 1)

            def o_high(u, j):
                act.wait_ge(out_ps, u.g4 + j // GH * ST + 4)
                act.wait_ge(pv, u.g16 + (j * ST + ST + 2))
                act.copy(o_s[:, j % GH, HI], ops[:]).then_inc(o_hi, 1)

            def decay(u, k):
                if k < KT:
                    act.wait_ge(dt_in[k], u.it // TPB * 16 + 16)
                act.wait_ge(m_scan, u.g16 + (k + 1))
                n = u.it % TPB * NG + k // KT
                act.activation(d_a[:, k % DA], mam_s[:, DT, k % KT], ACT.Exp,
                               scale=g.a_neg[:, n, k % KT:k % KT + 1]).then_inc(m_da, 1)

            def body(u):
                if u.first:
                    q_high(u, 0)
                for i in range(STEPS):
                    if i in Q_OUT and not u.tail and u.has(Q_OUT[i] * ST):
                        q_high(u, Q_OUT[i])
                    if i % ST == V_LAG % ST and u.has(i - V_LAG - ST):
                        o_high(u, (i - V_LAG - ST) // ST)
                    if not u.tail:
                        for k in range(FIRST_SCAN[i], FIRST_SCAN[i + 1]):
                            decay(u, k)
                        exps(u, i)
                    if u.has(i - T_LAG):
                        pt_out(u, i - T_LAG)

            turns(act, body)

        @block.vector
        def _(dve):
            dve.sem_inc(q_lo, 1)
            dve.sem_inc(o_lo, 1)
            dve.sem_inc(acc, 2)
            dve.sem_inc(m_scan, DA)

            def q_low(u, j):
                dve.wait_ge(q_hi, u.g4 + (j + 1))
                dve.scalar_tensor_tensor(q_s[:, j % 2, LO], qps[:], SCALE, q_s[:, j % 2, HI].bitcast(F32),
                                         ALU.mult, ALU.subtract).then_inc(q_lo, 1)

            def row_max(u, i):
                dve.wait_ge(s_ps, u.g16 + (i + 1 + 8))
                dve.tensor_reduce(nmax[:, i:i + 1], sps[i % 2][:], axis=AX_X, op=ALU.max, negate=True).then_inc(smax, 1)

            def normalise(u, i):
                s = i % ST
                dve.wait_ge(p_exp, u.g16 + (i + 1 + 2))
                dve.reciprocal(rinv[:, i % STEPS:i % STEPS + 1], rsum[:, i % STEPS:i % STEPS + 1]).then_inc(rc, 1)
                dve.wait_ge(rc, u.g16 + (i + 1))
                dve.tensor_scalar(p_s[:, i // ST % 2, s], p_s[:, i // ST % 2, s], rinv[:, i % STEPS:i % STEPS + 1], None,
                                  ALU.mult).then_inc(p_nrm, 1)

            def o_low(u, j):
                dve.wait_ge(o_hi, u.g4 + (j + 1))
                dve.tensor_tensor(o_s[:, j % GH, LO], ops[:], o_s[:, j % GH, HI].bitcast(F32), ALU.subtract)\
                    .then_inc(o_lo, 1)

            def add_out(u, s):
                if s == 0:
                    dve.wait_ge(x_in, (u.it - 1) // TPB * 16 + 16)
                dve.wait_ge(out_ps, u.g4 + (s + 1))
                dve.wait_ge(acc, u.g4 + (s - ST + 2))
                dve.tensor_tensor(xa[:, s], ups[s % 2][:], xa[:, s], ALU.add).then_inc(acc, 1)

            def scan(u, k):
                dve.wait_ge(m_da, u.g16 + (k + 1))
                dve.wait_ge(m_dbu, u.g16 + (k + 1))
                dve.tensor_tensor_scan(hb[:, k % HB], d_a[:, k % DA], hb[:, k % HB], 0.0, ALU.mult, ALU.add)\
                    .then_inc(m_scan, 1)

            def times_c(u, k):
                dve.wait_ge(m_scan, u.g16 + (k + 1 + DA))
                dve.tensor_tensor(hb[:, k % HB], hb[:, k % HB], bcs[:, k // KT % 2, 1], ALU.mult).then_inc(m_prod, 1)

            def body(u):
                if u.first:
                    q_low(u, 0)
                if u.tail:
                    normalise(u, -1)
                    times_c(u, -1)
                for i in range(STEPS):
                    if i in Q_OUT and not u.tail and u.has(Q_OUT[i] * ST):
                        q_low(u, Q_OUT[i])
                    if not u.tail:
                        row_max(u, i)
                    if i % ST == V_LAG % ST and u.has(i - V_LAG - ST):
                        o_low(u, (i - V_LAG - ST) // ST)
                    if not u.tail:
                        if u.has(i - 1):
                            normalise(u, i - 1)
                        for k in range(FIRST_SCAN[i], FIRST_SCAN[i + 1]):
                            scan(u, k)
                            if u.has(k - 1):
                                times_c(u, k - 1)
                    if not u.first and OUT0 <= i < OUT0 + ST:
                        add_out(u, i - OUT0)

            turns(dve, body)

        @block.gpsimd
        def _(pool):
            pool.sem_inc(m_add, HB)

            def dbu(u, k):
                n = k // KT
                if k < KT:
                    pool.wait_ge(dt_in[k], u.it // TPB * 16 + 16)
                if k % KT == 0:
                    pool.wait_ge(bc_in[n % 2], u.it * (NG // 2 * 16) + (n // 2 + 1) * 16)
                pool.wait_ge(m_add, u.g16 + (k + 1))
                pool.tensor_tensor(hb[:, k % HB], mam_s[:, DTU, k % KT], bcs[:, n % 2, 0], ALU.mult).then_inc(m_dbu, 1)

            def add_y(u, k):
                if 0 <= k < KT:
                    pool.wait_ge(y_in[k], u.it // TPB * 16 + 16)
                pool.wait_ge(m_prod, u.g16 + (k + 1))
                pool.wait_ge(m_add, u.g16 + (k - KT + 1 + HB))
                y = mam_s[:, Y0, k % KT]
                pool.tensor_tensor(y, y, hb[:, k % HB], ALU.add).then_inc(m_add, 1)

            def body(u):
                for k in range(PIECES):
                    if u.has(k):
                        dbu(u, k)
                    if u.has(k - ADD_LAG):
                        add_y(u, k - ADD_LAG)

            turns(pool, body)


def gate_route_shared(nc, dm, g, gate_w, gate_bias, fc1_w, fc2_w, up_w, down_w, scr):
    B, KT, ST, E, L, S = dm.B, dm.KT, dm.ST, dm.E, dm.L, dm.S
    LT, SJ = L // P, S // P
    G, TOPG, TOPK, ROUTED = 4, 2, 8, 2.5
    OUT = -1e30
    TAKEN = -3e38
    GATE_AT, ROOT_AT = 2, 4
    with ExitStack() as ctx:
        sb = lambda n, s, d=F32: ctx.enter_context(nc.sbuf_tensor(n, s, d))
        ps = lambda n: ctx.enter_context(nc.psum_tensor(n, [P, T], F32))
        ident = g.ident
        x2 = sb("x2", [P, ST, T])
        y_t = sb("y_t", [P, KT, T])
        xn = sb("xn3", [P, ST, T])
        stats = sb("stats3", [P, ST, 6])
        mv = sb("mv3", [P, ST, 2])
        sc = sb("sc3", [P, 6, ST])
        xt = sb("xt", [P, 2, KT, T], F32R)
        with nc.sbuf_tensor("w_n", [P, 2, SJ, T], F32) as w_n:
            pass
        s_t = sb("s_t", [P, 2, SJ, T], F32R)
        hr = sb("hr", [P, 4, T])
        xb = sb("xb", [P, ST, T])
        bias = sb("bias", [P, E])
        lower = sb("lower", [P, G, G])
        score = sb("score", [P, ST, E])
        sbias = sb("sbias", [P, ST, E])
        top = sb("top", [P, ST, G, 8])
        gs = sb("gs", [P, ST, G])
        gt = sb("gt", [P, ST, G, G])
        eq = sb("eq", [P, ST, G, G])
        rank = sb("rank", [P, ST, G])
        cand = sb("cand", [P, ST, E])
        top8 = sb("top8", [P, ST, 8])
        repl = sbias
        cw = sb("cw3", [P, ST, E])
        wsum = sb("wsum", [P, ST])
        winv = sb("winv", [P, ST])
        cw_t = sb("cw_t", [E, T])
        lgt = cw_t
        tp = [ps("tp0"), ps("tp1")]
        lg, ct = ps("lg"), ps("ct")
        up = [ps("up0"), ps("up1")]
        dn = [ps("dn0"), ps("dn1")]
        up_n = w_n[:, HI]
        dn_n = w_n[:, LO].rearrange("p (k a) c -> p k (a c)", k=KT)
        f1_n = hr[:, 0:LT]
        f2_n = hr[:, LT:2 * LT].rearrange("p a (b c) -> p (a b) c", c=L)
        gt_n = cw_t
        wps = up + dn
        gt_in, f1_in, f2_in, up_in, dn_in, w_ps, w_hi, w_lo = [
            ctx.enter_context(nc.semaphore("w_" + n)) for n in "gt_in f1_in f2_in up_in dn_in w_ps w_hi w_lo".split()]
        items = [(gt_in, [gt_n[:, k * P:k * P + P] for k in range(KT)], g.gate_t[:, HI], g.gate_t[:, LO])]
        for i in range(LT):
            items.append((f1_in, [f1_n[:, i, k * P:k * P + P] for k in range(KT)],
                          g.fc1_t[:, HI, :, i * P:i * P + P], g.fc1_t[:, LO, :, i * P:i * P + P]))
            items.append((f2_in, [f2_n[:, k, i * P:i * P + P] for k in range(KT)], g.fc2_t[:, HI, i], g.fc2_t[:, LO, i]))
        for j in range(SJ):
            items.append((up_in, [up_n[:, j, k * P:k * P + P] for k in range(KT)],
                          g.up_t[:, HI, :, j * P:j * P + P], g.up_t[:, LO, :, j * P:j * P + P]))
        for j in range(SJ):
            items.append((dn_in, [dn_n[:, k, j * P:j * P + P] for k in range(KT)], g.dn_t[:, HI, j], g.dn_t[:, LO, j]))

        def shaped(bank, blocks, like):
            w = blocks[0].shape[0]
            ap = bank[:, 0:len(blocks) * w]
            return ap.rearrange("p (k c) -> p k c", c=w) if len(like.shape) == 3 else ap

        names = ("c_in x_in y_in z_ok var1 std1 sz_ok yt_ps g1 x2_ok var2 std2 xn_ok t_ps xt_hi xt_lo l_ps sc_ok cw_ok "
                 "cwt_ps cwt_sb cw_st f_ps f_hi f_lo u_ps r_ok h_ok h_hi h_lo d_ps d_ok chain low0 low1 lgt_ok x2_st").split()
        (c_in, x_in, y_in, z_ok, var1, std1, sz_ok, yt_ps, g1, x2_ok, var2, std2, xn_ok, t_ps, xt_hi, xt_lo, l_ps, sc_ok,
         cw_ok, cwt_ps, cwt_sb, cw_st, f_ps, f_hi, f_lo, u_ps, r_ok, h_ok, h_hi, h_lo, d_ps, d_ok, chain, low0,
         low1, lgt_ok, x2_st) = [ctx.enter_context(nc.semaphore("g_" + n)) for n in names]
        xb_in = [ctx.enter_context(nc.semaphore(f"g_xb_in{q}")) for q in range(ST)]
        part_st = [ctx.enter_context(nc.semaphore(f"g_part_st{q}")) for q in range(ST)]
        block = ctx.enter_context(nc.Block())

        def batches(eng, first_body, body):
            first_body()
            with eng.Fori(0, B - 1) as b:
                body(b, eng.snap(b + 1))
            body(B - 1, None)

        @block.sync
        def _(sp):
            sp.sem_inc(cw_st, 16)
            sp.dma_start(bias[:], gate_bias.rearrange("(o e) -> o e", o=1).to_broadcast([P, E])).then_inc(c_in, 16)

            def load(f):
                sp.dma_start(x2[:], scr.x1[f]).then_inc(x_in, 16)

            def load_y(f):
                sp.dma_start(y_t[:], scr.y[f]).then_inc(y_in, 16)

            def load_xb(g_, s):
                sp.dma_start(xb[:, s], scr.x1[g_, :, s]).then_inc(xb_in[s], 16)

            load(0)
            sp.dma_start(gt_n[:], gate_w).then_inc(gt_in, 16)
            sp.dma_start(f1_n, fc1_w.rearrange("(j p) f -> p j f", p=P)).then_inc(f1_in, 16)
            sp.dma_start(f2_n, fc2_w.rearrange("(j p) f -> p j f", p=P)).then_inc(f2_in, 16)
            sp.dma_start(up_n, up_w.rearrange("(j p) f -> p j f", p=P)).then_inc(up_in, 16)
            load_y(0)
            sp.dma_start(dn_n, down_w.rearrange("(j p) f -> p j f", p=P)).then_inc(dn_in, 16)
            for g_ in range(-1, B):
                f = g_ + 1
                if g_ >= 0:
                    for s in range(ST):
                        if g_:
                            sp.wait_ge(part_st[s], g_ * 16)
                        load_xb(g_, s)
                if f < B:
                    sp.wait_ge(x2_ok, (f + 1) * ST + 2)
                    sp.dma_start(scr.x1[f], x2[:]).then_inc(x2_st, 16)
                    if f + 1 < B:
                        sp.wait_ge(yt_ps, (f + 1) * ST)
                        load_y(f + 1)
                    sp.wait_ge(x2_st, (f + 1) * 16)
                    if f + 1 < B:
                        sp.wait_ge(xn_ok, (f + 1) * ST)
                        load(f + 1)
                if g_ >= 0:
                    for s in range(ST):
                        sp.wait_ge(d_ok, g_ * ST + s + 1 + 2)
                        sp.dma_start(scr.part[g_, :, s], xb[:, s]).then_inc(part_st[s], 16)
                        if s == 1:
                            sp.wait_ge(cwt_sb, g_ + 1)
                            sp.dma_start(scr.cw.rearrange("e (b t) -> b e t", b=B)[g_], cw_t[:]).then_inc(cw_st, 16)
            for q in range(ST):
                sp.wait_ge(part_st[q], 16 * B)
            sp.wait_ge(cw_st, B * 16 + 16)

        @block.gpsimd
        def _(pool):
            pool.sem_inc(h_lo, 4)
            pool.memset(lower[:], 1.0).then_inc(low0, 1)
            pool.wait_ge(low0, 1)
            pool.affine_select(out=lower[:], in_=lower[:], compare_op=ALU.is_gt, fill=0.0, base=0,
                               pattern=[[1, G], [-1, G]], channel_multiplier=0).then_inc(low1, 1)
            with pool.Fori(0, B) as b:
                for j in range(SJ + 1):
                    if j < SJ:
                        pool.wait_ge(r_ok, b * SJ + j + 1 + 2)
                        pool.tensor_tensor(hr[:, j % 4], hr[:, j % 4], hr[:, j % 4], ALU.mult).then_inc(h_ok, 1)
                    if j:
                        i = j - 1
                        pool.wait_ge(h_hi, b * SJ + i + 1)
                        pool.tensor_tensor(s_t[:, LO, i], hr[:, i % 4], s_t[:, HI, i].bitcast(F32), ALU.subtract)\
                            .then_inc(h_lo, 1)

        @block.scalar
        def _(act):
            act.sem_inc(r_ok, 2)
            act.sem_inc(sc_ok, 1)

            def weight_high(n):
                loaded, blocks, hi, lo = items[n]
                act.wait_ge(w_ps, n + 1)
                act.copy(hi, shaped(wps[n % 4], blocks, hi)).then_inc(w_hi, 1)

            def root(ready, done, count):
                act.wait_ge(ready, count)
                act.activation(sc[:, 1], sc[:, 0], ACT.Sqrt).then_inc(done, 1)

            def latent_high(g_, i):
                act.wait_ge(f_ps, g_ * LT + i + 1)
                act.copy(g.xl[:, HI, i, bass.ds(g_ * T, T)], dn[i % 2][:]).then_inc(f_hi, 1)

            def relu(g_, j):
                act.wait_ge(u_ps, g_ * SJ + j + 1 + 8)
                act.wait_ge(h_lo, g_ * SJ + j + 1)
                act.activation(hr[:, j % 4], up[j % 2][:], ACT.Relu).then_inc(r_ok, 1)

            def high(g_, j):
                if j == 0:
                    act.wait_ge(d_ps, g_ * ST + 4)
                act.wait_ge(h_ok, g_ * SJ + j + 1)
                act.copy(s_t[:, HI, j], hr[:, j % 4]).then_inc(h_hi, 1)

            def first_body():
                for n in range(2):
                    weight_high(n)
                root(var1, std1, 1)
                n = 2
                for s in range(ST):
                    weight_high(n)
                    n += 1
                    act.wait_ge(z_ok, s + 1)
                    act.activation(xn[:, s], xn[:, s], ACT.Silu).then_inc(sz_ok, 1)
                while n < 17:
                    weight_high(n)
                    n += 1
                root(var2, std2, 1)
                for k in range(KT):
                    act.wait_ge(t_ps, k + 1)
                    act.copy(xt[:, HI, k], tp[k % 2][:]).then_inc(xt_hi, 1)
                    weight_high(n)
                    n += 1

            def body(g_, f):
                if g_ is not None:
                    act.wait_ge(l_ps, g_ * 2 + 1)
                    act.wait_ge(cw_st, g_ * 16 + 16)
                    act.copy(lgt[:], lg[0:E, :]).then_inc(lgt_ok, 1)
                if f is not None:
                    root(var1, std1, f + 1)
                    for s in range(ST):
                        act.wait_ge(z_ok, f * ST + s + 1)
                        act.activation(xn[:, s], xn[:, s], ACT.Silu).then_inc(sz_ok, 1)
                if g_ is not None:
                    act.wait_ge(l_ps, g_ * 2 + 2)
                    act.activation(score[:], lg[:, 0:ST * E], ACT.Sigmoid).then_inc(sc_ok, 1)
                    for j in range(SJ):
                        relu(g_, j)
                        if j:
                            high(g_, j - 1)
                        if j == ROOT_AT and f is not None:
                            root(var2, std2, f + 1)
                    high(g_, SJ - 1)
                    for i in range(LT):
                        latent_high(g_, i)
                else:
                    root(var2, std2, f + 1)
                if f is not None:
                    for k in range(KT):
                        act.wait_ge(t_ps, f * KT + k + 1)
                        if k == 0:
                            act.wait_ge(u_ps, f * SJ + 8)
                        act.copy(xt[:, HI, k], tp[k % 2][:]).then_inc(xt_hi, 1)
                if g_ is not None:
                    act.wait_ge(cwt_ps, g_ + 1)
                    act.copy(cw_t[:], ct[0:E, :]).then_inc(cwt_sb, 1)

            batches(act, first_body, body)

        @block.vector
        def _(dve):
            dve.sem_inc(x2_ok, 2)
            dve.sem_inc(xt_lo, 2)
            dve.sem_inc(d_ok, 2)
            dve.sem_inc(f_lo, 2)
            dve.wait_ge(c_in, 16)
            dve.wait_ge(low1, 1)

            def weight_low(n):
                loaded, blocks, hi, lo = items[n]
                dve.wait_ge(w_hi, n + 1)
                dve.tensor_tensor(lo, shaped(wps[n % 4], blocks, hi), hi.bitcast(F32), ALU.subtract).then_inc(w_lo, 1)

            def norm(f, m, var, std, done):
                n = layer_norm(dve, chain, m, x2, xn, stats, mv, sc, var, std, f + 1, lambda i: i.then_inc(done, 1))
                dve.wait_ge(chain, n)
                return n

            def gate(f, s):
                dve.wait_ge(sz_ok, f * ST + s + 1)
                dve.tensor_tensor(y_t[:, s], y_t[:, s], xn[:, s], ALU.mult).then_inc(g1, 1)

            def add_gated(f, s):
                dve.wait_ge(yt_ps, f * ST + s + 1)
                dve.tensor_tensor(x2[:, s], x2[:, s], tp[s % 2][:], ALU.add).then_inc(x2_ok, 1)

            def x_low(f, k):
                dve.wait_ge(xt_hi, f * KT + k + 1)
                dve.tensor_tensor(xt[:, LO, k], tp[k % 2][:], xt[:, HI, k].bitcast(F32), ALU.subtract).then_inc(xt_lo, 1)

            def first_body():
                dve.wait_ge(x_in, 16)
                m = norm(0, 0, var1, std1, z_ok)
                dve.wait_ge(y_in, 16)
                for n in range(5):
                    weight_low(n)
                for s in range(ST):
                    gate(0, s)
                for n in range(5, 9):
                    weight_low(n)
                for s in range(ST):
                    add_gated(0, s)
                    weight_low(9 + s)
                dve.wait_ge(x2_ok, ST + 2)
                m = norm(0, m, var2, std2, xn_ok)
                for n in range(13, 17):
                    weight_low(n)
                dve.sem_clear(chain)
                for k in range(KT):
                    x_low(0, k)
                    weight_low(17 + k)

            def body(g_, f):
                m = [0]
                if f is not None:
                    dve.wait_ge(x_in, f * 16 + 16)
                    m[0] = layer_norm(dve, chain, 0, x2, xn, stats, mv, sc, var1, std1, f + 1,
                                      lambda i: i.then_inc(z_ok, 1))
                    dve.wait_ge(chain, m[0])
                if f is not None:
                    dve.wait_ge(y_in, f * 16 + 16)
                    for s in range(ST):
                        dve.wait_ge(sz_ok, f * ST + s + 1)
                        dve.tensor_tensor(y_t[:, s], y_t[:, s], xn[:, s], ALU.mult).then_inc(g1, 1)
                    for s in range(ST):
                        dve.wait_ge(yt_ps, f * ST + s + 1)
                        dve.tensor_tensor(x2[:, s], x2[:, s], tp[s % 2][:], ALU.add).then_inc(x2_ok, 1)
                    dve.wait_ge(x2_ok, f * ST + ST + 2)
                    m[0] = layer_norm(dve, chain, m[0], x2, xn, stats, mv, sc, var2, std2, f + 1,
                                      lambda i: i.then_inc(xn_ok, 1))
                    dve.wait_ge(chain, m[0])
                if g_ is not None:
                    for i in range(LT):
                        dve.wait_ge(f_hi, g_ * LT + i + 1)
                        dve.tensor_tensor(g.xl[:, LO, i, bass.ds(g_ * T, T)], dn[i % 2][:],
                                          g.xl[:, HI, i, bass.ds(g_ * T, T)].bitcast(F32), ALU.subtract).then_inc(f_lo, 1)
                if f is not None:
                    for k in range(KT):
                        dve.wait_ge(xt_hi, f * KT + k + 1)
                        dve.tensor_tensor(xt[:, LO, k], tp[k % 2][:], xt[:, HI, k].bitcast(F32), ALU.subtract)\
                            .then_inc(xt_lo, 1)
                if g_ is not None:
                    add_shared(g_, 0)
                    router(g_, m)
                dve.sem_clear(chain)
                if g_ is not None:
                    dve.sem_inc(cw_ok, 1)
                    for s in range(1, ST):
                        add_shared(g_, s)

            def add_shared(g_, s):
                dve.wait_ge(xb_in[s], g_ * 16 + 16)
                dve.wait_ge(d_ps, g_ * ST + s + 1 + 4)
                dve.tensor_tensor(xb[:, s], xb[:, s], dn[s % 2][:], ALU.add).then_inc(d_ok, 1)

            def router(g_, m):
                def step(ins, *waits):
                    m[0] += 1
                    ins.then_inc(chain, 1)

                def settled():
                    dve.wait_ge(chain, m[0])

                settled()
                dve.wait_ge(sc_ok, g_ + 2)
                step(dve.tensor_tensor(sbias[:], score[:], bias[:].unsqueeze(1).to_broadcast([P, ST, E]), ALU.add))
                settled()
                for s in range(ST):
                    for q in range(G):
                        step(dve.max(top[:, s, q], sbias[:, s, q * (E // G):(q + 1) * (E // G)]))
                settled()
                step(dve.tensor_tensor(gs[:], top[:, :, :, 0], top[:, :, :, 1], ALU.add))
                settled()
                for s in range(ST):
                    mine = gs[:, s].unsqueeze(2).to_broadcast([P, G, G])
                    other = gs[:, s].unsqueeze(1).to_broadcast([P, G, G])
                    step(dve.tensor_tensor(gt[:, s], other, mine, ALU.is_gt))
                    step(dve.tensor_tensor(eq[:, s], other, mine, ALU.is_equal))
                settled()
                for s in range(ST):
                    step(dve.tensor_tensor(eq[:, s], eq[:, s], lower[:], ALU.mult))
                settled()
                step(dve.tensor_tensor(gt[:], gt[:], eq[:], ALU.add))
                settled()
                step(dve.tensor_reduce(rank[:], gt[:], axis=AX_X, op=ALU.add))
                settled()
                step(dve.tensor_scalar(rank[:], rank[:], TOPG - 0.5, OUT, ALU.is_gt, ALU.mult))
                settled()
                for s in range(ST):
                    step(dve.tensor_tensor(cand[:, s].rearrange("p (g e) -> p g e", g=G),
                                           sbias[:, s].rearrange("p (g e) -> p g e", g=G),
                                           rank[:, s].unsqueeze(2).to_broadcast([P, G, E // G]), ALU.add))
                settled()
                for s in range(ST):
                    step(dve.max(top8[:, s], cand[:, s]))
                settled()
                for s in range(ST):
                    step(dve.match_replace(repl[:, s], top8[:, s], cand[:, s], TAKEN))
                settled()
                step(dve.scalar_tensor_tensor(cw[:], repl[:], TAKEN, score[:], ALU.is_equal, ALU.mult))
                settled()
                step(dve.tensor_reduce(wsum[:], cw[:], axis=AX_X, op=ALU.add))
                settled()
                step(dve.reciprocal(winv[:], wsum[:]))
                settled()
                for s in range(ST):
                    step(dve.tensor_scalar(cw[:, s], cw[:, s], winv[:, s:s + 1], ROUTED, ALU.mult, ALU.mult))
                settled()
            batches(dve, first_body, body)

        @block.tensor
        def _(pe):
            pe.sem_inc(u_ps, 8)
            pe.sem_inc(d_ps, 4)

            def gated_transpose(f, s):
                if s == 0:
                    pe.wait_ge(g1, f * ST + ST)
                    pe.wait_ge(xt_lo, f * KT + 2)
                pe.wait_ge(x2_ok, f * ST + s + 1)
                for k in range(KT):
                    last = pe.transpose(tp[s % 2][:, k * P:k * P + P], y_t[:, k, s * P:s * P + P], ident[:])
                last.then_inc(yt_ps, 1)

            def x_transpose(f, k):
                if k == 0:
                    pe.wait_ge(xn_ok, f * ST + ST)
                pe.wait_ge(xt_lo, f * KT + k + 1)
                for s in range(ST):
                    last = pe.transpose(tp[k % 2][:, s * P:s * P + P], xn[:, s, k * P:k * P + P], ident[:])
                last.then_inc(t_ps, 1)

            def shared_up(g_, j):
                pe.wait_ge(r_ok, g_ * SJ + j + 1)
                c = slice(j * P, j * P + P)
                split_matmuls(pe, up[j % 2][:], [(g.up_t[:, HI, k, c], g.up_t[:, LO, k, c]) for k in range(KT)],
                              x_t).then_inc(u_ps, 1)

            def shared_down(g_, s):
                if s == 0:
                    pe.wait_ge(h_lo, g_ * SJ + SJ + 4)
                    pe.wait_ge(f_lo, g_ * LT + LT + 2)
                pe.wait_ge(d_ok, g_ * ST + s + 1)
                c = slice(s * P, s * P + P)
                split_matmuls(pe, dn[s % 2][:], [(s_t[:, HI, j, c], s_t[:, LO, j, c]) for j in range(SJ)],
                              [(g.dn_t[:, HI, j], g.dn_t[:, LO, j]) for j in range(SJ)]).then_inc(d_ps, 1)

            x_t = [(xt[:, HI, k], xt[:, LO, k]) for k in range(KT)]

            def weight(n):
                loaded, blocks, hi, lo = items[n]
                pe.wait_ge(loaded, 16)
                if n >= 4:
                    pe.wait_ge(w_lo, n - 3)
                for k, blk in enumerate(blocks):
                    w = blk.shape[0]
                    last = pe.transpose(wps[n % 4][:, k * w:k * w + w], blk, ident[0:w, 0:w])
                last.then_inc(w_ps, 1)

            def first_body():
                for n in range(9):
                    weight(n)
                for s in range(ST):
                    gated_transpose(0, s)
                    weight(9 + s)
                for n in range(13, 17):
                    weight(n)
                for k in range(KT):
                    x_transpose(0, k)
                    weight(17 + k)
                pe.wait_ge(w_lo, len(items))

            def body(g_, f):
                if g_ is not None:
                    pe.wait_ge(xt_lo, g_ * KT + KT + 2)
                    pe.wait_ge(sc_ok, g_ + 1)
                    split_matmuls(pe, lg[0:E, :], [(g.gate_t[:, HI, k * E:k * E + E], g.gate_t[:, LO, k * E:k * E + E])
                                                   for k in range(KT)], x_t).then_inc(l_ps, 1)
                    pe.wait_ge(lgt_ok, g_ + 1)
                    shared_up(g_, 0)
                    for s in range(ST):
                        last = pe.transpose(lg[:, s * E:s * E + E], lgt[:, s * P:s * P + P], ident[0:E, 0:E])
                    last.then_inc(l_ps, 1)
                    for j in range(1, GATE_AT):
                        shared_up(g_, j)
                for s in range(ST):
                    if f is not None:
                        gated_transpose(f, s)
                    if g_ is not None:
                        shared_up(g_, GATE_AT + s)
                if g_ is not None:
                    for j in range(GATE_AT + ST, SJ):
                        shared_up(g_, j)
                    for i in range(LT):
                        pe.wait_ge(d_ok, g_ * ST + 2)
                        c = slice(i * P, i * P + P)
                        split_matmuls(pe, dn[i % 2][:], [(g.fc1_t[:, HI, k, c], g.fc1_t[:, LO, k, c]) for k in range(KT)],
                                      x_t).then_inc(f_ps, 1)
                for k in range(KT):
                    if f is not None:
                        x_transpose(f, k)
                    if g_ is not None and k % 2:
                        shared_down(g_, k // 2)
                if g_ is not None:
                    shared_down(g_, 2)
                    pe.wait_ge(cw_ok, g_ + 1)
                    for s in range(ST):
                        last = pe.transpose(ct[0:E, s * P:s * P + P], cw[:, s], ident[:])
                    last.then_inc(cwt_ps, 1)
                    shared_down(g_, 3)

            batches(pe, first_body, body)


def routed_experts(nc, dm, g, w1, w2, scr):
    E, I, L, B = dm.E, dm.I, dm.L, dm.B
    IT, LT = I // P, L // P
    HALVES = 2
    HTOK = B * T // HALVES
    TC = HTOK // T
    TILES = TC * IT
    with ExitStack() as ctx:
        sb = lambda n, s, d=F32: ctx.enter_context(nc.sbuf_tensor(n, s, d))
        ps = lambda n: ctx.enter_context(nc.psum_tensor(n, [P, T], F32))
        ident = g.ident
        w_nat = sb("w_nat", [P, 2, 2, IT * L])
        w_s = sb("w_s", [P, 2, 2, 2, T], F32R)
        cwb = sb("cwb", [P, 2, HTOK])
        rt = sb("rt", [P, 2, T])
        rc = sb("rc", [P, 2, T])
        hf = sb("hf", [P, TILES, T])
        h_s = sb("h_s", [P, TILES, 2, T], F32R)
        yps = [[ps(f"y{l}{c}") for c in range(TC)] for l in range(LT)]
        zps = [ps("z0"), ps("z1")]
        wps = [ps("wt0"), ps("wt1")]
        names = "wt_ps w_hi w_lo z_ps r_ok c_ok h_ok hh_ok hl_ok y_ps ye_hi ye_lo".split()
        (wt_ps, w_hi, w_lo, z_ps, r_ok, c_ok, h_ok, hh_ok, hl_ok, y_ps, ye_hi, ye_lo) = [
            ctx.enter_context(nc.semaphore("e_" + n)) for n in names]
        w_in = [ctx.enter_context(nc.semaphore(f"e_w_in{q}")) for q in range(2)]
        cw_in = [ctx.enter_context(nc.semaphore(f"e_cw_in{q}")) for q in range(2)]
        block = ctx.enter_context(nc.Block())

        @block.sync
        def _(sp):
            for X in range(HALVES * E):
                q, e, half = X % 2, X % E, X // E
                if X >= 2:
                    sp.wait_ge(wt_ps, 2 * (X - 2) + 2)
                for m, w in ((0, w1), (1, w2)):
                    sp.dma_start(w_nat[:, q, m], w[e].rearrange("(a p) c -> p a c", p=P)).then_inc(w_in[q], 16)
                if X >= 2:
                    sp.wait_ge(c_ok, TILES * (X - 2) + TILES)
                sp.dma_start(cwb[:, q], scr.cw[e:e + 1, half * HTOK:(half + 1) * HTOK].to_broadcast([P, HTOK]))\
                    .then_inc(cw_in[q], 16)

        def halves(eng, expert, finish):
            for half in range(HALVES):
                X0 = half * E
                for q in range(2):
                    expert(X0 + q, q, half, 2 * (X0 + q), TILES * (X0 + q), half * (E // 2), q == 0)
                with eng.Fori(1, E // 2) as pair:
                    x2_, x4_ = eng.snap(pair * 4 + 2 * X0), eng.snap(pair * (2 * TILES) + TILES * X0)
                    for q in range(2):
                        expert(None, q, half, x2_ + 2 * q, x4_ + TILES * q, pair + half * (E // 2), False)
                finish(half, X0 + E)

        @block.tensor
        def _(pe):
            pe.sem_inc(y_ps, 8)

            def down(q, n2, n4, n, first, last):
                if n == 0:
                    pe.wait_ge(w_lo, n2 + (2 + 2))
                c, i = divmod(n, IT)
                pe.wait_ge(hl_ok, n4 + (n + 1 + TILES))
                for l in range(LT):
                    col = slice(i * L + l * P, i * L + l * P + P)
                    ins = split_matmul(pe, yps[l][c][:], w_s[:, q, 1, HI, col], w_s[:, q, 1, LO, col],
                                       h_s[:, n, HI], h_s[:, n, LO], first and i == 0, last and i == IT - 1)
                ins.then_inc(y_ps, 1)

            def expert(X, q, half, n2, n4, pair, first):
                pe.wait_ge(w_in[q], pair * 32 + 32)
                for m in range(2):
                    pe.wait_ge(w_lo, n2 + (m + 1))
                    for a in range(2):
                        for c in range(2):
                            col = a * 2 * P + c * P
                            last = pe.transpose(wps[m][:, col:col + P],
                                                w_nat[:, q, m, c * 2 * P + a * P:c * 2 * P + a * P + P], ident[:])
                    last.then_inc(wt_ps, 1)
                is_first = X is not None and X % E == 1
                if is_first and half:
                    pe.wait_ge(ye_lo, half * LT * TC)
                for n in range(TILES):
                    if not first:
                        down(1 - q, n2 - 2, n4 - TILES, n, is_first, False)
                    if n == 0:
                        pe.wait_ge(w_lo, n2 + (1 + 2))
                    c, i = divmod(n, IT)
                    pe.wait_ge(r_ok, n4 + (n + 1))
                    tok = slice(half * HTOK + c * T, half * HTOK + c * T + T)
                    split_matmuls(pe, zps[n % 2][:],
                                  [(w_s[:, q, 0, HI, l * I + i * P:l * I + i * P + P],
                                    w_s[:, q, 0, LO, l * I + i * P:l * I + i * P + P]) for l in range(LT)],
                                  [(g.xl[:, HI, l, tok], g.xl[:, LO, l, tok]) for l in range(LT)]).then_inc(z_ps, 1)

            def finish(half, X):
                for n in range(TILES):
                    down(1, 2 * X - 2, TILES * X - TILES, n, False, True)

            halves(pe, expert, finish)

        @block.scalar
        def _(act):
            act.sem_inc(r_ok, 2)

            def high(n4, n):
                act.wait_ge(h_ok, n4 + (n + 1 + 2))
                act.wait_ge(y_ps, n4 + (n + 5))
                act.copy(h_s[:, n, HI], hf[:, n]).then_inc(hh_ok, 1)

            def last_tiles(n4):
                high(n4, TILES - 2)
                high(n4, TILES - 1)

            def expert(X, q, half, n2, n4, pair, first):
                for m in range(2):
                    act.wait_ge(wt_ps, n2 + (m + 1))
                    if m == 0:
                        act.wait_ge(y_ps, n4 + 4)
                    act.copy(w_s[:, q, m, HI], wps[m][:]).then_inc(w_hi, 1)
                if not first:
                    last_tiles(n4 - TILES)
                for n in range(TILES):
                    act.wait_ge(z_ps, n4 + (n + 1))
                    act.wait_ge(h_ok, n4 + (n + 1))
                    act.activation(rt[:, n % 2], zps[n % 2][:], ACT.Relu).then_inc(r_ok, 1)
                    if 1 <= n < TILES - 1:
                        high(n4, n - 1)

            def finish(half, X):
                last_tiles(TILES * X - TILES)
                for l in range(LT):
                    for c in range(TC):
                        act.wait_ge(y_ps, TILES * X + 8)
                        tok = slice(half * HTOK + c * T, half * HTOK + c * T + T)
                        act.copy(g.yl[:, HI, l, tok], yps[l][c][:]).then_inc(ye_hi, 1)

            halves(act, expert, finish)

        @block.gpsimd
        def _(pool):
            def expert(X, q, half, n2, n4, pair, first):
                pool.wait_ge(cw_in[q], pair * 16 + 16)
                for n in range(TILES):
                    c = n // IT
                    pool.wait_ge(r_ok, n4 + (n + 1 + 2))
                    pool.wait_ge(h_ok, n4 + (n + 1))
                    pool.tensor_tensor(rc[:, n % 2], rt[:, n % 2], cwb[:, q, c * T:c * T + T], ALU.mult).then_inc(c_ok, 1)

            halves(pool, expert, lambda half, X: None)

        @block.vector
        def _(dve):
            dve.sem_inc(w_lo, 2)
            dve.sem_inc(h_ok, 2)
            dve.sem_inc(hl_ok, TILES)

            def square(n4, n):
                dve.wait_ge(c_ok, n4 + (n + 1))
                dve.wait_ge(hl_ok, n4 + (n + 1))
                dve.tensor_tensor(hf[:, n], rc[:, n % 2], rt[:, n % 2], ALU.mult).then_inc(h_ok, 1)

            def low(n4, n):
                dve.wait_ge(hh_ok, n4 + (n + 1))
                dve.tensor_tensor(h_s[:, n, LO], hf[:, n], h_s[:, n, HI].bitcast(F32), ALU.subtract).then_inc(hl_ok, 1)

            def last_tiles(n4):
                low(n4, TILES - 2)
                square(n4, TILES - 1)
                low(n4, TILES - 1)

            def expert(X, q, half, n2, n4, pair, first):
                for m in range(2):
                    dve.wait_ge(w_hi, n2 + (m + 1))
                    dve.tensor_tensor(w_s[:, q, m, LO], wps[m][:], w_s[:, q, m, HI].bitcast(F32), ALU.subtract)\
                        .then_inc(w_lo, 1)
                if not first:
                    last_tiles(n4 - TILES)
                for n in range(TILES - 1):
                    square(n4, n)
                    if n:
                        low(n4, n - 1)

            def finish(half, X):
                last_tiles(TILES * X - TILES)
                for l in range(LT):
                    for c in range(TC):
                        dve.wait_ge(ye_hi, half * LT * TC + l * TC + c + 1)
                        tok = slice(half * HTOK + c * T, half * HTOK + c * T + T)
                        dve.tensor_tensor(g.yl[:, LO, l, tok], yps[l][c][:], g.yl[:, HI, l, tok].bitcast(F32),
                                          ALU.subtract).then_inc(ye_lo, 1)

            halves(dve, expert, finish)


def routed_output(nc, dm, g, scr, out):
    B, ST, LT = dm.B, dm.ST, dm.L // P
    with ExitStack() as ctx:
        part = ctx.enter_context(nc.sbuf_tensor("part", [P, B, ST, T], F32))
        ops = [ctx.enter_context(nc.psum_tensor(f"o{i}", [P, T], F32)) for i in range(4)]
        o_ps, o_ok, o_st = [ctx.enter_context(nc.semaphore("o_" + n)) for n in "ps ok st".split()]
        p_in = [ctx.enter_context(nc.semaphore(f"o_in{b}")) for b in range(B)]
        block = ctx.enter_context(nc.Block())

        @block.sync
        def _(sp):
            for b in range(B):
                sp.dma_start(part[:, b], scr.part[b]).then_inc(p_in[b], 16)
            for b in range(B):
                sp.wait_ge(o_ok, (b + 1) * ST)
                sp.dma_start(out[b].rearrange("(s p) f -> p s f", p=P), part[:, b]).then_inc(o_st, 16)
            sp.wait_ge(o_st, 16 * B)

        @block.tensor
        def _(pe):
            for n in range(B * ST):
                if n >= 4:
                    pe.wait_ge(o_ok, n - 3)
                c = slice(n * P, n * P + P)
                split_matmuls(pe, ops[n % 4][:], [(g.yl[:, HI, l, c], g.yl[:, LO, l, c]) for l in range(LT)],
                              [(g.fc2_t[:, HI, l], g.fc2_t[:, LO, l]) for l in range(LT)]).then_inc(o_ps, 1)

        @block.vector
        def _(dve):
            for n in range(B * ST):
                b, s = n // ST, n % ST
                if s == 0:
                    dve.wait_ge(p_in[b], 16)
                dve.wait_ge(o_ps, n + 1)
                dve.tensor_tensor(part[:, b, s], part[:, b, s], ops[n % 4][:], ALU.add).then_inc(o_ok, 1)


class Held:
    pass


class Scratch:
    pass


def program(nc, a, out):
    dm = Dims(a["x"], a["ctx_1024"], a["L0_attn_Wq"], a["L0_attn_Wk"], a["L0_xattn_in_proj_w"], a["L0_xattn_x_proj_w"],
              a["L0_xattn_dt_proj_w"], a["L0_xattn_A_log"], a["L0_ffn_w1"])
    dm.S = a["L0_ffn_shared_up_w"].shape[0]
    scr = Scratch()
    dram = lambda n, s, d=F32: nc.dram_tensor("s_" + n, s, d, kind="Internal").ap()
    scr.wq = dram("wq", [dm.H, P, 2, dm.KT, dm.HD])
    scr.wo = dram("wo", [dm.H, P, 2, dm.D])
    scr.xk = dram("xk", [dm.B, P, XK_ROWS, T])
    scr.v = dram("v", [dm.B, P, T])
    scr.mam = dram("mam", [dm.B, P, 3, dm.KT, T])
    scr.bc = dram("bc", [dm.B, dm.N, 2, T])
    scr.x1 = dram("x1", [dm.B, P, dm.ST, dm.D])
    scr.part = dram("part", [dm.B, P, dm.ST, dm.D])
    scr.cw = dram("cw", [dm.E, dm.B * T])
    scr.y = dram("y", [dm.B, P, dm.KT, T])
    with ExitStack() as ctx:
        g = Held()
        g.ident = ctx.enter_context(nc.sbuf_tensor("ident", [P, P], F32))
        g.a_neg = ctx.enter_context(nc.sbuf_tensor("a_neg", [P, dm.N, dm.KT], F32))
        prepare(nc, dm, g, a["x"], a["ctx_1024"], a["L0_attn_Wq"], a["L0_attn_Wk"], a["L0_attn_Wv"],
                a["L0_attn_Wo"],
                a["L0_xattn_in_proj_w"], a["L0_xattn_conv_w"], a["L0_xattn_conv_b"], a["L0_xattn_x_proj_w"],
                a["L0_xattn_dt_proj_w"], a["L0_xattn_dt_proj_b"], a["L0_xattn_A_log"], a["L0_xattn_D"], scr)
        attention_and_scan(nc, dm, g, a["x"], scr)
        held = lambda n, s: ctx.enter_context(nc.sbuf_tensor(n, s, F32R))
        g.fc2_t = held("fc2_t", [P, 2, dm.L // P, dm.D])
        g.xl = held("xl", [P, 2, dm.L // P, dm.B * T])
        with ExitStack() as shared:
            held = lambda n, s: shared.enter_context(nc.sbuf_tensor(n, s, F32R))
            g.gate_t = held("gate_t", [P, 2, dm.KT * dm.E])
            g.fc1_t = held("fc1_t", [P, 2, dm.KT, dm.L])
            g.up_t = held("up_t", [P, 2, dm.KT, dm.S])
            g.dn_t = held("dn_t", [P, 2, dm.S // P, dm.D])
            gate_route_shared(nc, dm, g, a["L0_ffn_gate_w"], a["L0_ffn_gate_bias"], a["L0_ffn_fc1_w"],
                              a["L0_ffn_fc2_w"], a["L0_ffn_shared_up_w"], a["L0_ffn_shared_down_w"], scr)
        g.yl = ctx.enter_context(nc.sbuf_tensor("yl", [P, 2, dm.L // P, dm.B * T], F32R))
        routed_experts(nc, dm, g, a["L0_ffn_w1"], a["L0_ffn_w2"], scr)
        routed_output(nc, dm, g, scr, out)


_INS = ['x', 'ctx_1024', 'L0_attn_Wq', 'L0_attn_Wk', 'L0_attn_Wv', 'L0_attn_Wo', 'L0_xattn_in_proj_w',
        'L0_xattn_conv_w', 'L0_xattn_conv_b', 'L0_xattn_x_proj_w', 'L0_xattn_dt_proj_w', 'L0_xattn_dt_proj_b',
        'L0_xattn_A_log', 'L0_xattn_D', 'L0_ffn_gate_w', 'L0_ffn_gate_bias', 'L0_ffn_fc1_w', 'L0_ffn_fc2_w',
        'L0_ffn_w1', 'L0_ffn_w2', 'L0_ffn_shared_up_w', 'L0_ffn_shared_down_w']


def kernel(**inputs):
    import numpy as np
    import concourse.bacc as bacc
    from concourse.bass_utils import run_bass_kernel_spmd

    nc = bacc.Bacc("TRN2", target_bir_lowering=False, num_devices=1)
    arrays, a = {}, {}
    for name in _INS:
        arrays["in_" + name] = v = np.ascontiguousarray(inputs[name])
        a[name] = nc.dram_tensor("in_" + name, v.shape, mybir.dt.from_np(v.dtype), kind="ExternalInput").ap()
    out = nc.dram_tensor("out_0", inputs["x"].shape, F32, kind="ExternalOutput").ap()
    program(nc, a, out)
    r = run_bass_kernel_spmd(nc, [arrays], core_ids=[0])
    return r.results[0]["out_0"]
```
